# Optimizing a Trainium2 kernel written in Bass

```python
import numpy as np
import jax
import jax.numpy as jnp

def _softmax(x, axis=-1):
    return jax.nn.softmax(x, axis=axis)

def _gelu(x):
    return jax.nn.gelu(x, approximate=True)

def _silu(x):
    return jax.nn.silu(x)

def _sigmoid(x):
    return jax.nn.sigmoid(x)

def _layernorm(x, axis=-1, eps=1e-05):
    m = jnp.mean(x, axis=axis, keepdims=True)
    v = jnp.var(x, axis=axis, keepdims=True)
    return (x - m) / jnp.sqrt(v + eps)

def _scatter_add(tgt, idx, src, axis=0):
    return tgt.at[idx].add(src)

def _segment_sum(src, seg, n):
    return jax.ops.segment_sum(src, seg, n)
kernel_name = 'mk_vit_tower_d2_tok_img768_r4_0331c0'

def setup_inputs(seed: int=0):
    np.random.seed(seed)
    _w = jnp.asarray

    def _rec_inputs():
        import jax
        import jax.numpy as jnp
        _rk = jax.random.key(seed)
        x = -0.00016672 + 0.999947 * jax.random.normal(jax.random.fold_in(_rk, 1), (64, 3, 224, 224), jnp.float32)
        return x
    x = _rec_inputs()

    def _L0_tok_setup():
        import jax, jax.numpy as jnp
        import numpy as np
        PATCH = 16

        def _patchify(x, p):
            B, C, H, W = x.shape
            Hp, Wp = (H // p, W // p)
            xu = x.reshape(B, C, Hp, p, Wp, p).transpose(0, 1, 2, 4, 3, 5)
            num_patches = Hp * Wp
            return xu.reshape(B, num_patches, -1)
        key = jax.random.key(seed)
        k1, k2, k3 = jax.random.split(key, 3)
        B, C, H = (64, 3, 96)
        hidden = 192
        d = C * PATCH * PATCH
        x = jax.random.normal(k1, (B, C, H, H), dtype=jnp.float32)
        W = jax.random.normal(k2, (hidden, d), dtype=jnp.float32) * 0.02
        b = jax.random.normal(k3, (hidden,), dtype=jnp.float32) * 0.02
        return {'x': x, 'W': W, 'b': b}
    _L0_tok_all = _L0_tok_setup()
    _L0_tok_in = {k: v for k, v in _L0_tok_all.items() if k in ('W', 'b')}
    del _L0_tok_all

    def _L0_attn_setup():
        import jax, jax.numpy as jnp
        import numpy as np
        H = 12
        D = 64
        L = 14
        SCALE = D ** (-0.5)

        def _rel_indices(N, length):
            n = N - 1
            s = int(n ** 0.5)
            r = np.arange(n)
            dv = r[None, :] // s - r[:, None] // s
            dh = r[None, :] % s - r[:, None] % s
            iv = np.clip(dv, -length, length) + length + 1
            ih = np.clip(dh, -length, length) + length + 1
            iv = np.pad(iv, ((1, 0), (1, 0)))
            ih = np.pad(ih, ((1, 0), (1, 0)))
            return (jnp.asarray(iv), jnp.asarray(ih))
        key = jax.random.key(seed)
        ks = jax.random.split(key, 10)
        B, N, E = (16, 577, 192)
        T = 2 * L + 2
        return {'x': jax.random.normal(ks[0], (B, N, E), jnp.float32), 'Wq': jax.random.normal(ks[1], (E, H * D), jnp.float32) * 0.02, 'Wk': jax.random.normal(ks[2], (E, H * D), jnp.float32) * 0.02, 'Wv': jax.random.normal(ks[3], (E, H * D), jnp.float32) * 0.02, 'Wp': jax.random.normal(ks[4], (H * D, E), jnp.float32) * 0.02, 'bp': jnp.zeros((E,), jnp.float32), 'tvk': jax.random.normal(ks[5], (T, D), jnp.float32) * 0.02, 'thk': jax.random.normal(ks[6], (T, D), jnp.float32) * 0.02, 'tvv': jax.random.normal(ks[7], (T, D), jnp.float32) * 0.02, 'thv': jax.random.normal(ks[8], (T, D), jnp.float32) * 0.02}
    _L0_attn_all = _L0_attn_setup()
    _L0_attn_in = {k: v for k, v in _L0_attn_all.items() if k in ('Wq', 'Wk', 'Wv', 'Wp', 'bp', 'tvk', 'thk', 'tvv', 'thv')}
    del _L0_attn_all

    def _L0_ffn_setup():
        import jax, jax.numpy as jnp
        import numpy as np
        CAPACITY_FACTOR = 1.25
        key = jax.random.key(seed)
        ks = jax.random.split(key, 5)
        B, S, D, F, E = (8, 512, 192, 768, 8)
        return {'x': jax.random.normal(ks[0], (B, S, D), jnp.float32), 'switch_w': jax.random.normal(ks[1], (D, E), jnp.float32) * 0.02, 'switch_b': jnp.zeros((E,), jnp.float32), 'w1': jax.random.normal(ks[2], (E, D, F), jnp.float32) * 0.02, 'b1': jnp.zeros((E, F), jnp.float32), 'w2': jax.random.normal(ks[3], (E, F, D), jnp.float32) * 0.02, 'b2': jnp.zeros((E, D), jnp.float32)}
    _L0_ffn_all = _L0_ffn_setup()
    _L0_ffn_in = {k: v for k, v in _L0_ffn_all.items() if k in ('switch_w', 'switch_b', 'w1', 'b1', 'w2', 'b2')}
    del _L0_ffn_all

    def _L1_attn_setup():
        import jax, jax.numpy as jnp
        import numpy as np
        B, T, D = (8, 1024, 192)
        BS = 3
        NB = D // BS

        def _rodrigues(b, v):
            theta = jnp.linalg.norm(b, axis=-1, keepdims=True)
            k = b / jnp.maximum(theta, 1e-08)
            c = jnp.cos(theta)
            s = jnp.sin(theta)
            cross = jnp.cross(k, v)
            dot = jnp.sum(k * v, axis=-1, keepdims=True)
            return v * c + cross * s + k * dot * (1.0 - c)
        key = jax.random.key(seed)
        ks = jax.random.split(key, 6)
        s = 1.0 / np.sqrt(D)
        return {'x_seq': jax.random.normal(ks[0], (B, T, D), jnp.float32), 'W_biv': jax.random.uniform(ks[1], (NB * 3, D), jnp.float32, -s, s), 'b_biv': jnp.zeros((NB * 3,), jnp.float32), 'W_decay': jax.random.uniform(ks[2], (1, D), jnp.float32, -s, s), 'b_decay': jnp.full((1,), 1.4, jnp.float32), 'W_in': jax.random.uniform(ks[3], (D, D), jnp.float32, -s, s), 'b_in': jax.random.uniform(ks[4], (D,), jnp.float32, -s, s)}
    _L1_attn_all = _L1_attn_setup()
    _L1_attn_in = {k: v for k, v in _L1_attn_all.items() if k in ('W_biv', 'b_biv', 'W_decay', 'b_decay', 'W_in', 'b_in')}
    del _L1_attn_all

    def _L1_ffn_setup():
        import jax, jax.numpy as jnp
        import numpy as np
        GT0 = [[0, 1, 0, 0, 1, 0], [0, 1, 0, 0, 0, 1], [0, 0, 1, 0, 1, 0], [0, 0, 1, 0, 0, 1], [0, 0, 0, 1, 1, 0], [0, 0, 0, 1, 0, 1]]
        NCLS = 6
        K = 1

        def _expert_pairs():
            pairs = []
            for i in range(NCLS):
                p = [(j - 1, k - 1) for j in range(1, 6) for k in range(1, 6) if j != k and GT0[i][j] == 1 and (GT0[i][k] == 1)]
                pairs.append(p)
            return pairs
        PAIRS = _expert_pairs()
        B, P, D, H = (64, 64, 192, 768)

        def _gelu(t):
            return jax.nn.gelu(t, approximate=False)
        key = jax.random.key(seed)
        ks = jax.random.split(key, 8)
        s = 0.02
        x = jax.random.normal(ks[0], (B, NCLS + P, D), dtype=jnp.float32)
        mids = jax.random.randint(ks[1], (B,), 0, 6)
        moe0_W1 = jax.random.normal(ks[2], (D, H), dtype=jnp.float32) * s
        moe0_b1 = jnp.zeros((H,), jnp.float32)
        moe0_W2 = jax.random.normal(ks[3], (H, D), dtype=jnp.float32) * s
        moe0_b2 = jnp.zeros((D,), jnp.float32)
        A1_W = jax.random.normal(ks[4], (5, D, H), dtype=jnp.float32) * s
        A1_b = jnp.zeros((5, H), jnp.float32)
        A2_W = jax.random.normal(ks[5], (5, H, D), dtype=jnp.float32) * s
        A2_b = jnp.zeros((5, D), jnp.float32)
        G_W = jax.random.normal(ks[6], (NCLS, D, 2), dtype=jnp.float32) * s
        return {'x': x, 'moe0_W1': moe0_W1, 'moe0_b1': moe0_b1, 'moe0_W2': moe0_W2, 'moe0_b2': moe0_b2, 'A1_W': A1_W, 'A1_b': A1_b, 'A2_W': A2_W, 'A2_b': A2_b, 'G_W': G_W, 'mids': mids}
    _L1_ffn_all = _L1_ffn_setup()
    _L1_ffn_in = {k: v for k, v in _L1_ffn_all.items() if k in ('moe0_W1', 'moe0_b1', 'moe0_W2', 'moe0_b2', 'A1_W', 'A1_b', 'A2_W', 'A2_b', 'G_W', 'mids')}
    del _L1_ffn_all
    return {'x': x, 'L0_tok_W': _L0_tok_in['W'], 'L0_tok_b': _L0_tok_in['b'], 'L0_attn_Wq': _L0_attn_in['Wq'], 'L0_attn_Wk': _L0_attn_in['Wk'], 'L0_attn_Wv': _L0_attn_in['Wv'], 'L0_attn_Wp': _L0_attn_in['Wp'], 'L0_attn_bp': _L0_attn_in['bp'], 'L0_attn_tvk': _L0_attn_in['tvk'], 'L0_attn_thk': _L0_attn_in['thk'], 'L0_attn_tvv': _L0_attn_in['tvv'], 'L0_attn_thv': _L0_attn_in['thv'], 'L0_ffn_switch_w': _L0_ffn_in['switch_w'], 'L0_ffn_switch_b': _L0_ffn_in['switch_b'], 'L0_ffn_w1': _L0_ffn_in['w1'], 'L0_ffn_b1': _L0_ffn_in['b1'], 'L0_ffn_w2': _L0_ffn_in['w2'], 'L0_ffn_b2': _L0_ffn_in['b2'], 'L1_attn_W_biv': _L1_attn_in['W_biv'], 'L1_attn_b_biv': _L1_attn_in['b_biv'], 'L1_attn_W_decay': _L1_attn_in['W_decay'], 'L1_attn_b_decay': _L1_attn_in['b_decay'], 'L1_attn_W_in': _L1_attn_in['W_in'], 'L1_attn_b_in': _L1_attn_in['b_in'], 'L1_ffn_moe0_W1': _L1_ffn_in['moe0_W1'], 'L1_ffn_moe0_b1': _L1_ffn_in['moe0_b1'], 'L1_ffn_moe0_W2': _L1_ffn_in['moe0_W2'], 'L1_ffn_moe0_b2': _L1_ffn_in['moe0_b2'], 'L1_ffn_A1_W': _L1_ffn_in['A1_W'], 'L1_ffn_A1_b': _L1_ffn_in['A1_b'], 'L1_ffn_A2_W': _L1_ffn_in['A2_W'], 'L1_ffn_A2_b': _L1_ffn_in['A2_b'], 'L1_ffn_G_W': _L1_ffn_in['G_W'], 'L1_ffn_mids': _L1_ffn_in['mids']}

def reference(x, L0_tok_W, L0_tok_b, L0_attn_Wq, L0_attn_Wk, L0_attn_Wv, L0_attn_Wp, L0_attn_bp, L0_attn_tvk, L0_attn_thk, L0_attn_tvv, L0_attn_thv, L0_ffn_switch_w, L0_ffn_switch_b, L0_ffn_w1, L0_ffn_b1, L0_ffn_w2, L0_ffn_b2, L1_attn_W_biv, L1_attn_b_biv, L1_attn_W_decay, L1_attn_b_decay, L1_attn_W_in, L1_attn_b_in, L1_ffn_moe0_W1, L1_ffn_moe0_b1, L1_ffn_moe0_W2, L1_ffn_moe0_b2, L1_ffn_A1_W, L1_ffn_A1_b, L1_ffn_A2_W, L1_ffn_A2_b, L1_ffn_G_W, L1_ffn_mids):
    import jax
    import jax.numpy as jnp

    def _L0_tok_ref(x, W, b):
        import jax, jax.numpy as jnp
        import numpy as np
        PATCH = 16

        def _patchify(x, p):
            B, C, H, W = x.shape
            Hp, Wp = (H // p, W // p)
            xu = x.reshape(B, C, Hp, p, Wp, p).transpose(0, 1, 2, 4, 3, 5)
            num_patches = Hp * Wp
            return xu.reshape(B, num_patches, -1)
        patches = _patchify(x, PATCH)
        return jnp.einsum('bnd,hd->bnh', patches, W) + b

    def _L0_attn_ref(x, Wq, Wk, Wv, Wp, bp, tvk, thk, tvv, thv):
        import jax, jax.numpy as jnp
        import numpy as np
        H = 12
        D = 64
        L = 14
        SCALE = D ** (-0.5)

        def _rel_indices(N, length):
            n = N - 1
            s = int(n ** 0.5)
            r = np.arange(n)
            dv = r[None, :] // s - r[:, None] // s
            dh = r[None, :] % s - r[:, None] % s
            iv = np.clip(dv, -length, length) + length + 1
            ih = np.clip(dh, -length, length) + length + 1
            iv = np.pad(iv, ((1, 0), (1, 0)))
            ih = np.pad(ih, ((1, 0), (1, 0)))
            return (jnp.asarray(iv), jnp.asarray(ih))
        B, N, E = x.shape
        iv, ih = _rel_indices(N, L)
        q = (x @ Wq).reshape(B, N, H, D).transpose(0, 2, 1, 3)
        k = (x @ Wk).reshape(B, N, H, D).transpose(0, 2, 1, 3)
        v = (x @ Wv).reshape(B, N, H, D).transpose(0, 2, 1, 3)
        attn = jnp.einsum('bhnd,bhmd->bhnm', q, k) * SCALE
        r_p_k = tvk[iv] + thk[ih]
        attn = attn + jnp.einsum('bhnd,nmd->bhnm', q, r_p_k) * SCALE
        attn = jax.nn.softmax(attn, axis=-1)
        out = jnp.einsum('bhnm,bhmd->bhnd', attn, v)
        r_p_v = tvv[iv] + thv[ih]
        out = out + jnp.einsum('bhnm,nmd->bhnd', attn, r_p_v)
        out = out.transpose(0, 2, 1, 3).reshape(B, N, H * D)
        return out @ Wp + bp

    def _L0_ffn_ref(x, switch_w, switch_b, w1, b1, w2, b2):
        import jax, jax.numpy as jnp
        import numpy as np
        CAPACITY_FACTOR = 1.25
        B, S, D = x.shape
        E = w1.shape[0]
        xf = x.reshape(-1, D)
        N = xf.shape[0]
        capacity = int(CAPACITY_FACTOR * N / E)
        probs = jax.nn.softmax(xf @ switch_w + switch_b, axis=-1)
        prob_max = jnp.max(probs, axis=-1)
        routes = jnp.argmax(probs, axis=-1)
        sort_idx = jnp.lexsort((-prob_max, routes))
        counts = jnp.bincount(routes, length=E)
        starts = jnp.concatenate([jnp.zeros((1,), counts.dtype), jnp.cumsum(counts)[:-1]])
        rank_sorted = jnp.arange(N) - starts[routes[sort_idx]]
        rank = jnp.zeros((N,), jnp.int32).at[sort_idx].set(rank_sorted.astype(jnp.int32))
        keep = rank < capacity
        dest_e = jnp.where(keep, routes, E)
        dest_c = jnp.where(keep, rank, 0)
        buf = jnp.zeros((E + 1, capacity, D), xf.dtype).at[dest_e, dest_c].set(xf)
        h = jax.nn.gelu(jnp.einsum('ecd,edf->ecf', buf[:E], w1) + b1[:, None, :], approximate=False)
        o = jnp.einsum('ecf,efd->ecd', h, w2) + b2[:, None, :]
        y_exp = o[routes, dest_c]
        y = jnp.where(keep[:, None], y_exp, xf)
        out = y * prob_max[:, None]
        return out.reshape(B, S, D)

    def _L1_attn_ref(x_seq, W_biv, b_biv, W_decay, b_decay, W_in, b_in):
        import jax, jax.numpy as jnp
        import numpy as np
        B, T, D = (8, 1024, 192)
        BS = 3
        NB = D // BS

        def _rodrigues(b, v):
            theta = jnp.linalg.norm(b, axis=-1, keepdims=True)
            k = b / jnp.maximum(theta, 1e-08)
            c = jnp.cos(theta)
            s = jnp.sin(theta)
            cross = jnp.cross(k, v)
            dot = jnp.sum(k * v, axis=-1, keepdims=True)
            return v * c + cross * s + k * dot * (1.0 - c)
        Bb, Tt, Dd = x_seq.shape
        nb = Dd // BS
        biv = (jnp.einsum('btd,od->bto', x_seq, W_biv) + b_biv).reshape(Bb, Tt, nb, 3)
        decay = jax.nn.sigmoid(jnp.einsum('btd,od->bto', x_seq, W_decay) + b_decay)[..., 0]
        inj = (jnp.einsum('btd,od->bto', x_seq, W_in) + b_in).reshape(Bb, Tt, nb, 3)

        def step(h, xs):
            b_t, d_t, u_t = xs
            h_new = d_t[:, None, None] * _rodrigues(b_t, h) + u_t
            return (h_new, h_new)
        h0 = jnp.zeros((Bb, nb, 3), x_seq.dtype)
        xs = (biv.transpose(1, 0, 2, 3), decay.T, inj.transpose(1, 0, 2, 3))
        _, states = jax.lax.scan(step, h0, xs)
        return states.transpose(1, 0, 2, 3).reshape(Bb, Tt, Dd)

    def _L1_ffn_ref(x, moe0_W1, moe0_b1, moe0_W2, moe0_b2, A1_W, A1_b, A2_W, A2_b, G_W, mids):
        import jax, jax.numpy as jnp
        import numpy as np
        GT0 = [[0, 1, 0, 0, 1, 0], [0, 1, 0, 0, 0, 1], [0, 0, 1, 0, 1, 0], [0, 0, 1, 0, 0, 1], [0, 0, 0, 1, 1, 0], [0, 0, 0, 1, 0, 1]]
        NCLS = 6
        K = 1

        def _expert_pairs():
            pairs = []
            for i in range(NCLS):
                p = [(j - 1, k - 1) for j in range(1, 6) for k in range(1, 6) if j != k and GT0[i][j] == 1 and (GT0[i][k] == 1)]
                pairs.append(p)
            return pairs
        PAIRS = _expert_pairs()
        B, P, D, H = (64, 64, 192, 768)

        def _gelu(t):
            return jax.nn.gelu(t, approximate=False)
        cls_tokens = x[:, :NCLS]
        patch_tokens = x[:, NCLS:]
        patch_out = _gelu(patch_tokens @ moe0_W1 + moe0_b1) @ moe0_W2 + moe0_b2
        cls_outs = []
        for i in range(NCLS):
            tok = cls_tokens[:, i]
            eouts = [_gelu(tok @ A1_W[a] + A1_b[a]) @ A2_W[c] + A2_b[c] for a, c in PAIRS[i]]
            out = jnp.stack(eouts, axis=-1)
            gate = jax.nn.softmax(tok @ G_W[i], axis=-1)
            thr = jnp.sort(gate, axis=-1)[..., -(K + 1)]
            mask = (gate > thr[..., None]).astype(gate.dtype)
            g = gate * mask
            g = g / jnp.clip(jnp.sum(g, axis=-1, keepdims=True), 1e-06)
            cls_outs.append(jnp.sum(out * g[:, None, :], axis=-1))
        cls_out = jnp.stack(cls_outs, axis=1)
        return jnp.concatenate([cls_out, patch_out], axis=1)
    h = _L0_tok_ref(x, L0_tok_W, L0_tok_b)
    h = h + _L0_attn_ref(_layernorm(h, axis=-1), L0_attn_Wq, L0_attn_Wk, L0_attn_Wv, L0_attn_Wp, L0_attn_bp, L0_attn_tvk, L0_attn_thk, L0_attn_tvv, L0_attn_thv)
    h = h + _L0_ffn_ref(_layernorm(h, axis=-1), L0_ffn_switch_w, L0_ffn_switch_b, L0_ffn_w1, L0_ffn_b1, L0_ffn_w2, L0_ffn_b2)
    h = h + _L1_attn_ref(_layernorm(h, axis=-1), L1_attn_W_biv, L1_attn_b_biv, L1_attn_W_decay, L1_attn_b_decay, L1_attn_W_in, L1_attn_b_in)
    h = h + _L1_ffn_ref(_layernorm(h, axis=-1), L1_ffn_moe0_W1, L1_ffn_moe0_b1, L1_ffn_moe0_W2, L1_ffn_moe0_b2, L1_ffn_A1_W, L1_ffn_A1_b, L1_ffn_A2_W, L1_ffn_A2_b, L1_ffn_G_W, L1_ffn_mids)
    return h

_drawn_inputs = setup_inputs


def setup_inputs(seed=0):
    import zlib

    import numpy as np

    out = dict(_drawn_inputs(seed))
    spreads = {'L0_attn_bp': (0.0, 0.1),
     'L0_ffn_switch_b': (0.0, 0.1),
     'L0_ffn_b1': (0.0, 0.49),
     'L0_ffn_b2': (0.0, 0.1),
     'L1_attn_b_biv': (0.0, 0.1),
     'L1_ffn_moe0_b1': (0.0, 0.373),
     'L1_ffn_moe0_b2': (0.0, 0.1),
     'L1_ffn_A1_b': (0.0, 0.8),
     'L1_ffn_A2_b': (0.0, 0.609)}
    factors = {'L0_attn_Wq': 8.0,
     'L0_attn_Wk': 7.877,
     'L0_attn_tvk': 8.0,
     'L0_attn_thk': 8.0,
     'L0_attn_tvv': 3.876,
     'L0_attn_thv': 3.382,
     'L1_ffn_A1_W': 5.112,
     'L1_ffn_A2_W': 4.724,
     'L1_ffn_G_W': 4.622}
    for name, (base, spread) in spreads.items():
        noise = np.random.default_rng([zlib.crc32(name.encode()), seed]).standard_normal(out[name].shape)
        drawn = base * np.exp(spread * noise) if base else spread * noise
        out[name] = jnp.asarray(drawn.astype(out[name].dtype))
    for name, factor in factors.items():
        out[name] = (out[name] * factor).astype(out[name].dtype)
    return out
```

```python
from contextlib import ExitStack

import numpy as np

import concourse.bass as bass
from concourse import mybir

F32 = mybir.dt.float32
I32 = mybir.dt.int32
U32 = mybir.dt.uint32
ALU = mybir.AluOpType
ACT = mybir.ActivationFunctionType
AX_X = mybir.AxisListType.X

B = 64
C_IN, IMG, PATCH = 3, 224, 16
GRID = IMG // PATCH
N = GRID * GRID
D = 192
HD = D // 2
TOK = B * N
H, DH = 12, 64
HW = H * DH
SIDE = 13
ROWS = 15
LREL = 14
CAP = int(1.25 * TOK / 8)
NE = 8
FF = 768
FC = FF // 128
SLOTS = NE * CAP
EPS = 1e-5
QK_SCALE = DH ** -0.5

NV = 2 * LREL + 2
NHR = 2 * SIDE - 1
TR = NV + NHR
TW = TR * H
VRUN, HRUN = ROWS * H, SIDE * H
AUG = 32
CLS = ROWS + SIDE
ONE = CLS + 1
VW = DH + ONE + 1
UC = TW // 6

PAIRS = B // 2
TM = 104
T0 = N - TM
SPI = C_IN * GRID
PST = 2 * SPI
TILE0 = [0, T0]
PART = [T0, TM]


class Count:

    def __init__(self, sem, per):
        self.sem, self.per = sem, per

    def now(self, it, k=None):
        return it * self.per + self.per + (self.per if k is None else k)

    def last(self, it, k=None):
        return it * self.per + (self.per if k is None else k)


class Dmas:

    def __init__(self, sem, per):
        self.sem, self.per = sem, per

    def now(self, it, k=None):
        return (it * self.per + (self.per if k is None else k)) * 16


def semaphore(nc, t, name):
    t["in_use"].append(nc.alloc_semaphore(name))
    return t["in_use"][-1]


def clear(nc, t):
    nc.clear_and_free_semaphores(t["in_use"])
    t["in_use"] = []
    nc.all_engine_barrier()


def halves(w):
    return w.rearrange("(c p) n -> p c n", p=HD)


def phase_setup(nc, a, t):
    with ExitStack() as ctx:
        def sb(name, shape, dt=F32):
            return ctx.enter_context(nc.sbuf_tensor(name, shape, dt))

        def sem(name):
            return semaphore(nc, t, name)

        w_tok = sb("su_w_tok", [HD, 2, 4 * D])
        wp_h = sb("su_wp_h", [DH, H, D])
        tab = sb("su_tab", [TR, 2, DH])
        tab0 = sb("su_tab0", [1, 2, DH])
        tab_t = sb("su_tab_t", [DH, 2, TR])
        wq_t = sb("su_wq_t", [DH, 2, 2, HD])
        u_h = sb("su_u_h", [TR, 2, D])
        zero = sb("su_zero", [120, 1536])
        ps = ctx.enter_context(nc.psum_tensor("su_ps", [128, 8, 512], F32))

        loaded = sem("su_loaded")
        added = sem("su_added")
        tables_turned = sem("su_tables_turned")
        tables_copied = sem("su_tables_copied")
        tok_turned = sem("su_tok_turned")
        tok_copied = sem("su_tok_copied")
        wq_turned = sem("su_wq_turned")
        wq_copied = sem("su_wq_copied")
        cq_made = sem("su_cq_made")
        cq_copied = sem("su_cq_copied")
        u_made = sem("su_u_made")
        u_copied = sem("su_u_copied")
        u_stored = [sem(f"su_u_stored{i}") for i in range(2)]
        u_loaded = sem("su_u_loaded")
        cleared = sem("su_cleared")
        zeroed = sem("su_zeroed")
        aug_cleared = sem("su_aug_cleared")

        u_dram = t["u"].rearrange("(r h) e -> r h e", h=H)

        block = ctx.enter_context(nc.Block())

        @block.sync
        def _(sp):
            loads = [(t["ident"][:, :], a["const_ident"]), (w_tok[:, :, :], halves(a["L0_tok_W"])),
                     (t["wq"][:, :, :], halves(a["L0_attn_Wq"])), (t["wk"][:, :, :], halves(a["L0_attn_Wk"])),
                     (t["wv"][:, :, :], halves(a["L0_attn_Wv"])),
                     (t["wp2"][:, :, :], a["L0_attn_Wp"].rearrange("(c p) n -> p c n", p=128)),
                     (wp_h[:, :, :], a["L0_attn_Wp"].rearrange("(h p) n -> p h n", p=DH)),
                     (t["sw"][:, :, :], halves(a["L0_ffn_switch_w"])),
                     (t["b_tok"][:, :], a["L0_tok_b"].partition_broadcast(TM)),
                     (t["b_proj"][:, :], a["L0_attn_bp"].partition_broadcast(TM)),
                     (t["b_gate"][:, :], a["L0_ffn_switch_b"].partition_broadcast(TM))]
            for k, (v, h) in enumerate((("tvk", "thk"), ("tvv", "thv"))):
                loads += [(tab[0:NV, k, :], a["L0_attn_" + v]),
                          (tab[NV:TR, k, :], a["L0_attn_" + h][LREL + 2 - SIDE:LREL + 1 + SIDE, :]),
                          (tab0[0:1, k, :], a["L0_attn_" + h][0:1, :])]
            for h in range(H):
                loads.append((t["ka"][DH:DH + AUG, h, :], a["const_key_aug"]))
            for q in range(4):
                loads.append((t["va"][:, q, :, DH:VW], a["const_val_aug"][q % 2]))
            for dst, src in loads:
                sp.dma_start(dst, src).then_inc(loaded, 16)
            sp.wait_ge(cleared, 1)
            rows = 960
            xs = t["xs"]
            n_big = SLOTS // rows
            for r in range(n_big):
                sp.dma_start(xs[r * rows:(r + 1) * rows, :].rearrange("(p r) d -> p (r d)", p=120),
                             zero[:, :]).then_inc(zeroed, 16)
            left = SLOTS - n_big * rows
            sp.dma_start(xs[n_big * rows:SLOTS, :].rearrange("(p r) d -> p (r d)", p=40),
                         zero[0:40, 0:left // 40 * D]).then_inc(zeroed, 16)
            for i in range(2):
                for j in range(2):
                    sp.dma_start(t["pr"][i, j * 98 * TW:(j + 1) * 98 * TW].rearrange("(p f) -> p f", p=98),
                                 zero[0:98, 0:TW]).then_inc(zeroed, 16)
            for h in range(H):
                sp.wait_ge(u_copied, h + 1)
                sp.dma_start(u_dram[:, h, :], u_h[:, h % 2, :]).then_inc(u_stored[h % 2], 16)
            for i in range(2):
                sp.wait_ge(u_stored[i], 16 * H // 2)
            sp.dma_start(t["u_sb"][:, :, :], t["u"].rearrange("(c p) e -> p c e", p=UC)).then_inc(u_loaded, 16)
            sp.wait_ge(u_loaded, 16)
            sp.wait_ge(zeroed, 16 * (n_big + 5))

        @block.gpsimd
        def _(pool):
            pool.memset(zero[:, :], 0.0).then_inc(cleared, 1)
            pool.memset(t["eps"][:, :], EPS)
            pool.memset(t["qaug"][:, :, :, :], 0.0).then_inc(aug_cleared, 1)
            pool.wait_ge(aug_cleared, 1)

        n_loads = 11 + 6 + H + 4

        @block.vector
        def _(dve):
            dve.wait_ge(loaded, 16 * n_loads)
            dve.tensor_tensor(tab[0:1, :, :], tab[0:1, :, :], tab0[:, :, :], ALU.add).then_inc(added, 1)
            dve.wait_ge(tables_turned, 1)
            dve.tensor_copy(tab_t[:, :, :], ps[0:DH, 0, 0:2 * TR].rearrange("p (k r) -> p k r", k=2)).then_inc(tables_copied, 1)
            for c in range(6):
                dve.wait_ge(tok_turned, c + 1)
                dve.tensor_copy(t["w_tok_t"][:, c, :], ps[:, 1 + c % 3, 0:D]).then_inc(tok_copied, 1)
            for h in range(H):
                dve.wait_ge(wq_turned, h + 1)
                if h >= 2:
                    dve.wait_ge(cq_made, h - 1)
                dve.tensor_copy(wq_t[:, h % 2, :, :],
                                ps[0:DH, 4 + h % 2, 0:D].rearrange("p (c e) -> p c e", c=2)).then_inc(wq_copied, 1)
            for h in range(H):
                dve.wait_ge(u_made, h + 1)
                if h >= 2:
                    dve.wait_ge(u_stored[h % 2], 16 * (h // 2))
                dve.tensor_copy(u_h[:, h % 2, :], ps[0:TR, 1 + h % 2, 0:D]).then_inc(u_copied, 1)

        @block.scalar
        def _(act):
            for h in range(H):
                act.wait_ge(cq_made, h + 1)
                act.mul(t["cq"].rearrange("p c (r h) -> p c r h", h=H)[:, :, :, h],
                        ps[0:HD, 6 + h % 2, 0:2 * TR].rearrange("p (c r) -> p c r", c=2), QK_SCALE).then_inc(cq_copied, 1)
            act.wait_ge(cq_copied, H)

        @block.tensor
        def _(pe):
            ident = t["ident"]
            pe.wait_ge(loaded, 16 * n_loads)
            pe.wait_ge(added, 1)
            for k in range(2):
                last = pe.transpose(ps[0:DH, 0, k * TR:(k + 1) * TR], tab[:, k, :], ident[0:TR, 0:TR])
            last.then_inc(tables_turned, 1)
            for c in range(6):
                if c >= 3:
                    pe.wait_ge(tok_copied, c - 2)
                for k in range(2):
                    last = pe.transpose(ps[:, 1 + c % 3, k * HD:(k + 1) * HD], w_tok[:, k, c * 128:(c + 1) * 128],
                                        ident[0:HD, 0:HD])
                last.then_inc(tok_turned, 1)
            pe.wait_ge(tables_copied, 1)
            for h in range(H):
                if h >= 2:
                    pe.wait_ge(wq_copied, h - 1)
                for k in range(2):
                    last = pe.transpose(ps[0:DH, 4 + h % 2, k * HD:(k + 1) * HD],
                                        t["wq"][:, k, h * DH:(h + 1) * DH], ident[0:HD, 0:HD])
                last.then_inc(wq_turned, 1)
                pe.wait_ge(wq_copied, h + 1)
                if h >= 2:
                    pe.wait_ge(cq_copied, h - 1)
                for k in range(2):
                    last = pe.matmul(ps[0:HD, 6 + h % 2, k * TR:(k + 1) * TR], wq_t[:, h % 2, k, :],
                                     tab_t[:, 0, :], start=True, stop=True)
                last.then_inc(cq_made, 1)
            pe.wait_ge(tok_copied, 6)
            for h in range(H):
                if h >= 2:
                    pe.wait_ge(u_copied, h - 1)
                pe.matmul(ps[0:TR, 1 + h % 2, 0:D], tab_t[:, 1, :], wp_h[:, h, :], start=True, stop=True).then_inc(u_made, 1)


class Chain:

    def __init__(self, eng, sem, it, per):
        self.eng, self.sem, self.it, self.per, self.k = eng, sem, it, per, 0

    def __call__(self, instruction):
        self.k += 1
        instruction.then_inc(self.sem, 1)
        self.eng.wait_ge(self.sem, self.it * self.per + self.k)

    def end(self):
        assert self.k == self.per, self.k


def spread(ap, n):
    return ap.unsqueeze(2).to_broadcast([ap.shape[0], ap.shape[1], n])


def phase_tokens(nc, a, t):
    with ExitStack() as ctx:
        def sb(name, shape, dt=F32):
            return ctx.enter_context(nc.sbuf_tensor("a_" + name, shape, dt))

        def sem(name):
            return semaphore(nc, t, "a_" + name)

        NT = 2 * N
        raw = sb("raw", [PST, PATCH * IMG])
        pix = sb("pix", [PST, GRID, PATCH * PATCH])
        pt = sb("pt", [128, 2, PST * GRID])
        h_sb = sb("h", [TM, 4, D])
        xn = sb("xn", [TM, 4, D])
        stats = sb("stats", [TM, 4, 6])
        mv = sb("mv", [TM, 4, 2])
        std = sb("std", [TM, 4])
        rstd = sb("rstd", [TM, 4])
        xt = sb("xt", [HD, 2, NT])
        qt = sb("qt", [TM, 4, TW])
        qa = sb("qa", [DH + AUG, H, NT])
        qrow = sb("qrow", [TM, 4, H, AUG])
        probs = sb("probs", [TM, 2, 2, N])
        pts = sb("pts", [TM, 2, 2, N])
        shift = sb("shift", [TM, 2, 2])
        rl = sb("rl", [TM, 2, 4])
        on = sb("on", [TM, 2, 2, HW])
        rel = sb("rel", [TM, 2, 2, ONE + 1, H])
        pf = sb("pf", [TM, 2, 2, TW])
        ot = sb("ot", [128, 6, N])
        pft = sb("pft", [UC, 6, N])
        lg = sb("lg", [TM, 4, NE])
        ka, va, qaug, ident = t["ka"], t["va"], t["qaug"], t["ident"]
        ps = ctx.enter_context(nc.psum_tensor("a_ps", [128, 8, 512], F32))

        patch_turned = Count(sem("patch_turned"), 6)
        patch_copied_a = Count(sem("patch_copied_a"), 3)
        patch_copied_v = Count(sem("patch_copied_v"), 3)
        tok_made = Count(sem("tok_made"), 2)
        embedded = Count(sem("embedded"), 2)
        var_ready = Count(sem("var_ready"), 2)
        std_ready = Count(sem("std_ready"), 2)
        xn_ready = Count(sem("xn_ready"), 2)
        x_turned = Count(sem("x_turned"), 4)
        x_copied_a = Count(sem("x_copied_a"), 2)
        x_copied_v = Count(sem("x_copied_v"), 2)
        LIN = [("qt", q, n) for q in range(4) for n in range(2)]
        LIN += [("v", q, n) for q in range(4) for n in range(2)]
        LIN += [("q", c, 0) for c in range(6)] + [("k", c, 0) for c in range(6)]
        LIN += [("aug", g, 0) for g in range(3)]
        NL = len(LIN)
        lin_made = Count(sem("lin_made"), NL)
        lin_copied_a = Count(sem("lin_copied_a"), (NL + 1) // 2)
        lin_copied_v = Count(sem("lin_copied_v"), NL // 2)
        pix_ready = Count(sem("pix_ready"), 1)
        biased = Count(sem("biased"), 1)
        token0_set = Count(sem("token0_set"), 1)
        aug_fixed = Count(sem("aug_fixed"), 1)
        U = 2 * H
        scored = Count(sem("scored"), U)
        shift_ready = Count(sem("shift_ready"), U)
        probs_ready = Count(sem("probs_ready"), U)
        probs_turned = Count(sem("probs_turned"), U)
        probs_copied = Count(sem("probs_copied"), U)
        heads_made = Count(sem("heads_made"), U)
        heads_copied = Count(sem("heads_copied"), 6)
        TAIL = 7
        tail_made = Count(sem("tail_made"), 2 * TAIL)
        tail_copied_a = Count(sem("tail_copied_a"), 6)
        tail_copied_v = Count(sem("tail_copied_v"), 8)
        gate_made = Count(sem("gate_made"), 1)
        gate_ready = Count(sem("gate_ready"), 1)
        stores_done = Count(sem("stores_done"), 1)
        raw_loaded = Dmas(sem("raw_loaded"), 1)
        qt_stored = Dmas(sem("qt_stored"), 4)
        aug_loaded = Dmas(sem("aug_loaded"), 8)
        rel_stored = Dmas(sem("rel_stored"), 14)
        pf_loaded = [Dmas(sem(f"pf_loaded{i}"), 2) for i in range(2)]
        stored = Dmas(sem("stored"), 12)
        dve_chain = sem("dve_chain")
        CHAINED = 2 * 2 + 6

        strips = a["x"].rearrange("b c (g i) w -> (b c g) (i w)", i=PATCH)
        qt_rows = t["qt"].rearrange("i (n f) -> i n f", f=TW)
        GROUPS = [(half, w0, min(w0 + 6, GRID)) for half in range(2) for w0 in range(0, GRID, 6)]

        def skew(dram, im, tile, base, run):
            first, rows = (1, 7) if tile == 0 else (T0, 8)
            rn = (first - 1) // SIDE
            at = im * N * TW + first * TW
            if base == 0:
                at += (LREL + 1 - rn) * H
                return bass.AP(dram.tensor, at, [[SIDE * TW - H, rows], [TW, SIDE], [1, run]])
            at += NV * H + (SIDE - 1) * H
            return bass.AP(dram.tensor, at, [[SIDE * TW, rows], [TW - H, SIDE], [1, run]])

        def tail_copy(k):
            im, j = divmod(k, TAIL)
            return (tail_copied_a, 3 * im + j // 2 + 1) if j in (0, 2, 4) else (tail_copied_v, 4 * im + {1: 1, 3: 2, 5: 3, 6: 4}[j])

        block = ctx.enter_context(nc.Block())

        @block.sync
        def _(sp):
            sp.sem_inc(stores_done.sem, 1)
            sp.dma_start(raw[:, :], strips[0:PST, :]).then_inc(raw_loaded.sem, 16)

            def one(it, more):
                if more:
                    sp.wait_ge(pix_ready.sem, pix_ready.now(it))
                    sp.dma_start(raw[:, :], strips[bass.ds(it * PST + PST, PST), :]).then_inc(raw_loaded.sem, 16)
                for q in range(4):
                    im, tile = divmod(q, 2)
                    sp.wait_ge(lin_copied_a.sem, lin_copied_a.now(it, q + 1))
                    sp.sem_inc(t["held"], 1)
                    sp.wait_ge(lin_copied_v.sem, lin_copied_v.now(it, q + 1))
                    sp.dma_start(qt_rows[im, TILE0[tile]:TILE0[tile] + PART[tile], :],
                                 qt[0:PART[tile], q, :]).then_inc(qt_stored.sem, 16)
                sp.wait_ge(qt_stored.sem, qt_stored.now(it))
                for q in range(4):
                    im, tile = divmod(q, 2)
                    p0 = 1 - tile
                    for base, r0, run in ((0, 0, VRUN), (1, ROWS, HRUN)):
                        sp.dma_start(qaug[p0:PART[tile], q, r0:r0 + run // H, :].rearrange("p r h -> p (r h)"),
                                     skew(t["qt"], im, tile, base, run)).then_inc(aug_loaded.sem, 16)
                for im in range(2):
                    sp.wait_ge(heads_copied.sem, heads_copied.now(it, 3 * (im + 1)))
                    for tile in range(2):
                        p0, p1 = 1 - tile, PART[tile]
                        for base, r0, run in ((0, 0, VRUN), (1, ROWS, HRUN)):
                            sp.dma_start(skew(t["pr"], im, tile, base, run),
                                         rel[p0:p1, im, tile, r0:r0 + run // H, :].rearrange("p r h -> p (r h)")).then_inc(rel_stored.sem, 16)
                        sp.dma_start(t["pr"][im].rearrange("(n f) -> n f", f=TW)[TILE0[tile] + p0:TILE0[tile] + p1, 0:H],
                                     rel[p0:p1, im, tile, CLS, :]).then_inc(rel_stored.sem, 16)
                    sp.dma_start(t["pr"][im:im + 1, 0:H], rel[0:1, im, 0, ONE, :]).then_inc(rel_stored.sem, 16)
                    sp.wait_ge(rel_stored.sem, rel_stored.now(it, 7 * (im + 1)))
                    for tile in range(2):
                        sp.dma_start(pf[0:PART[tile], im, tile, :],
                                     t["pr"][im].rearrange("(n f) -> n f", f=TW)[TILE0[tile]:TILE0[tile] + PART[tile], :]
                                     ).then_inc(pf_loaded[im].sem, 16)
                sp.wait_ge(xn_ready.sem, xn_ready.now(it, 2))
                for q in range(4):
                    im, tile = divmod(q, 2)
                    at = it * NT + (im * N + TILE0[tile])
                    sp.dma_start(t["h1"][bass.ds(at, PART[tile]), :], h_sb[0:PART[tile], q, :]).then_inc(stored.sem, 16)
                    sp.dma_start(t["ys"][bass.ds(at + SLOTS, PART[tile]), :], xn[0:PART[tile], q, :]).then_inc(stored.sem, 16)
                sp.wait_ge(gate_ready.sem, gate_ready.now(it))
                for q in range(4):
                    im, tile = divmod(q, 2)
                    at = it * NT + (im * N + TILE0[tile])
                    sp.dma_start(t["lg"][bass.ds(at, PART[tile]), :], lg[0:PART[tile], q, :]).then_inc(stored.sem, 16)
                sp.wait_ge(stored.sem, stored.now(it))
                sp.sem_inc(stores_done.sem, 1)

            with sp.Fori(0, PAIRS - 1) as it:
                one(it, True)
            one(PAIRS - 1, False)

        @block.gpsimd
        def _(pool):
            for c in (pix_ready, biased, token0_set, aug_fixed):
                pool.sem_inc(c.sem, 1)
            with pool.Fori(0, PAIRS) as it:
                pool.wait_ge(raw_loaded.sem, raw_loaded.now(it))
                pool.wait_ge(patch_turned.sem, patch_turned.last(it))
                pool.sem_inc(t["held"], 1)
                pool.tensor_copy(pix[:, :, :].rearrange("p w (i j) -> p i w j", j=PATCH),
                                 raw[:, :].rearrange("p (i w j) -> p i w j", i=PATCH, j=PATCH)).then_inc(pix_ready.sem, 1)
                pool.wait_ge(xn_ready.sem, xn_ready.now(it, 1))
                for q in range(4):
                    last = pool.tensor_tensor(h_sb[:, q, :], h_sb[:, q, :], t["b_proj"][:, :], ALU.add)
                last.then_inc(biased.sem, 1)
                pool.wait_ge(lin_copied_a.sem, lin_copied_a.now(it, 4))
                pool.wait_ge(lin_copied_v.sem, lin_copied_v.now(it, 4))
                pool.sem_inc(t["held"], 1)
                for q in range(4):
                    last = pool.tensor_copy(qaug[:, q, CLS, :], qt[:, q, 0:H])
                for q in (0, 2):
                    last = pool.tensor_copy(qaug[0:1, q, 0:ROWS, :], qt[0:1, q, 0:H].unsqueeze(1).to_broadcast([1, ROWS, H]))
                last.then_inc(token0_set.sem, 1)
                pool.wait_ge(token0_set.sem, token0_set.now(it))
                pool.wait_ge(aug_loaded.sem, aug_loaded.now(it))
                pool.sem_inc(t["held"], 1)
                for q in range(4):
                    last = pool.tensor_copy(qrow[:, q, :, :].rearrange("p h r -> p r h"), qaug[:, q, :, :])
                last.then_inc(aug_fixed.sem, 1)

        @block.scalar
        def _(act):
            for c in (patch_copied_a, std_ready, x_copied_a, lin_copied_a, probs_ready, tail_copied_a):
                act.sem_inc(c.sem, c.per)
            with act.Fori(0, PAIRS) as it:
                for g in (0, 2, 4):
                    half, w0, w1 = GROUPS[g]
                    act.wait_ge(patch_turned.sem, patch_turned.now(it, g + 1))
                    act.copy(pt[:, half, :].rearrange("p (s w) -> p w s", w=GRID)[:, w0:w1, :],
                             ps[:, g, 0:(w1 - w0) * PST].rearrange("p (w s) -> p w s", s=PST)).then_inc(patch_copied_a.sem, 1)

                def norm_step(n):
                    act.wait_ge(var_ready.sem, var_ready.now(it, n + 1))
                    act.activation(std[:, :], mv[:, :, 1], ACT.Sqrt, bias=t["eps"][0:TM, :]).then_inc(std_ready.sem, 1)
                    act.wait_ge(x_turned.sem, x_turned.now(it, 2 * n + 1))
                    act.copy(xt[:, 0, :], ps[0:HD, 4 * n, 0:NT]).then_inc(x_copied_a.sem, 1)

                norm_step(0)
                for j in range(0, NL, 2):
                    act.wait_ge(lin_made.sem, lin_made.now(it, j + 1))
                    bank, (kind, c, n) = (2 + j) % 8, LIN[j]
                    if kind == "qt":
                        last = act.copy(qt[:, c, n * TW // 2:(n + 1) * TW // 2], ps[0:TM, bank, 0:TW // 2])
                    elif kind == "v":
                        last = act.copy(va[:, c, 6 * n:6 * n + 6, 0:DH], ps[0:TM, bank, 0:HW // 2].rearrange("p (h d) -> p h d", d=DH))
                    elif kind == "q":
                        for s in range(2):
                            last = act.mul(qa[0:DH, 2 * c + s, :], ps[DH * s:DH * s + DH, bank, 0:NT], QK_SCALE)
                    elif kind == "k":
                        for s in range(2):
                            last = act.copy(ka[0:DH, 2 * c + s, :], ps[DH * s:DH * s + DH, bank, 0:NT])
                    else:
                        for s in range(4):
                            last = act.copy(qa[DH:DH + AUG, 4 * c + s, :], ps[AUG * s:AUG * s + AUG, bank, 0:NT])
                    last.then_inc(lin_copied_a.sem, 1)
                for u in range(U):
                    act.wait_ge(shift_ready.sem, shift_ready.now(it, u + 1))
                    if u >= 2:
                        act.wait_ge(probs_turned.sem, probs_turned.now(it, u - 1))
                    for tile in range(2):
                        last = act.activation(probs[:, u % 2, tile, :], ps[0:TM, u % 2, tile * N:(tile + 1) * N], ACT.Exp,
                                              bias=shift[:, u % 2, tile:tile + 1])
                    last.then_inc(probs_ready.sem, 1)
                for k in range(2 * TAIL):
                    im, j = divmod(k, TAIL)
                    if j in (0, 2, 4):
                        act.wait_ge(tail_made.sem, tail_made.now(it, k + 1))
                        if j < 3:
                            last = act.copy(ot[:, 2 * j:2 * j + 2, :], ps[:, k % 4, 0:2 * N].rearrange("p (c n) -> p c n", c=2))
                        else:
                            last = act.copy(pft[:, 2 * j - 6:2 * j - 4, :], ps[0:UC, k % 4, 0:2 * N].rearrange("p (c n) -> p c n", c=2))
                        last.then_inc(tail_copied_a.sem, 1)
                norm_step(1)

        @block.vector
        def _(dve):
            for c in (patch_copied_v, embedded, var_ready, xn_ready, x_copied_v, lin_copied_v, shift_ready, probs_copied,
                      heads_copied, tail_copied_v, gate_ready):
                dve.sem_inc(c.sem, c.per)
            with dve.Fori(0, PAIRS) as it:
                link = Chain(dve, dve_chain, it, CHAINED)

                def norm_step(n):
                    for q in range(4):
                        last = dve.bn_stats(stats[:, q, :], h_sb[:, q, :])
                    link(last)
                    dve.sem_inc(t["held"], 1)
                    for q in range(4):
                        last = dve.bn_aggr(mv[:, q, :], stats[:, q, :])
                    last.then_inc(var_ready.sem, 1)
                    dve.wait_ge(std_ready.sem, std_ready.now(it, n + 1))
                    link(dve.reciprocal(rstd[:, :], std[:, :]))
                    for q in range(4):
                        last = dve.tensor_scalar(xn[:, q, :], h_sb[:, q, :], mv[:, q, 0:1], rstd[:, q:q + 1], ALU.subtract, ALU.mult)
                    last.then_inc(xn_ready.sem, 1)
                    dve.wait_ge(x_turned.sem, x_turned.now(it, 2 * n + 2))
                    dve.tensor_copy(xt[:, 1, :], ps[0:HD, 4 * n + 1, 0:NT]).then_inc(x_copied_v.sem, 1)

                for g in (1, 3, 5):
                    half, w0, w1 = GROUPS[g]
                    dve.wait_ge(patch_turned.sem, patch_turned.now(it, g + 1))
                    dve.tensor_copy(pt[:, half, :].rearrange("p (s w) -> p w s", w=GRID)[:, w0:w1, :],
                                    ps[:, g, 0:(w1 - w0) * PST].rearrange("p (w s) -> p w s", s=PST)).then_inc(patch_copied_v.sem, 1)
                dve.wait_ge(stores_done.sem, stores_done.last(it))
                for im in range(2):
                    dve.wait_ge(tok_made.sem, tok_made.now(it, im + 1))
                    dve.tensor_tensor(h_sb[:, 2 * im:2 * im + 2, :], ps[0:TM, 6 + im, 0:2 * D].rearrange("p (q d) -> p q d", q=2),
                                      t["b_tok"][:, :].unsqueeze(1).to_broadcast([TM, 2, D]), ALU.add).then_inc(embedded.sem, 1)
                dve.wait_ge(embedded.sem, embedded.now(it))
                norm_step(0)
                for j in range(1, NL, 2):
                    dve.wait_ge(lin_made.sem, lin_made.now(it, j + 1))
                    bank, (kind, c, n) = (2 + j) % 8, LIN[j]
                    if kind == "qt":
                        last = dve.tensor_copy(qt[:, c, n * TW // 2:(n + 1) * TW // 2], ps[0:TM, bank, 0:TW // 2])
                    elif kind == "v":
                        last = dve.tensor_copy(va[:, c, 6 * n:6 * n + 6, 0:DH], ps[0:TM, bank, 0:HW // 2].rearrange("p (h d) -> p h d", d=DH))
                    elif kind == "q":
                        for s in range(2):
                            last = dve.tensor_scalar(qa[0:DH, 2 * c + s, :], ps[DH * s:DH * s + DH, bank, 0:NT], QK_SCALE, None, ALU.mult)
                    elif kind == "k":
                        for s in range(2):
                            last = dve.tensor_copy(ka[0:DH, 2 * c + s, :], ps[DH * s:DH * s + DH, bank, 0:NT])
                    else:
                        for s in range(4):
                            last = dve.tensor_copy(qa[DH:DH + AUG, 4 * c + s, :], ps[AUG * s:AUG * s + AUG, bank, 0:NT])
                    last.then_inc(lin_copied_v.sem, 1)
                for s in range(U + 5):
                    if s < U:
                        dve.wait_ge(scored.sem, scored.now(it, s + 1))
                        if s >= 2:
                            dve.wait_ge(probs_ready.sem, probs_ready.now(it, s - 1))
                        dve.tensor_reduce(shift[:, s % 2, :], ps[0:TM, s % 2, 0:NT].rearrange("p (q m) -> p q m", q=2), AX_X, ALU.max,
                                          negate=True).then_inc(shift_ready.sem, 1)
                    if 0 <= s - 2 < U:
                        u = s - 2
                        dve.wait_ge(probs_turned.sem, probs_turned.now(it, u + 1))
                        if u >= 2:
                            dve.wait_ge(heads_made.sem, heads_made.now(it, u - 1))
                        dve.tensor_copy(pts[:, u % 2, :, :], ps[0:TM, 2 + u % 2, 0:NT].rearrange("p (q n) -> p q n", q=2)).then_inc(probs_copied.sem, 1)
                    if s >= 7 and (s - 7) % 4 == 0 and (s - 7) // 4 < 6:
                        grp = (s - 7) // 4
                        im, g = divmod(grp, 3)
                        dve.wait_ge(heads_made.sem, heads_made.now(it, 4 * grp + 4))
                        acc = ps[0:TM, 4 + 2 * (grp % 2):6 + 2 * (grp % 2), 0:4 * VW].rearrange("p q (h w) -> p q h w", w=VW)
                        link(dve.reciprocal(rl[:, :, :], acc[:, :, :, VW - 1]))
                        for tile in range(2):
                            dve.tensor_tensor(on[:, im, tile, 4 * g * DH:(4 * g + 4) * DH].rearrange("p (h d) -> p h d", d=DH),
                                              acc[:, tile, :, 0:DH], spread(rl[:, tile, :], DH), ALU.mult)
                            last = dve.tensor_tensor(rel[:, im, tile, :, 4 * g:4 * g + 4].rearrange("p r h -> p h r"),
                                                     acc[:, tile, :, DH:VW], spread(rl[:, tile, :], ONE + 1), ALU.mult)
                        last.then_inc(heads_copied.sem, 1)
                for k in range(2 * TAIL):
                    im, j = divmod(k, TAIL)
                    if j in (0, 2, 4):
                        continue
                    dve.wait_ge(tail_made.sem, tail_made.now(it, k + 1))
                    if j < 3:
                        last = dve.tensor_copy(ot[:, 2 * j:2 * j + 2, :], ps[:, k % 4, 0:2 * N].rearrange("p (c n) -> p c n", c=2))
                    elif j < 6:
                        last = dve.tensor_copy(pft[:, 2 * j - 6:2 * j - 4, :], ps[0:UC, k % 4, 0:2 * N].rearrange("p (c n) -> p c n", c=2))
                    else:
                        if im == 0:
                            dve.wait_ge(biased.sem, biased.now(it))
                        last = dve.tensor_tensor(h_sb[:, 2 * im:2 * im + 2, :], ps[0:TM, k % 4, 0:2 * D].rearrange("p (q d) -> p q d", q=2),
                                                 h_sb[:, 2 * im:2 * im + 2, :], ALU.add)
                    last.then_inc(tail_copied_v.sem, 1)
                dve.wait_ge(tail_copied_v.sem, tail_copied_v.now(it))
                norm_step(1)
                dve.wait_ge(gate_made.sem, gate_made.now(it))
                dve.tensor_tensor(lg[:, :, :], ps[0:TM, 6, 0:4 * NE].rearrange("p (q e) -> p q e", q=4),
                                  t["b_gate"][:, :].unsqueeze(1).to_broadcast([TM, 4, NE]), ALU.add).then_inc(gate_ready.sem, 1)
                link.end()

        @block.tensor
        def _(pe):
            for c in (patch_turned, tok_made, x_turned, lin_made, scored, probs_turned, heads_made, tail_made, gate_made):
                pe.sem_inc(c.sem, c.per)
            with pe.Fori(0, PAIRS) as it:
                def turn_x(n):
                    pe.wait_ge(xn_ready.sem, xn_ready.now(it, n + 1))
                    for c in range(2):
                        for q in range(4):
                            im, tile = divmod(q, 2)
                            m = PART[tile]
                            at = im * N + TILE0[tile]
                            last = pe.transpose(ps[0:HD, 4 * n + c, at:at + m], xn[0:m, q, c * HD:(c + 1) * HD], ident[0:m, 0:m])
                        last.then_inc(x_turned.sem, 1)
                    pe.wait_ge(x_copied_a.sem, x_copied_a.now(it, n + 1))
                    pe.wait_ge(x_copied_v.sem, x_copied_v.now(it, n + 1))

                pe.wait_ge(pix_ready.sem, pix_ready.now(it))
                pe.wait_ge(gate_ready.sem, gate_ready.last(it))
                for g, (half, w0, w1) in enumerate(GROUPS):
                    for w in range(w0, w1):
                        last = pe.transpose(ps[:, g, (w - w0) * PST:(w - w0 + 1) * PST], pix[:, w, 128 * half:128 * half + 128], ident[0:PST, 0:PST])
                    last.then_inc(patch_turned.sem, 1)
                pe.wait_ge(patch_copied_a.sem, patch_copied_a.now(it))
                pe.wait_ge(patch_copied_v.sem, patch_copied_v.now(it))
                for im in range(2):
                    for tile in range(2):
                        at = im * 3 * N + 3 * TILE0[tile]
                        for c in range(6):
                            first = at + c // 2
                            last = pe.matmul(ps[0:TM, 6 + im, tile * D:(tile + 1) * D], pt[:, c % 2, first:first + 3 * (TM - 1) + 1:3],
                                             t["w_tok_t"][:, c, :], start=(c == 0), stop=(c == 5))
                    last.then_inc(tok_made.sem, 1)
                turn_x(0)
                for j, (kind, c, n) in enumerate(LIN):
                    bank = (2 + j) % 8
                    if j >= 8:
                        copied = lin_copied_v if j % 2 else lin_copied_a
                        pe.wait_ge(copied.sem, copied.now(it, (j - 8) // 2 + 1))
                    at = (c // 2) * N + TILE0[c % 2]
                    if kind == "aug" and c == 0:
                        pe.wait_ge(aug_loaded.sem, aug_loaded.now(it))
                        pe.wait_ge(aug_fixed.sem, aug_fixed.now(it))
                    if kind == "aug":
                        for q in range(4):
                            im, tile = divmod(q, 2)
                            m, to = PART[tile], im * N + TILE0[tile]
                            last = pe.transpose(ps[:, bank, to:to + m], qrow[0:m, q, 4 * c:4 * c + 4, :].rearrange("p h r -> p (h r)"),
                                                ident[0:m, 0:m])
                    else:
                        for k in range(2):
                            if kind == "qt":
                                last = pe.matmul(ps[0:TM, bank, 0:TW // 2], xt[:, k, at:at + TM], t["cq"][:, k, n * TW // 2:(n + 1) * TW // 2],
                                                 start=(k == 0), stop=(k == 1))
                            elif kind == "v":
                                last = pe.matmul(ps[0:TM, bank, 0:HW // 2], xt[:, k, at:at + TM], t["wv"][:, k, n * HW // 2:(n + 1) * HW // 2],
                                                 start=(k == 0), stop=(k == 1))
                            else:
                                last = pe.matmul(ps[:, bank, 0:NT], t["w" + kind][:, k, c * 128:(c + 1) * 128], xt[:, k, :],
                                                 start=(k == 0), stop=(k == 1))
                    last.then_inc(lin_made.sem, 1)
                pe.wait_ge(lin_copied_a.sem, lin_copied_a.now(it))
                pe.wait_ge(lin_copied_v.sem, lin_copied_v.now(it))
                for s in range(U + 3):
                    if s < U:
                        im, h = divmod(s, H)
                        if s >= 2:
                            pe.wait_ge(probs_ready.sem, probs_ready.now(it, s - 1))
                        for tile in range(2):
                            at = im * N + TILE0[tile]
                            last = pe.matmul(ps[0:TM, s % 2, tile * N:(tile + 1) * N], qa[:, h, at:at + TM], ka[:, h, im * N:(im + 1) * N],
                                             start=True, stop=True)
                        last.then_inc(scored.sem, 1)
                    if 0 <= s - 2 < U:
                        u = s - 2
                        pe.wait_ge(probs_ready.sem, probs_ready.now(it, u + 1))
                        if u >= 2:
                            pe.wait_ge(probs_copied.sem, probs_copied.now(it, u - 1))
                        for mt in range(2):
                            for tile in range(2):
                                m = PART[tile]
                                last = pe.transpose(ps[0:TM, 2 + u % 2, mt * N + TILE0[tile]:mt * N + TILE0[tile] + m],
                                                    probs[0:m, u % 2, tile, TILE0[mt]:TILE0[mt] + TM], ident[0:m, 0:m])
                        last.then_inc(probs_turned.sem, 1)
                    if 0 <= s - 3 < U:
                        u = s - 3
                        im, h = divmod(u, H)
                        grp = u // 4
                        pe.wait_ge(probs_copied.sem, probs_copied.now(it, u + 1))
                        if u % 4 == 0 and grp >= 2:
                            pe.wait_ge(heads_copied.sem, heads_copied.now(it, grp - 1))
                        for tile in range(2):
                            for mt in range(2):
                                last = pe.matmul(ps[0:TM, 4 + 2 * (grp % 2) + tile, (u % 4) * VW:(u % 4 + 1) * VW],
                                                 pts[0:PART[mt], u % 2, mt, TILE0[tile]:TILE0[tile] + TM],
                                                 va[0:PART[mt], 2 * im + mt, h, :], start=(mt == 0), stop=(mt == 1))
                        last.then_inc(heads_made.sem, 1)
                for k in range(2 * TAIL):
                    im, j = divmod(k, TAIL)
                    if k >= 4:
                        copied, n = tail_copy(k - 4)
                        pe.wait_ge(copied.sem, copied.now(it, n))
                    if j == 0:
                        pe.wait_ge(heads_copied.sem, heads_copied.now(it, 3 * im + 3))
                    if j == 3:
                        pe.wait_ge(pf_loaded[im].sem, pf_loaded[im].now(it))
                    if j < 6:
                        src, w = (on, 128) if j < 3 else (pf, UC)
                        for c in range(2):
                            at = (2 * (j % 3) + c) * w
                            for tile in range(2):
                                m = PART[tile]
                                last = pe.transpose(ps[0:w, k % 4, c * N + TILE0[tile]:c * N + TILE0[tile] + m],
                                                    src[0:m, im, tile, at:at + w], ident[0:m, 0:m])
                    else:
                        pe.wait_ge(tail_copied_a.sem, tail_copied_a.now(it, 3 * im + 3))
                        pe.wait_ge(tail_copied_v.sem, tail_copied_v.now(it, 4 * im + 3))
                        for tile in range(2):
                            n0 = TILE0[tile]
                            for c in range(12):
                                lhs, rhs = (ot[:, c, n0:n0 + TM], t["wp2"][:, c, :]) if c < 6 else (pft[:, c - 6, n0:n0 + TM], t["u_sb"][:, c - 6, :])
                                last = pe.matmul(ps[0:TM, k % 4, tile * D:(tile + 1) * D], lhs, rhs, start=(c == 0), stop=(c == 11))
                    last.then_inc(tail_made.sem, 1)
                turn_x(1)
                for q in range(4):
                    at = (q // 2) * N + TILE0[q % 2]
                    for k in range(2):
                        last = pe.matmul(ps[0:TM, 6, q * NE:(q + 1) * NE], xt[:, k, at:at + TM], t["sw"][:, k, :], start=(k == 0), stop=(k == 1))
                last.then_inc(gate_made.sem, 1)


def constants():
    key = np.zeros((N, ONE + 1), np.float32)
    m = np.arange(1, N)
    key[m, (m - 1) // SIDE] = 1
    key[m, ROWS + (m - 1) % SIDE] = 1
    key[0, CLS] = 1
    key_aug = np.zeros((AUG, 2 * N), np.float32)
    key_aug[:ONE + 1] = np.concatenate([key, key]).T
    key[:, ONE] = 1
    val = np.stack([key[n0:n0 + TM] for n0 in TILE0])
    val_aug = np.ascontiguousarray(np.broadcast_to(val[:, :, None, :], (2, TM, H, ONE + 1)))
    rep = lambda v: np.ascontiguousarray(np.broadcast_to(v.astype(np.float32), (98, v.shape[-1])))
    return {
        "const_ident": np.eye(128, dtype=np.float32), "const_key_aug": key_aug, "const_val_aug": val_aug,
        "const_ones": np.ones((98, 98), np.float32),
        "const_before": np.triu(np.ones((98, 98), np.float32), 1),
        "const_rank": rep(NE - np.arange(NE)), "const_base": rep(CAP * np.arange(NE)),
        "const_own": (SLOTS + np.arange(128)[None, :] * 98 + np.arange(98)[:, None]).astype(np.float32),
    }


def dram(nc, kind="Internal"):
    def d(name, shape, dt=F32, kind=kind):
        return nc.dram_tensor(name, shape, dt, kind=kind).ap()

    return {
        "u": d("u", (TW, D), kind="Internal"),
        "qt": d("qt", (2, N * TW), kind="Internal"),
        "pr": d("pr", (2, N * TW), kind="Internal"),
        "h1": d("h1", (TOK, D)),
        "xs": d("xs", (SLOTS + TOK, D)),
        "ys": d("ys", (SLOTS + TOK, D)),
        "lg": d("lg", (TOK, NE)),
        "h3": d("h3", (TOK, D)),
        "slot": d("slot", (TOK, 1), I32),
        "pm": d("pm", (TOK, 1)),
    }


def keep(nc, ctx, t):
    for name, shape in {
        "eps": [128, 1], "w_tok_t": [128, 6, D], "wq": [HD, 2, HW], "wk": [HD, 2, HW],
        "wv": [HD, 2, HW], "wp2": [128, 6, D], "u_sb": [UC, 6, D], "cq": [HD, 2, TW], "sw": [HD, 2, NE],
        "b_tok": [TM, D], "b_proj": [TM, D], "b_gate": [TM, NE], "ka": [DH + AUG, H, 2 * N], "va": [TM, 4, H, VW],
        "qaug": [TM, 4, AUG, H],
    }.items():
        t[name] = ctx.enter_context(nc.sbuf_tensor("k_" + name, shape, F32))


RP = 98
RQ = TOK // RP
BITS = 28


def phase_route(nc, a, t):
    with ExitStack() as ctx:
        def sb(name, shape, dt=F32):
            return ctx.enter_context(nc.sbuf_tensor("r_" + name, shape, dt))

        def sem(name):
            return semaphore(nc, t, "r_" + name)

        lg = sb("lg", [RP, RQ, NE])
        e = sb("e", [RP, NE, RQ])
        eq = sb("eq", [RP, NE, RQ])
        key = sb("key", [RP, NE, RQ])
        hit = sb("hit", [RP, NE, RQ])
        kept = sb("kept", [RP, NE, RQ])
        before = sb("before", [RP, NE, RQ])
        totals = sb("totals", [RP, NE, RQ])
        ones_row = sb("ones_row", [RP, RQ])
        mx = sb("mx", [RP, RQ])
        sm = sb("sm", [RP, RQ])
        pm = sb("pm", [RP, RQ])
        slot = sb("slot", [RP, RQ])
        has = sb("has", [RP, RQ])
        own = sb("own", [RP, RQ])
        slot_t = sb("slot_t", [RQ, RP])
        pm_t = sb("pm_t", [RQ, RP])
        slot_ti = sb("slot_ti", [RQ, RP], I32)
        slot_i = sb("slot_i", [RP, RQ], I32)
        rank_w = sb("rank_w", [RP, NE])
        base_w = sb("base_w", [RP, NE])
        thr = sb("thr", [RP, NE])
        trial = sb("trial", [RP, NE])
        step = sb("step", [RP, 1])
        cnt = sb("cnt", [RP, NE])
        need = sb("need", [RP, NE])
        ok = sb("ok", [RP, NE])
        ones = sb("ones", [RP, RP])
        lower = sb("lower", [RP, RP])
        ident = t["ident"]
        now = sb("now", [RP, 8], I32)
        xin = sb("xin", [RP, 8, D])
        ps = ctx.enter_context(nc.psum_tensor("r_ps", [128, 8, 512], F32))

        loaded = sem("loaded")
        chain = sem("chain")
        bit_chain = sem("bit_chain")
        counted = sem("counted")
        summed = sem("summed")
        maxed = sem("maxed")
        expd = sem("expd")
        masked = sem("masked")
        ranked = sem("ranked")
        placed = sem("placed")
        slots_turned = sem("slots_turned")
        slots_copied = sem("slots_copied")
        stored = sem("stored")
        x_loaded = [sem(f"x_loaded{i}") for i in range(8)]
        x_sent = [sem(f"x_sent{i}") for i in range(8)]
        picked = sem("picked")
        block = ctx.enter_context(nc.Block())

        @block.sync
        def _(sp):
            for dst, src in ((lg[:, :, :], t["lg"].rearrange("(q p) e -> p q e", p=RP)),
                             (ones[:, :], a["const_ones"]), (lower[:, :], a["const_before"]), (rank_w[:, :], a["const_rank"]),
                             (base_w[:, :], a["const_base"]), (own[:, :], a["const_own"])):
                sp.dma_start(dst, src).then_inc(loaded, 16)
            rows = t["ys"][SLOTS:SLOTS + TOK, :].rearrange("(g p) d -> g p d", p=RP)
            for i in range(8):
                sp.dma_start(xin[:, i, :], rows[i]).then_inc(x_loaded[i], 16)
            sp.wait_ge(slots_copied, 1)
            sp.dma_start(t["slot"].rearrange("(q p) o -> q (p o)", p=RP), slot_ti[:, :]).then_inc(stored, 16)
            sp.dma_start(t["pm"].rearrange("(q p) o -> q (p o)", p=RP), pm_t[:, :]).then_inc(stored, 16)
            with sp.Fori(1, RQ // 8) as n:
                for i in range(8):
                    sp.wait_ge(x_sent[i], 16 * n)
                    sp.sem_inc(t["held"], 1)
                    sp.dma_start(xin[:, i, :], t["ys"][bass.ds(n * (8 * RP) + (SLOTS + i * RP), RP), :]).then_inc(x_loaded[i], 16)
            sp.wait_ge(stored, 32)

        @block.gpsimd
        def _(pool):
            pool.wait_ge(placed, 1)
            def send(n):
                pool.tensor_copy(now[:, :], slot_i[:, bass.ds(n * 8, 8)]).then_inc(picked, 1)
                pool.wait_ge(picked, n + 1)
                for i in range(8):
                    pool.wait_ge(x_loaded[i], n * 16 + 16)
                    pool.sem_inc(t["held"], 1)
                    pool.indirect_dma_start(t["xs"], bass.IndirectOffsetOnAxis(ap=now[:, i:i + 1], axis=0), xin[:, i, :], None
                                            ).then_inc(x_sent[i], 16)

            send(0)
            with pool.Fori(1, RQ // 8) as n:
                for i in range(8):
                    pool.wait_ge(x_sent[i], n * 16)
                pool.sem_inc(t["held"], 1)
                send(n)
            for i in range(8):
                pool.wait_ge(x_sent[i], 16 * (RQ // 8))

        @block.scalar
        def _(act):
            act.wait_ge(maxed, 1)
            act.activation(e[:, :, :], eq[:, :, :], ACT.Exp).then_inc(expd, 1)

        @block.vector
        def _(dve):
            done = [0]

            def link(ins):
                done[0] += 1
                ins.then_inc(chain, 1)
                dve.wait_ge(chain, done[0])

            def by_expert(v):
                return v.unsqueeze(1).to_broadcast([RP, NE, RQ])

            def by_token(v):
                return v.unsqueeze(2).to_broadcast([RP, NE, RQ])

            def sum_e(out, src, op=ALU.add):
                link(dve.tensor_reduce(out, src.rearrange("p e q -> p q e"), AX_X, op))

            dve.wait_ge(loaded, 16 * 6)
            link(dve.memset(ones_row[:, :], 1.0))
            link(dve.memset(thr[:, :], 0.0))
            link(dve.memset(step[:, :], 1.0))
            link(dve.tensor_reduce(mx[:, :], lg[:, :, :], AX_X, ALU.max))
            dve.tensor_tensor(eq[:, :, :], lg[:, :, :].rearrange("p q e -> p e q"), by_expert(mx[:, :]), ALU.subtract).then_inc(maxed, 1)
            dve.wait_ge(expd, 1)
            sum_e(sm[:, :], e[:, :, :])
            link(dve.reciprocal(mx[:, :], sm[:, :]))
            link(dve.tensor_tensor(e[:, :, :], e[:, :, :], by_expert(mx[:, :]), ALU.mult))
            sum_e(pm[:, :], e[:, :, :], ALU.max)
            link(dve.tensor_tensor(eq[:, :, :], e[:, :, :], by_expert(pm[:, :]), ALU.is_equal))
            link(dve.tensor_tensor(eq[:, :, :], eq[:, :, :], by_token(rank_w[:, :]), ALU.mult))
            sum_e(sm[:, :], eq[:, :, :], ALU.max)
            link(dve.tensor_tensor(eq[:, :, :], by_expert(sm[:, :]), by_token(rank_w[:, :]), ALU.is_equal))
            link(dve.tensor_scalar(hit[:, :, :], eq[:, :, :], 1.0, None, ALU.subtract))
            link(dve.tensor_tensor(key[:, :, :], eq[:, :, :], by_expert(pm[:, :]), ALU.mult))
            link(dve.tensor_tensor(key[:, :, :], key[:, :, :], hit[:, :, :], ALU.add))

            def reach(op, bound, ordered):
                ordered(dve.tensor_tensor(hit[:, :, :], key[:, :, :], by_token(bound), op))
                dve.tensor_reduce(cnt[:, :], hit[:, :, :], AX_X, ALU.add).then_inc(counted, 1)

            with dve.Fori(0, BITS) as b:
                bit = Chain(dve, bit_chain, b, 5)
                bit(dve.tensor_scalar(trial[:, :], thr[:, :], step[:, 0:1], None, ALU.add))
                reach(ALU.is_ge, trial[:, :], bit)
                dve.wait_ge(summed, b + 1)
                bit(dve.tensor_scalar(ok[:, :], ps[0:RP, 0, 0:NE], float(CAP), step[:, 0:1], ALU.is_ge, ALU.mult))
                bit(dve.tensor_tensor(thr[:, :], thr[:, :], ok[:, :], ALU.add))
                bit(dve.tensor_scalar(step[:, :], step[:, :], 0.5, None, ALU.mult))
                bit.end()
            reach(ALU.is_gt, thr[:, :], link)
            dve.wait_ge(summed, BITS + 1)
            link(dve.tensor_scalar(need[:, :], ps[0:RP, 0, 0:NE], -1.0, float(CAP), ALU.mult, ALU.add))
            link(dve.tensor_copy(kept[:, :, :], hit[:, :, :]))

            def rank(n):
                dve.wait_ge(ranked, n + 1)
                link(dve.tensor_copy(totals[:, :, :], ps[0:RP, 4:6, :].rearrange("p b (e q) -> p (b e) q", q=RQ)))
                for x in range(NE):
                    link(dve.tensor_tensor_scan(before[:, x, :], ones_row[:, :], totals[:, x, :], 0.0, ALU.mult, ALU.add))
                link(dve.tensor_tensor(before[:, :, :], before[:, :, :], totals[:, :, :], ALU.subtract))
                link(dve.tensor_tensor(before[:, :, :], before[:, :, :], ps[0:RP, 2:4, :].rearrange("p b (e q) -> p (b e) q", q=RQ), ALU.add))

            link(dve.tensor_tensor(hit[:, :, :], key[:, :, :], by_token(thr[:, :]), ALU.is_equal))
            dve.sem_inc(masked, 1)
            rank(0)
            link(dve.tensor_tensor(before[:, :, :], before[:, :, :], by_token(need[:, :]), ALU.is_lt))
            link(dve.tensor_tensor(hit[:, :, :], hit[:, :, :], before[:, :, :], ALU.mult))
            link(dve.tensor_tensor(hit[:, :, :], hit[:, :, :], kept[:, :, :], ALU.add))
            dve.sem_inc(masked, 1)
            rank(1)
            link(dve.tensor_tensor(before[:, :, :], before[:, :, :], by_token(base_w[:, :]), ALU.add))
            link(dve.tensor_tensor(before[:, :, :], before[:, :, :], hit[:, :, :], ALU.mult))
            sum_e(slot[:, :], before[:, :, :])
            sum_e(has[:, :], hit[:, :, :])
            link(dve.tensor_scalar(has[:, :], has[:, :], -1.0, 1.0, ALU.mult, ALU.add))
            link(dve.tensor_tensor(has[:, :], has[:, :], own[:, :], ALU.mult))
            link(dve.tensor_tensor(slot[:, :], slot[:, :], has[:, :], ALU.add))
            dve.tensor_copy(slot_i[:, :], slot[:, :]).then_inc(placed, 1)
            dve.wait_ge(slots_turned, 1)
            dve.tensor_copy(slot_ti[:, :], ps[0:RQ, 1, 0:RP])
            dve.tensor_copy(pm_t[:, :], ps[0:RQ, 1, RP:2 * RP]).then_inc(slots_copied, 1)

        @block.tensor
        def _(pe):
            pe.wait_ge(loaded, 16 * 6)
            with pe.Fori(0, BITS + 1) as b:
                pe.wait_ge(counted, b + 1)
                pe.matmul(ps[0:RP, 0, 0:NE], ones[:, :], cnt[:, :], start=True, stop=True).then_inc(summed, 1)
            for n in range(2):
                pe.wait_ge(masked, n + 1)
                for half in range(2):
                    src = hit[:, 4 * half:4 * half + 4, :].rearrange("p e q -> p (e q)")
                    pe.matmul(ps[0:RP, 2 + half, :], lower[:, :], src, start=True, stop=True)
                    last = pe.matmul(ps[0:RP, 4 + half, :], ones[:, :], src, start=True, stop=True)
                last.then_inc(ranked, 1)
            pe.wait_ge(placed, 1)
            pe.transpose(ps[0:RQ, 1, 0:RP], slot[:, :], ident[0:RP, 0:RP])
            pe.transpose(ps[0:RQ, 1, RP:2 * RP], pm[:, :], ident[0:RP, 0:RP]).then_inc(slots_turned, 1)


CT = CAP // 4
CQ = CT // RP


def phase_experts(nc, a, t):
    with ExitStack() as ctx:
        def sb(name, shape, dt=F32):
            return ctx.enter_context(nc.sbuf_tensor("e_" + name, shape, dt))

        def sem(name):
            return semaphore(nc, t, "e_" + name)

        ident = t["ident"]
        w1 = sb("w1", [HD, 2, FF])
        w2 = sb("w2", [128, FC, D])
        b1 = sb("b1", [128, FC])
        b2 = sb("b2", [RP, D])
        xin = sb("xin", [RP, 2, CQ, D])
        xt = sb("xt", [HD, 2, 2, CT])
        ht = sb("ht", [128, FC, CT])
        y = sb("y", [RP, 2, CQ, D])
        ps = ctx.enter_context(nc.psum_tensor("e_ps", [128, 8, 512], F32))

        w1_loaded = Dmas(sem("w1_loaded"), 2)
        w2_loaded = Dmas(sem("w2_loaded"), 2)
        x_loaded = [Dmas(sem(f"x_loaded{i}"), 2) for i in range(2)]
        stored = [Dmas(sem(f"stored{i}"), 2) for i in range(2)]
        x_turned = Count(sem("x_turned"), 8)
        x_copied_a = Count(sem("x_copied_a"), 4)
        x_copied_v = Count(sem("x_copied_v"), 4)
        up_made = Count(sem("up_made"), 4 * FC)
        gelu_done = Count(sem("gelu_done"), 4 * FC)
        down_made = Count(sem("down_made"), 12)
        y_ready = Count(sem("y_ready"), 12)
        block = ctx.enter_context(nc.Block())

        @block.sync
        def _(sp):
            with sp.Fori(0, NE) as e:
                sp.wait_ge(up_made.sem, up_made.last(e))
                sp.sem_inc(t["held"], 1)
                sp.dma_start(w1[:, :, :].unsqueeze(1), a["L0_ffn_w1"].rearrange("e (c p) n -> p e c n", p=HD)[:, bass.ds(e, 1), :, :]).then_inc(w1_loaded.sem, 16)
                sp.wait_ge(gelu_done.sem, gelu_done.last(e))
                sp.sem_inc(t["held"], 1)
                sp.dma_start(b1[:, :].unsqueeze(1), a["L0_ffn_b1"].rearrange("e (c p) -> p e c", p=128)[:, bass.ds(e, 1), :], allow_slow_non_contiguous=True).then_inc(w1_loaded.sem, 16)

                def load(j):
                    if j < 2:
                        sp.wait_ge(x_turned.sem, x_turned.last(e, 2 * (j + 2) + 2))
                    else:
                        sp.wait_ge(x_turned.sem, x_turned.now(e, 2 * (j - 2) + 2))
                    sp.sem_inc(t["held"], 1)
                    sp.dma_start(xin[:, j % 2, :, :], t["xs"][bass.ds(e * CAP + j * CT, CT), :].rearrange("(q p) d -> p q d", p=RP)
                                 ).then_inc(x_loaded[j % 2].sem, 16)

                load(0)
                sp.wait_ge(down_made.sem, down_made.last(e))
                sp.sem_inc(t["held"], 1)
                sp.dma_start(w2[:, :, :].unsqueeze(1), a["L0_ffn_w2"].rearrange("e (c p) n -> p e c n", p=128)[:, bass.ds(e, 1), :, :]).then_inc(w2_loaded.sem, 16)
                sp.wait_ge(y_ready.sem, y_ready.last(e))
                sp.sem_inc(t["held"], 1)
                sp.dma_start(b2[:, :].unsqueeze(1), a["L0_ffn_b2"][bass.ds(e, 1), :].partition_broadcast(RP)).then_inc(w2_loaded.sem, 16)
                load(1)
                for j in range(4):
                    if j + 2 < 4:
                        load(j + 2)
                    sp.wait_ge(y_ready.sem, y_ready.now(e, 3 * j + 3))
                    sp.sem_inc(t["held"], 1)
                    sp.dma_start(t["ys"][bass.ds(e * CAP + j * CT, CT), :].rearrange("(q p) d -> p q d", p=RP), y[:, j % 2, :, :]
                                 ).then_inc(stored[j % 2].sem, 16)
                for i in range(2):
                    sp.wait_ge(stored[i].sem, stored[i].now(e))
                sp.sem_inc(t["held"], 1)

        @block.scalar
        def _(act):
            for c in (x_copied_a, gelu_done):
                act.sem_inc(c.sem, c.per)
            with act.Fori(0, NE) as e:
                def copy_x(j):
                    act.wait_ge(x_turned.sem, x_turned.now(e, 2 * j + 1))
                    act.copy(xt[:, j % 2, 0, :], ps[0:HD, 0, 0:CT]).then_inc(x_copied_a.sem, 1)

                copy_x(0)
                act.wait_ge(w1_loaded.sem, w1_loaded.now(e))
                for j in range(4):
                    for f in range(FC):
                        act.wait_ge(up_made.sem, up_made.now(e, FC * j + f + 1))
                        act.activation(ht[:, f, :], ps[:, 2 + f, 0:CT], ACT.Gelu, bias=b1[:, f:f + 1]).then_inc(gelu_done.sem, 1)
                    if j < 3:
                        copy_x(j + 1)

        @block.vector
        def _(dve):
            for c in (x_copied_v, y_ready):
                dve.sem_inc(c.sem, c.per)
            with dve.Fori(0, NE) as e:
                def copy_x(j):
                    dve.wait_ge(x_turned.sem, x_turned.now(e, 2 * j + 2))
                    dve.tensor_copy(xt[:, j % 2, 1, :], ps[0:HD, 1, 0:CT]).then_inc(x_copied_v.sem, 1)

                copy_x(0)
                dve.wait_ge(w2_loaded.sem, w2_loaded.now(e))
                for j in range(4):
                    if j < 3:
                        copy_x(j + 1)
                    if j >= 2:
                        dve.wait_ge(stored[j % 2].sem, stored[j % 2].now(e, 1))
                    for b in range(3):
                        n = min(2, CQ - 2 * b)
                        dve.wait_ge(down_made.sem, down_made.now(e, 3 * j + b + 1))
                        dve.tensor_tensor(y[:, j % 2, 2 * b:2 * b + n, :], ps[0:RP, 2 + b, 0:n * D].rearrange("p (q d) -> p q d", q=n),
                                          b2[:, :].unsqueeze(1).to_broadcast([RP, n, D]), ALU.add).then_inc(y_ready.sem, 1)

        @block.tensor
        def _(pe):
            for c in (x_turned, up_made, down_made):
                pe.sem_inc(c.sem, c.per)
            with pe.Fori(0, NE) as e:
                def turn_x(j):
                    pe.wait_ge(x_loaded[j % 2].sem, x_loaded[j % 2].now(e, j // 2 + 1))
                    for c in range(2):
                        for q in range(CQ):
                            last = pe.transpose(ps[0:HD, c, q * RP:(q + 1) * RP], xin[:, j % 2, q, c * HD:(c + 1) * HD], ident[0:RP, 0:RP])
                        last.then_inc(x_turned.sem, 1)

                turn_x(0)
                pe.wait_ge(w1_loaded.sem, w1_loaded.now(e))
                for j in range(4):
                    pe.wait_ge(x_copied_a.sem, x_copied_a.now(e, j + 1))
                    pe.wait_ge(x_copied_v.sem, x_copied_v.now(e, j + 1))
                    for f in range(FC):
                        if f < 3:
                            at = 3 * (j - 1) + f + 1
                            pe.wait_ge(y_ready.sem, y_ready.now(e, at) if j else y_ready.last(e, 9 + f + 1))
                        for c in range(2):
                            last = pe.matmul(ps[:, 2 + f, 0:CT], w1[:, c, f * 128:(f + 1) * 128], xt[:, j % 2, c, :], start=(c == 0), stop=(c == 1))
                        last.then_inc(up_made.sem, 1)
                    if j < 3:
                        turn_x(j + 1)
                    if j == 0:
                        pe.wait_ge(w2_loaded.sem, w2_loaded.now(e))
                    pe.wait_ge(gelu_done.sem, gelu_done.now(e, FC * j + FC))
                    for b in range(3):
                        for q in range(2 * b, min(2 * b + 2, CQ)):
                            for f in range(FC):
                                last = pe.matmul(ps[0:RP, 2 + b, (q % 2) * D:(q % 2 + 1) * D], ht[:, f, q * RP:(q + 1) * RP], w2[:, f, :],
                                                 start=(f == 0), stop=(f == FC - 1))
                        last.then_inc(down_made.sem, 1)


TC = 14
NTC = N // TC
ST = 8 * TC
SQ = 8
HB = B // 2
NB = D // 3
SF = TC * HB
TWO_PI = (6.28125, 1.9350051879882812e-03, 3.019916050561e-07)
ROUND = 1.5 * 2.0 ** 23


def phase_states(nc, a, t):
    with ExitStack() as ctx:
        def sb(name, shape, dt=F32):
            return ctx.enter_context(nc.sbuf_tensor("s_" + name, shape, dt))

        def sem(name):
            return semaphore(nc, t, "s_" + name)

        ident = t["ident"]
        wrow = sb("wrow", [NB, 6, D])
        dcol = sb("dcol", [HD, 2])
        wt = sb("wt", [HD, 2, 7, NB])
        bias = sb("bias", [128, 7])
        h = sb("h", [ST, 2, SQ, D])
        slot = sb("slot", [ST, 2, SQ], I32)
        pm = sb("pm", [ST, 2, SQ])
        y = sb("y", [ST, 2, SQ, D])
        xn = sb("xn", [ST, SQ, D])
        stats = sb("stats", [ST, SQ, 6])
        mv = sb("mv", [ST, SQ, 2])
        std = sb("std", [ST, SQ])
        rstd = sb("rstd", [ST, SQ])
        xt = sb("xt", [HD, 2, 2, SF])
        eps = sb("eps", [128, 1])
        biv = sb("biv", [128, 3, SF])
        sq = sb("sq", [128, 3, SF])
        k = sb("k", [128, 3, SF])
        sk = sb("sk", [128, 3, SF])
        qk = sb("qk", [128, 3, SF])
        dec = sb("dec", [128, SF])
        th = sb("th", [128, SF])
        ang = sb("ang", [128, SF])
        rnd = sb("rnd", [128, SF])
        sn = sb("sn", [128, SF])
        sh = sb("sh", [128, SF])
        om = sb("om", [128, SF])
        a0 = sb("a0", [128, SF])
        mat = sb("mat", [128, TC, 9, HB])
        u = sb("u", [128, 2, TC, 3, HB])
        prod = sb("prod", [128, 3, 3, HB])
        sum0 = sb("sum0", [128, 3, HB])
        sum1 = sb("sum1", [128, 3, HB])
        state = sb("state", [128, 2, TC, 3, HB])
        state2 = sb("state2", [128, 3, HB, TC])
        ps = ctx.enter_context(nc.psum_tensor("s_ps", [128, 8, 512], F32))

        w_loaded = sem("w_loaded")
        w_turned = sem("w_turned")
        w_copied = sem("w_copied")
        w_ready = sem("w_ready")
        h_loaded = [Dmas(sem(f"h_loaded{i}"), 3 * SQ) for i in range(2)]
        y_loaded = [Dmas(sem(f"y_loaded{i}"), SQ) for i in range(2)]
        stored = [Dmas(sem(f"stored{i}"), SQ) for i in range(2)]
        var_ready = Count(sem("var_ready"), 1)
        std_ready = Count(sem("std_ready"), 1)
        xn_ready = Count(sem("xn_ready"), 1)
        x_turned = Count(sem("x_turned"), 4)
        x_copied_a = Count(sem("x_copied_a"), 2)
        x_copied_v = Count(sem("x_copied_v"), 2)
        made = Count(sem("made"), 7)
        made_copied = Count(sem("made_copied"), 7)
        squared = Count(sem("squared"), 1)
        norm2_ready = Count(sem("norm2_ready"), 1)
        theta_ready = Count(sem("theta_ready"), 1)
        angle_ready = Count(sem("angle_ready"), 1)
        sines_ready = Count(sem("sines_ready"), 1)
        scanned = Count(sem("scanned"), 1)
        state_sorted = Count(sem("state_sorted"), 1)
        state_turned = Count(sem("state_turned"), 4)
        h3_ready = Count(sem("h3_ready"), 1)
        front_chain = sem("front_chain")
        elem_chain = sem("elem_chain")
        scan_chain = sem("scan_chain")
        setup_chain = sem("setup_chain")
        FRONT, ELEM = 3, 16

        def tile_rows(name, g, i, par):
            v = t[name].rearrange("(g b n) d -> g b n d", g=SQ, n=N)[g]
            return v[:, bass.ds(i * 2 * TC + par * TC, TC), :]

        block = ctx.enter_context(nc.Block())

        @block.sync
        def _(sp):
            n = 0
            wb = a["L1_attn_W_biv"].rearrange("(k c) d -> c k d", c=3)
            wi = a["L1_attn_W_in"].rearrange("(k c) d -> c k d", c=3)
            for c in range(3):
                sp.dma_start(wrow[:, c, :], wb[c]).then_inc(w_loaded, 16)
                sp.dma_start(wrow[:, 3 + c, :], wi[c]).then_inc(w_loaded, 16)
            sp.dma_start(dcol[:, :], a["L1_attn_W_decay"].rearrange("o (c p) -> p (o c)", p=HD), allow_slow_non_contiguous=True).then_inc(w_loaded, 16)
            for half in range(2):
                p = slice(half * NB, half * NB + NB)
                sp.dma_start(bias[p, 0:3], a["L1_attn_b_biv"].rearrange("(k c) -> k c", c=3)).then_inc(w_loaded, 16)
                sp.dma_start(bias[p, 3:6], a["L1_attn_b_in"].rearrange("(k c) -> k c", c=3)).then_inc(w_loaded, 16)
            sp.dma_start(bias[:, 6:7], a["L1_attn_b_decay"].partition_broadcast(128)).then_inc(w_loaded, 16)

            def load(i, par):
                for g in range(SQ):
                    sp.dma_start(h[:, par, g, :], tile_rows("h1", g, i, par)).then_inc(h_loaded[par].sem, 16)
                    for dst, name in ((slot, "slot"), (pm, "pm")):
                        sp.dma_start(dst[:, par, g:g + 1], tile_rows(name, g, i, par)).then_inc(h_loaded[par].sem, 16)

            def store(i, par):
                tc = i * 2 + par
                sp.wait_ge(h3_ready.sem, h3_ready.now(tc))
                sp.sem_inc(t["held"], 1)
                for g in range(SQ):
                    sp.dma_start(tile_rows("h3", g, i, par), h[:, par, g, :]).then_inc(stored[par].sem, 16)
                sp.wait_ge(stored[par].sem, stored[par].now(i))
                sp.sem_inc(t["held"], 1)

            load(0, 0)
            load(0, 1)
            with sp.Fori(0, NTC // 2 - 1) as i:
                for par in range(2):
                    store(i, par)
                    load(i + 1, par)
            store(NTC // 2 - 1, 0)
            store(NTC // 2 - 1, 1)

        @block.gpsimd
        def _(pool):
            with pool.Fori(0, NTC // 2) as i:
                for par in range(2):
                    pool.wait_ge(h_loaded[par].sem, h_loaded[par].now(i))
                    pool.sem_inc(t["held"], 1)
                    for g in range(SQ):
                        pool.indirect_dma_start(y[:, par, g, :], None, t["ys"], bass.IndirectOffsetOnAxis(ap=slot[:, par, g:g + 1], axis=0)
                                                ).then_inc(y_loaded[par].sem, 16)

        def chunks(eng, body):
            body(0, 0, False)
            body(0, 1, True)
            with eng.Fori(1, NTC // 2) as i:
                body(i, 0, True)
                body(i, 1, True)

        @block.scalar
        def _(act):
            for c in (std_ready, x_copied_a, made_copied, squared, theta_ready, sines_ready, state_sorted):
                act.sem_inc(c.sem, c.per)
            act.wait_ge(w_ready, 1)

            def sort_states(tc, par):
                act.wait_ge(scanned.sem, scanned.now(tc))
                act.copy(state2[:, :, :, :], state[:, par, :, :, :].rearrange("p t c b -> p c b t")).then_inc(state_sorted.sem, 1)

            def body(i, par, before):
                tc = i * 2 + par
                act.wait_ge(var_ready.sem, var_ready.now(tc))
                act.activation(std[:, :], mv[:, :, 1], ACT.Sqrt, bias=eps[0:ST, :]).then_inc(std_ready.sem, 1)
                for half in range(2):
                    act.wait_ge(x_turned.sem, x_turned.now(tc, half + 1))
                    act.copy(xt[:, 0, half, :].rearrange("p (t b) -> p t b", b=HB),
                             ps[0:HD, half, 0:SF].rearrange("p (b t) -> p t b", t=TC)).then_inc(x_copied_a.sem, 1)
                for c in range(7):
                    act.wait_ge(made.sem, made.now(tc, c + 1))
                    src = ps[:, (4 + c) % 8, 0:SF]
                    if c < 3:
                        last = act.activation(biv[:, c, :], src, ACT.Identity, bias=bias[:, c:c + 1])
                    elif c < 6:
                        last = act.activation(u[:, par, :, c - 3, :], src.rearrange("p (t b) -> p t b", b=HB), ACT.Identity, bias=bias[:, c:c + 1])
                    else:
                        last = act.activation(dec[:, :], src, ACT.Sigmoid, bias=bias[:, 6:7])
                    last.then_inc(made_copied.sem, 1)
                act.wait_ge(made_copied.sem, made_copied.now(tc))
                act.activation(sq[:, :, :], biv[:, :, :], ACT.Square).then_inc(squared.sem, 1)
                if before:
                    sort_states(tc - 1, 1 - par)
                act.wait_ge(norm2_ready.sem, norm2_ready.now(tc))
                act.activation(th[:, :], om[:, :], ACT.Sqrt).then_inc(theta_ready.sem, 1)
                act.wait_ge(angle_ready.sem, angle_ready.now(tc))
                act.activation(sn[:, :], ang[:, :], ACT.Sin)
                act.activation(sh[:, :], ang[:, :], ACT.Sin, scale=0.5).then_inc(sines_ready.sem, 1)

            chunks(act, body)
            sort_states(NTC - 1, 1)

        @block.vector
        def _(dve):
            for c in (var_ready, xn_ready, x_copied_v, norm2_ready, angle_ready, scanned, h3_ready):
                dve.sem_inc(c.sem, c.per)
            dve.memset(eps[:, :], EPS)
            dve.memset(state[:, 1, TC - 1, :, :], 0.0)
            for c in range(6):
                dve.wait_ge(w_turned, c + 1)
                dve.tensor_copy(wt[:, :, c, :], ps[0:HD, c, 0:2 * NB].rearrange("p (k n) -> p k n", k=2)).then_inc(w_copied, 1)
            dve.wait_ge(w_loaded, 16 * 12)
            dve.tensor_copy(wt[:, :, 6, :], dcol[:, :].unsqueeze(2).to_broadcast([HD, 2, NB])).then_inc(w_ready, 1)

            def three(v):
                return v.unsqueeze(1).to_broadcast([128, 3, SF])

            def front(tc, i, par):
                link = Chain(dve, front_chain, tc, FRONT)
                dve.wait_ge(h_loaded[par].sem, h_loaded[par].now(i))
                dve.wait_ge(y_loaded[par].sem, y_loaded[par].now(i))
                for g in range(SQ):
                    last = dve.scalar_tensor_tensor(h[:, par, g, :], y[:, par, g, :], pm[:, par, g:g + 1], h[:, par, g, :], ALU.mult, ALU.add)
                link(last)
                for g in range(SQ):
                    last = dve.bn_stats(stats[:, g, :], h[:, par, g, :])
                link(last)
                dve.sem_inc(t["held"], 1)
                for g in range(SQ):
                    last = dve.bn_aggr(mv[:, g, :], stats[:, g, :])
                last.then_inc(var_ready.sem, 1)
                dve.wait_ge(std_ready.sem, std_ready.now(tc))
                link(dve.reciprocal(rstd[:, :], std[:, :]))
                for g in range(SQ):
                    last = dve.tensor_scalar(xn[:, g, :], h[:, par, g, :], mv[:, g, 0:1], rstd[:, g:g + 1], ALU.subtract, ALU.mult)
                last.then_inc(xn_ready.sem, 1)
                for half in range(2):
                    dve.wait_ge(x_turned.sem, x_turned.now(tc, 3 + half))
                    dve.tensor_copy(xt[:, 1, half, :].rearrange("p (t b) -> p t b", b=HB),
                                    ps[0:HD, 2 + half, 0:SF].rearrange("p (b t) -> p t b", t=TC)).then_inc(x_copied_v.sem, 1)
                link.end()

            def scan(tc, par):
                link = Chain(dve, scan_chain, tc, 3 * TC)
                for s in range(TC):
                    old = state[:, par, s - 1, :, :] if s else state[:, 1 - par, TC - 1, :, :]
                    link(dve.tensor_tensor(prod[:, :, :, :].rearrange("p i j b -> p i (j b)"),
                                           mat[:, s, :, :].rearrange("p (i j) b -> p i (j b)", i=3),
                                           old.rearrange("p j b -> p (j b)").unsqueeze(1).to_broadcast([128, 3, 3 * HB]), ALU.mult))
                    dve.tensor_tensor(sum0[:, :, :], prod[:, :, 0, :], prod[:, :, 1, :], ALU.add)
                    link(dve.tensor_tensor(sum1[:, :, :], prod[:, :, 2, :], u[:, par, s, :, :], ALU.add))
                    link(dve.tensor_tensor(state[:, par, s, :, :], sum0[:, :, :], sum1[:, :, :], ALU.add))
                link.end()
                dve.sem_inc(scanned.sem, 1)

            def elem(tc):
                link = Chain(dve, elem_chain, tc, ELEM)
                dve.wait_ge(squared.sem, squared.now(tc))
                link(dve.tensor_tensor(om[:, :], sq[:, 0, :], sq[:, 1, :], ALU.add))
                dve.scalar_tensor_tensor(om[:, :], sq[:, 2, :], 1e-32, om[:, :], ALU.max, ALU.add).then_inc(norm2_ready.sem, 1)
                dve.wait_ge(theta_ready.sem, theta_ready.now(tc))
                link(dve.tensor_scalar(rnd[:, :], th[:, :], 1.0 / (2.0 * np.pi), ROUND, ALU.mult, ALU.add))
                link(dve.tensor_scalar(rnd[:, :], rnd[:, :], ROUND, None, ALU.subtract))
                src = th
                for part in TWO_PI:
                    link(dve.scalar_tensor_tensor(ang[:, :], rnd[:, :], -part, src[:, :], ALU.mult, ALU.add))
                    src = ang
                dve.tensor_scalar(ang[:, :], ang[:, :], 3.1415925, -3.1415925, ALU.min, ALU.max).then_inc(angle_ready.sem, 1)
                link(dve.tensor_scalar(th[:, :], th[:, :], 1e-8, None, ALU.max))
                link(dve.reciprocal(rnd[:, :], th[:, :]))
                dve.tensor_tensor(k[:, :, :], biv[:, :, :], three(rnd[:, :]), ALU.mult)
                dve.wait_ge(sines_ready.sem, sines_ready.now(tc))
                link(dve.scalar_tensor_tensor(om[:, :], sh[:, :], 2.0, sh[:, :], ALU.mult, ALU.mult))
                link(dve.tensor_tensor(om[:, :], om[:, :], dec[:, :], ALU.mult))
                dve.tensor_tensor(a0[:, :], dec[:, :], om[:, :], ALU.subtract)
                link(dve.tensor_tensor(sn[:, :], sn[:, :], dec[:, :], ALU.mult))
                dve.tensor_tensor(sk[:, :, :], k[:, :, :], three(sn[:, :]), ALU.mult)
                link(dve.tensor_tensor(qk[:, :, :], k[:, :, :], three(om[:, :]), ALU.mult))

                def rows(v, n):
                    return v.rearrange("p c (t b) -> p c t b", b=HB) if n > 1 else v.rearrange("p (t b) -> p t b", b=HB)

                link(dve.tensor_tensor(sq[:, :, :], qk[:, :, :], k[:, :, :], ALU.mult))
                link(dve.tensor_tensor(mat[:, :, 0:9:4, :].rearrange("p t c b -> p c t b"), rows(sq[:, :, :], 3), rows(three(a0[:, :]), 3), ALU.add))
                dve.tensor_tensor(sq[:, 0, :], qk[:, 0, :], k[:, 1, :], ALU.mult)
                dve.tensor_tensor(sq[:, 1, :], qk[:, 0, :], k[:, 2, :], ALU.mult)
                link(dve.tensor_tensor(sq[:, 2, :], qk[:, 1, :], k[:, 2, :], ALU.mult))
                for cell, p, c, op in ((1, 0, 2, ALU.subtract), (3, 0, 2, ALU.add), (2, 1, 1, ALU.add), (6, 1, 1, ALU.subtract),
                                       (5, 2, 0, ALU.subtract), (7, 2, 0, ALU.add)):
                    last = dve.tensor_tensor(mat[:, :, cell, :], rows(sq[:, p, :], 1), rows(sk[:, c, :], 1), op)
                link(last)
                link.end()

            def add(tc, par):
                for g in range(4):
                    dve.wait_ge(state_turned.sem, state_turned.now(tc, g + 1))
                    for half in range(2):
                        v = h[:, par, 4 * half + g, :].rearrange("p (k c) -> p k c", c=3)
                        last = dve.tensor_tensor(v, ps[0:ST, 3 + g, 0:3 * 128].rearrange("p (c h k) -> p h k c", c=3, h=2)[:, half, :, :], v, ALU.add)
                last.then_inc(h3_ready.sem, 1)

            def body(i, par, before):
                tc = i * 2 + par
                front(tc, i, par)
                if before:
                    scan(tc - 1, 1 - par)
                elem(tc)
                if before:
                    add(tc - 1, 1 - par)

            chunks(dve, body)
            scan(NTC - 1, 1)
            add(NTC - 1, 1)

        @block.tensor
        def _(pe):
            for c in (x_turned, made, state_turned):
                pe.sem_inc(c.sem, c.per)
            pe.wait_ge(w_loaded, 16 * 12)
            for c in range(6):
                for n in range(2):
                    last = pe.transpose(ps[0:HD, c, n * NB:(n + 1) * NB], wrow[:, c, n * HD:(n + 1) * HD], ident[0:NB, 0:NB])
                last.then_inc(w_turned, 1)
            pe.wait_ge(w_copied, 6)
            pe.wait_ge(w_ready, 1)

            def turn_states(tc):
                pe.wait_ge(state_sorted.sem, state_sorted.now(tc))
                for g in range(4):
                    for c in range(3):
                        last = pe.transpose(ps[0:ST, 3 + g, c * 128:(c + 1) * 128],
                                            state2[:, c, 8 * g:8 * g + 8, :].rearrange("p b t -> p (b t)"), ident[:, :])
                    last.then_inc(state_turned.sem, 1)

            def body(i, par, before):
                tc = i * 2 + par
                pe.wait_ge(xn_ready.sem, xn_ready.now(tc))
                for c in range(2):
                    for half in range(2):
                        for g in range(4):
                            last = pe.transpose(ps[0:HD, 2 * c + half, g * ST:(g + 1) * ST], xn[:, 4 * half + g, c * HD:(c + 1) * HD], ident[0:ST, 0:ST])
                        last.then_inc(x_turned.sem, 1)
                pe.wait_ge(x_copied_a.sem, x_copied_a.now(tc))
                pe.wait_ge(x_copied_v.sem, x_copied_v.now(tc))
                for c in range(7):
                    for half in range(2):
                        for n in range(2):
                            last = pe.matmul(ps[half * NB:(half + 1) * NB, (4 + c) % 8, 0:SF], wt[:, n, c, :], xt[:, n, half, :],
                                             start=(n == 0), stop=(n == 1))
                    last.then_inc(made.sem, 1)
                if before:
                    pe.wait_ge(made_copied.sem, made_copied.now(tc))
                    turn_states(tc - 1)

            chunks(pe, body)
            turn_states(NTC - 1)


NCLS = 6
PE_PASS = 2
PT = 2 * N
GT0 = [[0, 1, 0, 0, 1, 0], [0, 1, 0, 0, 0, 1], [0, 0, 1, 0, 1, 0], [0, 0, 1, 0, 0, 1], [0, 0, 0, 1, 1, 0], [0, 0, 0, 1, 0, 1]]
EXPERT_PAIRS = [[(j - 1, k - 1) for j in range(1, 6) for k in range(1, 6) if j != k and row[j] and row[k]] for row in GT0]


def phase_patches(nc, a, t, out):
    with ExitStack() as ctx:
        def sb(name, shape, dt=F32):
            return ctx.enter_context(nc.sbuf_tensor("p_" + name, shape, dt))

        def sem(name):
            return semaphore(nc, t, "p_" + name)

        Q = PT // RP
        ident = t["ident"]
        w1 = sb("w1", [HD, 2, FF])
        w2 = sb("w2", [128, FC, D])
        b1 = sb("b1", [128, FC])
        b2 = sb("b2", [RP, D])
        eps = sb("eps", [128, 1])
        h = sb("h", [RP, 2, Q, D])
        xn = sb("xn", [RP, 2, Q, D])
        stats = sb("stats", [RP, Q, 6])
        mv = sb("mv", [RP, Q, 2])
        std = sb("std", [RP, Q])
        rstd = sb("rstd", [RP, Q])
        xt = sb("xt", [HD, 2, 2, PT])
        ht = sb("ht", [128, FC, PT])
        y = sb("y", [RP, 2, Q, D])
        ps = ctx.enter_context(nc.psum_tensor("p_ps", [128, 8, 512], F32))

        w_loaded = sem("w_loaded")
        eps_set = sem("eps_set")
        h_loaded = [Dmas(sem(f"h_loaded{i}"), 1) for i in range(2)]
        stored = [Dmas(sem(f"stored{i}"), Q) for i in range(2)]
        var_ready = Count(sem("var_ready"), 1)
        std_ready = Count(sem("std_ready"), 1)
        xn_ready = Count(sem("xn_ready"), 1)
        h_biased = Count(sem("h_biased"), 1)
        x_turned = Count(sem("x_turned"), 2)
        x_copied_a = Count(sem("x_copied_a"), 1)
        x_copied_v = Count(sem("x_copied_v"), 1)
        up_made = Count(sem("up_made"), FC)
        gelu_done = Count(sem("gelu_done"), FC)
        down_made = Count(sem("down_made"), 2)
        y_ready = Count(sem("y_ready"), 2)
        stores_done = Count(sem("stores_done"), 1)
        chain = sem("chain")
        CHUNKS = B // 2
        block = ctx.enter_context(nc.Block())

        def chunks(eng, body):
            with eng.Fori(0, CHUNKS // 2) as i:
                body(i, 0)
                body(i, 1)

        @block.sync
        def _(sp):
            for dst, src in ((w1[:, :, :], halves(a["L1_ffn_moe0_W1"])),
                             (w2[:, :, :], a["L1_ffn_moe0_W2"].rearrange("(c p) n -> p c n", p=128)),
                             (b2[:, :], a["L1_ffn_moe0_b2"].partition_broadcast(RP))):
                sp.dma_start(dst, src).then_inc(w_loaded, 16)
            sp.dma_start(b1[:, :], a["L1_ffn_moe0_b1"].rearrange("(c p) -> p c", p=128), allow_slow_non_contiguous=True).then_inc(w_loaded, 16)
            sp.sem_inc(stores_done.sem, 2)

            def load(i, par):
                rows = t["h3"][bass.ds(i * 2 * PT + par * PT, PT), :].rearrange("(q p) d -> p q d", p=RP)
                sp.dma_start(h[:, par, :, :], rows).then_inc(h_loaded[par].sem, 16)

            def store(i, par):
                c = i * 2 + par
                sp.wait_ge(y_ready.sem, y_ready.now(c))
                sp.sem_inc(t["held"], 1)
                for q in range(Q):
                    p0 = 0 if q % 2 else NCLS
                    at = i * 2 * PT + (par * PT + q * RP + p0)
                    sp.dma_start(out[bass.ds(at, RP - p0), :], y[p0:RP, par, q, :]).then_inc(stored[par].sem, 16)

            load(0, 0)
            load(0, 1)
            with sp.Fori(0, CHUNKS // 2 - 1) as i:
                for par in range(2):
                    store(i, par)
                    load(i + 1, par)
                for par in range(2):
                    sp.wait_ge(stored[par].sem, stored[par].now(i))
                    sp.sem_inc(stores_done.sem, 1)
            for par in range(2):
                store(CHUNKS // 2 - 1, par)
            for par in range(2):
                sp.wait_ge(stored[par].sem, stored[par].now(CHUNKS // 2 - 1))

        @block.gpsimd
        def _(pool):
            pool.memset(eps[:, :], EPS).then_inc(eps_set, 1)
            pool.wait_ge(w_loaded, 16 * 4)
            pool.sem_inc(h_biased.sem, 1)

            def body(i, par):
                pool.wait_ge(xn_ready.sem, xn_ready.now(i * 2 + par))
                for q in range(Q):
                    last = pool.tensor_tensor(h[:, par, q, :], h[:, par, q, :], b2[:, :], ALU.add)
                last.then_inc(h_biased.sem, 1)

            chunks(pool, body)

        @block.scalar
        def _(act):
            for c in (std_ready, x_copied_a, gelu_done):
                act.sem_inc(c.sem, c.per)
            act.wait_ge(eps_set, 1)
            act.wait_ge(w_loaded, 16 * 4)

            def root(c):
                act.wait_ge(var_ready.sem, var_ready.now(c))
                act.activation(std[:, :], mv[:, :, 1], ACT.Sqrt, bias=eps[0:RP, :]).then_inc(std_ready.sem, 1)

            def copy_x(c, par):
                act.wait_ge(x_turned.sem, x_turned.now(c, 1))
                act.copy(xt[:, par, 0, :], ps[0:HD, 0, 0:PT]).then_inc(x_copied_a.sem, 1)

            def gelu(c):
                for f in range(FC):
                    act.wait_ge(up_made.sem, up_made.now(c, f + 1))
                    act.activation(ht[:, f, :], ps[:, 2 + f, 0:PT], ACT.Gelu, bias=b1[:, f:f + 1]).then_inc(gelu_done.sem, 1)

            root(0)
            copy_x(0, 0)
            with act.Fori(0, CHUNKS // 2 - 1) as i:
                for par in range(2):
                    root(i * 2 + par + 1)
                    gelu(i * 2 + par)
                    copy_x(i * 2 + par + 1, 1 - par)
            root(CHUNKS - 1)
            gelu(CHUNKS - 2)
            copy_x(CHUNKS - 1, 1)
            gelu(CHUNKS - 1)

        @block.vector
        def _(dve):
            for c in (var_ready, xn_ready, x_copied_v, y_ready):
                dve.sem_inc(c.sem, c.per)

            def norm(i, par):
                c = i * 2 + par
                link = Chain(dve, chain, c, 2)
                dve.wait_ge(h_loaded[par].sem, h_loaded[par].now(i))
                for q in range(Q):
                    last = dve.bn_stats(stats[:, q, :], h[:, par, q, :])
                link(last)
                dve.sem_inc(t["held"], 1)
                for q in range(Q):
                    last = dve.bn_aggr(mv[:, q, :], stats[:, q, :])
                last.then_inc(var_ready.sem, 1)
                dve.wait_ge(std_ready.sem, std_ready.now(c))
                link(dve.reciprocal(rstd[:, :], std[:, :]))
                for q in range(Q):
                    last = dve.tensor_scalar(xn[:, par, q, :], h[:, par, q, :], mv[:, q, 0:1], rstd[:, q:q + 1], ALU.subtract, ALU.mult)
                last.then_inc(xn_ready.sem, 1)
                link.end()

            def copy_x(c, par):
                dve.wait_ge(x_turned.sem, x_turned.now(c, 2))
                dve.tensor_copy(xt[:, par, 1, :], ps[0:HD, 1, 0:PT]).then_inc(x_copied_v.sem, 1)

            def result(i, par):
                c = i * 2 + par
                dve.wait_ge(h_biased.sem, h_biased.now(c))
                dve.wait_ge(stores_done.sem, i * 2 + par + 1)
                for b in range(2):
                    dve.wait_ge(down_made.sem, down_made.now(c, b + 1))
                    dve.tensor_tensor(y[:, par, 2 * b:2 * b + 2, :], ps[0:RP, 2 + b, 0:2 * D].rearrange("p (q d) -> p q d", q=2),
                                      h[:, par, 2 * b:2 * b + 2, :], ALU.add).then_inc(y_ready.sem, 1)

            norm(0, 0)
            copy_x(0, 0)
            with dve.Fori(0, CHUNKS // 2 - 1) as i:
                norm(i, 1)
                copy_x(i * 2 + 1, 1)
                result(i, 0)
                norm(i + 1, 0)
                copy_x(i * 2 + 2, 0)
                result(i, 1)
            i = CHUNKS // 2 - 1
            norm(i, 1)
            copy_x(i * 2 + 1, 1)
            result(i, 0)
            result(i, 1)

        @block.tensor
        def _(pe):
            for c in (x_turned, up_made, down_made):
                pe.sem_inc(c.sem, c.per)
            pe.wait_ge(w_loaded, 16 * 4)

            def turn_x(c, par):
                pe.wait_ge(xn_ready.sem, xn_ready.now(c))
                for n in range(2):
                    for q in range(Q):
                        last = pe.transpose(ps[0:HD, n, q * RP:(q + 1) * RP], xn[:, par, q, n * HD:(n + 1) * HD], ident[0:RP, 0:RP])
                    last.then_inc(x_turned.sem, 1)

            def chunk(c, par, more):
                pe.wait_ge(x_copied_a.sem, x_copied_a.now(c))
                pe.wait_ge(x_copied_v.sem, x_copied_v.now(c))
                for f in range(FC):
                    if f < 2:
                        pe.wait_ge(y_ready.sem, y_ready.last(c, f + 1))
                    for n in range(2):
                        last = pe.matmul(ps[:, 2 + f, 0:PT], w1[:, n, f * 128:(f + 1) * 128], xt[:, par, n, :], start=(n == 0), stop=(n == 1))
                    last.then_inc(up_made.sem, 1)
                if more:
                    turn_x(c + 1, 1 - par)
                pe.wait_ge(gelu_done.sem, gelu_done.now(c))
                for b in range(2):
                    for q in range(2):
                        at = (2 * b + q) * RP
                        for f in range(FC):
                            last = pe.matmul(ps[0:RP, 2 + b, q * D:(q + 1) * D], ht[:, f, at:at + RP], w2[:, f, :], start=(f == 0), stop=(f == FC - 1))
                    last.then_inc(down_made.sem, 1)

            turn_x(0, 0)
            with pe.Fori(0, CHUNKS // 2 - 1) as i:
                chunk(i * 2, 0, True)
                chunk(i * 2 + 1, 1, True)
            chunk(CHUNKS - 2, 0, True)
            chunk(CHUNKS - 1, 1, False)


def phase_first(nc, a, t, out):
    with ExitStack() as ctx:
        def sb(name, shape, dt=F32):
            return ctx.enter_context(nc.sbuf_tensor("f_" + name, shape, dt))

        def sem(name):
            return semaphore(nc, t, "f_" + name)

        NA = 5
        users = [[(i, s) for i in range(NCLS) for s in range(2) if EXPERT_PAIRS[i][s][0] == x] for x in range(NA)]
        place, n = {}, 0
        for x in range(NA):
            for key in users[x]:
                place[key] = n
                n += 1
        ident = t["ident"]
        w1 = sb("w1", [HD, NA, 2, FF])
        w2 = sb("w2", [128, NA, FC, D])
        b1 = sb("b1", [128, NA, FC])
        b2 = sb("b2", [B, NA, D])
        gw = sb("gw", [HD, NCLS, 2, 2])
        eps = sb("eps", [128, 1])
        h = sb("h", [B, NCLS, D])
        xn = sb("xn", [B, NCLS, D])
        stats = sb("stats", [B, NCLS, 6])
        mv = sb("mv", [B, NCLS, 2])
        std = sb("std", [B, NCLS])
        rstd = sb("rstd", [B, NCLS])
        xt = sb("xt", [HD, 2, NCLS * B])
        ht = sb("ht", [128, FC, 2 * NCLS * B])
        lg = sb("lg", [B, NCLS, 2])
        g = sb("g", [B, NCLS, 2])
        mask = sb("mask", [B, NCLS, 2])
        one = sb("one", [B, NCLS])
        e0 = sb("e0", [B, NCLS, 2, D])
        ps = ctx.enter_context(nc.psum_tensor("f_ps", [128, 8, 512], F32))

        loaded = sem("loaded")
        late = sem("late")
        chain = sem("chain")
        eps_set = sem("eps_set")
        var_ready = sem("var_ready")
        std_ready = sem("std_ready")
        xn_ready = sem("xn_ready")
        x_turned = sem("x_turned")
        x_copied = sem("x_copied")
        gate_made = sem("gate_made")
        gate_in = sem("gate_in")
        gate_exp = sem("gate_exp")
        up_made = sem("up_made")
        gelu_done = sem("gelu_done")
        down_made = sem("down_made")
        down_copied = sem("down_copied")
        y_ready = sem("y_ready")
        stored = sem("stored")
        block = ctx.enter_context(nc.Block())
        rows = t["h3"].rearrange("(b n) d -> b n d", n=N)[:, 0:NCLS, :]

        @block.sync
        def _(sp):
            for dst, src in ((h[:, :, :], rows),
                             (gw[:, :, 0, :], a["L1_ffn_G_W"].rearrange("i (c p) o -> c p i o", p=HD)[0]),
                             (gw[:, :, 1, :], a["L1_ffn_G_W"].rearrange("i (c p) o -> c p i o", p=HD)[1])):
                sp.dma_start(dst, src).then_inc(loaded, 16)
            for x in range(NA):
                sp.dma_start(w1[:, x, :, :], halves(a["L1_ffn_A1_W"][x])).then_inc(late, 16)
                sp.dma_start(b1[:, x, :], a["L1_ffn_A1_b"][x].rearrange("(c p) -> p c", p=128), allow_slow_non_contiguous=True).then_inc(late, 16)
                sp.dma_start(w2[:, x, :, :], a["L1_ffn_A2_W"][x].rearrange("(c p) n -> p c n", p=128)).then_inc(late, 16)
                sp.dma_start(b2[:, x, :], a["L1_ffn_A2_b"][x].partition_broadcast(B)).then_inc(late, 16)
            sp.wait_ge(y_ready, 1)
            sp.dma_start(out.rearrange("(b n) d -> b n d", n=N)[:, 0:NCLS, :], h[:, :, :]).then_inc(stored, 16)
            sp.wait_ge(stored, 16)

        @block.gpsimd
        def _(pool):
            pool.memset(eps[:, :], EPS).then_inc(eps_set, 1)

        @block.scalar
        def _(act):
            act.wait_ge(eps_set, 1)
            act.wait_ge(var_ready, 1)
            act.activation(std[:, :], mv[:, :, 1], ACT.Sqrt, bias=eps[0:B, :]).then_inc(std_ready, 1)
            act.wait_ge(gate_in, 1)
            act.activation(g[:, :, :], lg[:, :, :], ACT.Exp).then_inc(gate_exp, 1)
            act.wait_ge(late, 16 * 4 * NA)
            n = 0
            for x in range(NA):
                lo = place[users[x][0]] * B
                for f in range(FC):
                    act.wait_ge(up_made, n + 1)
                    w = len(users[x]) * B
                    act.activation(ht[:, f, lo:lo + w], ps[:, 3 + n % 2, 0:w], ACT.Gelu, bias=b1[:, x, f:f + 1]).then_inc(gelu_done, 1)
                    n += 1

        @block.vector
        def _(dve):
            done = [0]

            def link(ins):
                done[0] += 1
                ins.then_inc(chain, 1)
                dve.wait_ge(chain, done[0])

            dve.wait_ge(loaded, 16 * 3)
            for i in range(NCLS):
                last = dve.bn_stats(stats[:, i, :], h[:, i, :])
            link(last)
            for i in range(NCLS):
                last = dve.bn_aggr(mv[:, i, :], stats[:, i, :])
            last.then_inc(var_ready, 1)
            dve.wait_ge(std_ready, 1)
            link(dve.reciprocal(rstd[:, :], std[:, :]))
            for i in range(NCLS):
                last = dve.tensor_scalar(xn[:, i, :], h[:, i, :], mv[:, i, 0:1], rstd[:, i:i + 1], ALU.subtract, ALU.mult)
            last.then_inc(xn_ready, 1)
            for c in range(2):
                dve.wait_ge(x_turned, c + 1)
                dve.tensor_copy(xt[:, c, :], ps[0:HD, c, 0:NCLS * B]).then_inc(x_copied, 1)
            dve.wait_ge(gate_made, 1)
            link(dve.tensor_copy(lg[:, :, :], ps[0:B, 2, 0:2 * NCLS].rearrange("p (i o) -> p i o", o=2)))
            link(dve.tensor_reduce(one[:, :], lg[:, :, :], AX_X, ALU.max))
            dve.tensor_tensor(lg[:, :, :], lg[:, :, :], spread(one[:, :], 2), ALU.subtract).then_inc(gate_in, 1)
            dve.wait_ge(gate_exp, 1)
            link(dve.tensor_reduce(one[:, :], g[:, :, :], AX_X, ALU.add))
            link(dve.reciprocal(one[:, :], one[:, :]))
            link(dve.tensor_tensor(g[:, :, :], g[:, :, :], spread(one[:, :], 2), ALU.mult))
            link(dve.tensor_reduce(one[:, :], g[:, :, :], AX_X, ALU.min))
            link(dve.tensor_tensor(mask[:, :, :], g[:, :, :], spread(one[:, :], 2), ALU.is_gt))
            link(dve.tensor_tensor(g[:, :, :], g[:, :, :], mask[:, :, :], ALU.mult))
            link(dve.tensor_reduce(one[:, :], g[:, :, :], AX_X, ALU.add))
            link(dve.tensor_scalar(one[:, :], one[:, :], 1e-6, None, ALU.max))
            link(dve.reciprocal(one[:, :], one[:, :]))
            link(dve.tensor_tensor(g[:, :, :], g[:, :, :], spread(one[:, :], 2), ALU.mult))
            for i in range(NCLS):
                dve.wait_ge(down_made, i + 1)
                for s in range(2):
                    last = dve.tensor_tensor(e0[:, i, s, :], ps[0:B, 5 + i % 3, s * D:(s + 1) * D], b2[:, EXPERT_PAIRS[i][s][1], :], ALU.add)
                last.then_inc(down_copied, 1)
                dve.wait_ge(down_copied, i + 1)
                for s in range(2):
                    link(dve.scalar_tensor_tensor(h[:, i, :], e0[:, i, s, :], g[:, i, s:s + 1], h[:, i, :], ALU.mult, ALU.add))
            dve.sem_inc(y_ready, 1)

        @block.tensor
        def _(pe):
            pe.wait_ge(xn_ready, 1)
            for c in range(2):
                for i in range(NCLS):
                    last = pe.transpose(ps[0:HD, c, i * B:(i + 1) * B], xn[:, i, c * HD:(c + 1) * HD], ident[0:B, 0:B])
                last.then_inc(x_turned, 1)
            pe.wait_ge(x_copied, 2)
            for i in range(NCLS):
                for c in range(2):
                    last = pe.matmul(ps[0:B, 2, 2 * i:2 * i + 2], xt[:, c, i * B:(i + 1) * B], gw[:, i, c, :], start=(c == 0), stop=(c == 1))
            last.then_inc(gate_made, 1)
            pe.wait_ge(late, 16 * 4 * NA)
            n = 0
            for x in range(NA):
                tokens = [i for i, _ in users[x]]
                step = tokens[1] - tokens[0]
                assert tokens == list(range(tokens[0], tokens[-1] + 1, step))
                for f in range(FC):
                    if n >= 2:
                        pe.wait_ge(gelu_done, n - 1)
                    for c in range(2):
                        cols = xt[:, c, :].rearrange("p (i b) -> p i b", b=B)[:, tokens[0]:tokens[-1] + 1:step, :]
                        last = pe.matmul(ps[:, 3 + n % 2, 0:len(tokens) * B].rearrange("p (i b) -> p i b", b=B), w1[:, x, c, f * 128:(f + 1) * 128], cols,
                                         start=(c == 0), stop=(c == 1))
                    last.then_inc(up_made, 1)
                    n += 1
            pe.wait_ge(gelu_done, NA * FC)
            for i in range(NCLS):
                if i >= 3:
                    pe.wait_ge(down_copied, i - 2)
                for s in range(2):
                    at = place[(i, s)] * B
                    for f in range(FC):
                        last = pe.matmul(ps[0:B, 5 + i % 3, s * D:(s + 1) * D], ht[:, f, at:at + B], w2[:, EXPERT_PAIRS[i][s][1], f, :],
                                         start=(f == 0), stop=(f == FC - 1))
                last.then_inc(down_made, 1)


def vit_tower(nc, a, out):
    t = dram(nc)
    t["held"] = nc.alloc_semaphore("held")
    t["in_use"] = []
    out = out.rearrange("b n d -> (b n) d")
    with nc.sbuf_tensor("ident", [128, 128], F32) as ident:
        t["ident"] = ident
        with ExitStack() as ctx:
            keep(nc, ctx, t)
            phase_setup(nc, a, t)
            clear(nc, t)
            phase_tokens(nc, a, t)
        clear(nc, t)
        phase_route(nc, a, t)
        clear(nc, t)
        phase_experts(nc, a, t)
        clear(nc, t)
        phase_states(nc, a, t)
        clear(nc, t)
        phase_patches(nc, a, t, out)
        clear(nc, t)
        phase_first(nc, a, t, out)


def kernel(**inputs):
    import concourse.bacc as bacc
    from concourse.bass_utils import run_bass_kernel_spmd

    nc = bacc.Bacc("TRN2", target_bir_lowering=False, num_devices=1)
    arrays = {k: np.ascontiguousarray(v) for k, v in inputs.items() if k != "L1_ffn_mids"}
    arrays.update(constants())
    a = {k: nc.dram_tensor("in_" + k, v.shape, mybir.dt.from_np(v.dtype), kind="ExternalInput").ap() for k, v in arrays.items()}
    out = nc.dram_tensor("out", (B, N, D), F32, kind="ExternalOutput").ap()
    vit_tower(nc, a, out)
    r = run_bass_kernel_spmd(nc, [{"in_" + k: v for k, v in arrays.items()}], core_ids=[0])
    return r.results[0]["out"]
```

```python
from contextlib import ExitStack

import numpy as np

import concourse.bass as bass
from concourse import mybir

F32 = mybir.dt.float32
I32 = mybir.dt.int32
U32 = mybir.dt.uint32
ALU = mybir.AluOpType
ACT = mybir.ActivationFunctionType
AX_X = mybir.AxisListType.X

B = 64
C_IN, IMG, PATCH = 3, 224, 16
GRID = IMG // PATCH
N = GRID * GRID
D = 192
HD = D // 2
TOK = B * N
H, DH = 12, 64
HW = H * DH
SIDE = 13
ROWS = 15
LREL = 14
CAP = int(1.25 * TOK / 8)
NE = 8
FF = 768
FC = FF // 128
SLOTS = NE * CAP
EPS = 1e-5
QK_SCALE = DH ** -0.5

NV = 2 * LREL + 2
NHR = 2 * SIDE - 1
TR = NV + NHR
TW = TR * H
VRUN, HRUN = ROWS * H, SIDE * H
AUG = 32
CLS = ROWS + SIDE
ONE = CLS + 1
VW = DH + ONE + 1
UC = TW // 6

PAIRS = B // 2
TM = 104
T0 = N - TM
SPI = C_IN * GRID
PST = 2 * SPI
TILE0 = [0, T0]
PART = [T0, TM]


class Count:

    def __init__(self, sem, per):
        self.sem, self.per = sem, per

    def now(self, it, k=None):
        return it * self.per + self.per + (self.per if k is None else k)

    def last(self, it, k=None):
        return it * self.per + (self.per if k is None else k)


class Dmas:

    def __init__(self, sem, per):
        self.sem, self.per = sem, per

    def now(self, it, k=None):
        return (it * self.per + (self.per if k is None else k)) * 16


def semaphore(nc, t, name):
    t["in_use"].append(nc.alloc_semaphore(name))
    return t["in_use"][-1]


def clear(nc, t):
    nc.clear_and_free_semaphores(t["in_use"])
    t["in_use"] = []
    nc.all_engine_barrier()


def halves(w):
    return w.rearrange("(c p) n -> p c n", p=HD)


def phase_setup(nc, a, t):
    with ExitStack() as ctx:
        def sb(name, shape, dt=F32):
            return ctx.enter_context(nc.sbuf_tensor(name, shape, dt))

        def sem(name):
            return semaphore(nc, t, name)

        w_tok = sb("su_w_tok", [HD, 2, 4 * D])
        wp_h = sb("su_wp_h", [DH, H, D])
        tab = sb("su_tab", [TR, 2, DH])
        tab0 = sb("su_tab0", [1, 2, DH])
        tab_t = sb("su_tab_t", [DH, 2, TR])
        wq_t = sb("su_wq_t", [DH, 2, 2, HD])
        u_h = sb("su_u_h", [TR, 2, D])
        zero = sb("su_zero", [120, 1536])
        ps = ctx.enter_context(nc.psum_tensor("su_ps", [128, 8, 512], F32))

        loaded = sem("su_loaded")
        added = sem("su_added")
        tables_turned = sem("su_tables_turned")
        tables_copied = sem("su_tables_copied")
        tok_turned = sem("su_tok_turned")
        tok_copied = sem("su_tok_copied")
        wq_turned = sem("su_wq_turned")
        wq_copied = sem("su_wq_copied")
        cq_made = sem("su_cq_made")
        cq_copied = sem("su_cq_copied")
        u_made = sem("su_u_made")
        u_copied = sem("su_u_copied")
        u_stored = [sem(f"su_u_stored{i}") for i in range(2)]
        u_loaded = sem("su_u_loaded")
        cleared = sem("su_cleared")
        zeroed = sem("su_zeroed")
        aug_cleared = sem("su_aug_cleared")

        u_dram = t["u"].rearrange("(r h) e -> r h e", h=H)

        block = ctx.enter_context(nc.Block())

        @block.sync
        def _(sp):
            loads = [(t["ident"][:, :], a["const_ident"]), (w_tok[:, :, :], halves(a["L0_tok_W"])),
                     (t["wq"][:, :, :], halves(a["L0_attn_Wq"])), (t["wk"][:, :, :], halves(a["L0_attn_Wk"])),
                     (t["wv"][:, :, :], halves(a["L0_attn_Wv"])),
                     (t["wp2"][:, :, :], a["L0_attn_Wp"].rearrange("(c p) n -> p c n", p=128)),
                     (wp_h[:, :, :], a["L0_attn_Wp"].rearrange("(h p) n -> p h n", p=DH)),
                     (t["sw"][:, :, :], halves(a["L0_ffn_switch_w"])),
                     (t["b_tok"][:, :], a["L0_tok_b"].partition_broadcast(TM)),
                     (t["b_proj"][:, :], a["L0_attn_bp"].partition_broadcast(TM)),
                     (t["b_gate"][:, :], a["L0_ffn_switch_b"].partition_broadcast(TM))]
            for k, (v, h) in enumerate((("tvk", "thk"), ("tvv", "thv"))):
                loads += [(tab[0:NV, k, :], a["L0_attn_" + v]),
                          (tab[NV:TR, k, :], a["L0_attn_" + h][LREL + 2 - SIDE:LREL + 1 + SIDE, :]),
                          (tab0[0:1, k, :], a["L0_attn_" + h][0:1, :])]
            for h in range(H):
                loads.append((t["ka"][DH:DH + AUG, h, :], a["const_key_aug"]))
            for q in range(4):
                loads.append((t["va"][:, q, :, DH:VW], a["const_val_aug"][q % 2]))
            for dst, src in loads:
                sp.dma_start(dst, src).then_inc(loaded, 16)
            sp.wait_ge(cleared, 1)
            rows = 960
            xs = t["xs"]
            n_big = SLOTS // rows
            for r in range(n_big):
                sp.dma_start(xs[r * rows:(r + 1) * rows, :].rearrange("(p r) d -> p (r d)", p=120),
                             zero[:, :]).then_inc(zeroed, 16)
            left = SLOTS - n_big * rows
            sp.dma_start(xs[n_big * rows:SLOTS, :].rearrange("(p r) d -> p (r d)", p=40),
                         zero[0:40, 0:left // 40 * D]).then_inc(zeroed, 16)
            for i in range(2):
                for j in range(2):
                    sp.dma_start(t["pr"][i, j * 98 * TW:(j + 1) * 98 * TW].rearrange("(p f) -> p f", p=98),
                                 zero[0:98, 0:TW]).then_inc(zeroed, 16)
            for h in range(H):
                sp.wait_ge(u_copied, h + 1)
                sp.dma_start(u_dram[:, h, :], u_h[:, h % 2, :]).then_inc(u_stored[h % 2], 16)
            for i in range(2):
                sp.wait_ge(u_stored[i], 16 * H // 2)
            sp.dma_start(t["u_sb"][:, :, :], t["u"].rearrange("(c p) e -> p c e", p=UC)).then_inc(u_loaded, 16)
            sp.wait_ge(u_loaded, 16)
            sp.wait_ge(zeroed, 16 * (n_big + 5))

        @block.gpsimd
        def _(pool):
            pool.memset(zero[:, :], 0.0).then_inc(cleared, 1)
            pool.memset(t["eps"][:, :], EPS)
            pool.memset(t["qaug"][:, :, :, :], 0.0).then_inc(aug_cleared, 1)
            pool.wait_ge(aug_cleared, 1)

        n_loads = 11 + 6 + H + 4

        @block.vector
        def _(dve):
            dve.wait_ge(loaded, 16 * n_loads)
            dve.tensor_tensor(tab[0:1, :, :], tab[0:1, :, :], tab0[:, :, :], ALU.add).then_inc(added, 1)
            dve.wait_ge(tables_turned, 1)
            dve.tensor_copy(tab_t[:, :, :], ps[0:DH, 0, 0:2 * TR].rearrange("p (k r) -> p k r", k=2)).then_inc(tables_copied, 1)
            for c in range(6):
                dve.wait_ge(tok_turned, c + 1)
                dve.tensor_copy(t["w_tok_t"][:, c, :], ps[:, 1 + c % 3, 0:D]).then_inc(tok_copied, 1)
            for h in range(H):
                dve.wait_ge(wq_turned, h + 1)
                if h >= 2:
                    dve.wait_ge(cq_made, h - 1)
                dve.tensor_copy(wq_t[:, h % 2, :, :],
                                ps[0:DH, 4 + h % 2, 0:D].rearrange("p (c e) -> p c e", c=2)).then_inc(wq_copied, 1)
            for h in range(H):
                dve.wait_ge(u_made, h + 1)
                if h >= 2:
                    dve.wait_ge(u_stored[h % 2], 16 * (h // 2))
                dve.tensor_copy(u_h[:, h % 2, :], ps[0:TR, 1 + h % 2, 0:D]).then_inc(u_copied, 1)

        @block.scalar
        def _(act):
            for h in range(H):
                act.wait_ge(cq_made, h + 1)
                act.mul(t["cq"].rearrange("p c (r h) -> p c r h", h=H)[:, :, :, h],
                        ps[0:HD, 6 + h % 2, 0:2 * TR].rearrange("p (c r) -> p c r", c=2), QK_SCALE).then_inc(cq_copied, 1)
            act.wait_ge(cq_copied, H)

        @block.tensor
        def _(pe):
            ident = t["ident"]
            pe.wait_ge(loaded, 16 * n_loads)
            pe.wait_ge(added, 1)
            for k in range(2):
                last = pe.transpose(ps[0:DH, 0, k * TR:(k + 1) * TR], tab[:, k, :], ident[0:TR, 0:TR])
            last.then_inc(tables_turned, 1)
            for c in range(6):
                if c >= 3:
                    pe.wait_ge(tok_copied, c - 2)
                for k in range(2):
                    last = pe.transpose(ps[:, 1 + c % 3, k * HD:(k + 1) * HD], w_tok[:, k, c * 128:(c + 1) * 128],
                                        ident[0:HD, 0:HD])
                last.then_inc(tok_turned, 1)
            pe.wait_ge(tables_copied, 1)
            for h in range(H):
                if h >= 2:
                    pe.wait_ge(wq_copied, h - 1)
                for k in range(2):
                    last = pe.transpose(ps[0:DH, 4 + h % 2, k * HD:(k + 1) * HD],
                                        t["wq"][:, k, h * DH:(h + 1) * DH], ident[0:HD, 0:HD])
                last.then_inc(wq_turned, 1)
                pe.wait_ge(wq_copied, h + 1)
                if h >= 2:
                    pe.wait_ge(cq_copied, h - 1)
                for k in range(2):
                    last = pe.matmul(ps[0:HD, 6 + h % 2, k * TR:(k + 1) * TR], wq_t[:, h % 2, k, :],
                                     tab_t[:, 0, :], start=True, stop=True)
                last.then_inc(cq_made, 1)
            pe.wait_ge(tok_copied, 6)
            for h in range(H):
                if h >= 2:
                    pe.wait_ge(u_copied, h - 1)
                pe.matmul(ps[0:TR, 1 + h % 2, 0:D], tab_t[:, 1, :], wp_h[:, h, :], start=True, stop=True).then_inc(u_made, 1)


class Chain:

    def __init__(self, eng, sem, it, per):
        self.eng, self.sem, self.it, self.per, self.k = eng, sem, it, per, 0

    def __call__(self, instruction):
        self.k += 1
        instruction.then_inc(self.sem, 1)
        self.eng.wait_ge(self.sem, self.it * self.per + self.k)

    def end(self):
        assert self.k == self.per, self.k


def spread(ap, n):
    return ap.unsqueeze(2).to_broadcast([ap.shape[0], ap.shape[1], n])


def phase_tokens(nc, a, t):
    with ExitStack() as ctx:
        def sb(name, shape, dt=F32):
            return ctx.enter_context(nc.sbuf_tensor("a_" + name, shape, dt))

        def sem(name):
            return semaphore(nc, t, "a_" + name)

        NT = 2 * N
        raw = sb("raw", [PST, PATCH * IMG])
        pix = sb("pix", [PST, GRID, PATCH * PATCH])
        pt = sb("pt", [128, 2, PST * GRID])
        h_sb = sb("h", [TM, 4, D])
        xn = sb("xn", [TM, 4, D])
        stats = sb("stats", [TM, 4, 6])
        mv = sb("mv", [TM, 4, 2])
        std = sb("std", [TM, 4])
        rstd = sb("rstd", [TM, 4])
        xt = sb("xt", [HD, 2, NT])
        qt = sb("qt", [TM, 4, TW])
        qa = sb("qa", [DH + AUG, H, NT])
        qrow = sb("qrow", [TM, 4, H, AUG])
        probs = sb("probs", [TM, 2, 2, N])
        pts = sb("pts", [TM, 2, 2, N])
        shift = sb("shift", [TM, 2, 2])
        rl = sb("rl", [TM, 2, 4])
        on = sb("on", [TM, 2, 2, HW])
        rel = sb("rel", [TM, 2, 2, ONE + 1, H])
        pf = sb("pf", [TM, 2, 2, TW])
        ot = sb("ot", [128, 6, N])
        pft = sb("pft", [UC, 6, N])
        lg = sb("lg", [TM, 4, NE])
        ka, va, qaug, ident = t["ka"], t["va"], t["qaug"], t["ident"]
        ps = ctx.enter_context(nc.psum_tensor("a_ps", [128, 8, 512], F32))

        patch_turned = Count(sem("patch_turned"), 6)
        patch_copied_a = Count(sem("patch_copied_a"), 3)
        patch_copied_v = Count(sem("patch_copied_v"), 3)
        tok_made = Count(sem("tok_made"), 2)
        embedded = Count(sem("embedded"), 2)
        var_ready = Count(sem("var_ready"), 2)
        std_ready = Count(sem("std_ready"), 2)
        xn_ready = Count(sem("xn_ready"), 2)
        x_turned = Count(sem("x_turned"), 4)
        x_copied_a = Count(sem("x_copied_a"), 2)
        x_copied_v = Count(sem("x_copied_v"), 2)
        LIN = [("qt", q, n) for q in range(4) for n in range(2)]
        LIN += [("v", q, n) for q in range(4) for n in range(2)]
        LIN += [("q", c, 0) for c in range(6)] + [("k", c, 0) for c in range(6)]
        LIN += [("aug", g, 0) for g in range(3)]
        NL = len(LIN)
        lin_made = Count(sem("lin_made"), NL)
        lin_copied_a = Count(sem("lin_copied_a"), (NL + 1) // 2)
        lin_copied_v = Count(sem("lin_copied_v"), NL // 2)
        pix_ready = Count(sem("pix_ready"), 1)
        biased = Count(sem("biased"), 1)
        token0_set = Count(sem("token0_set"), 1)
        aug_fixed = Count(sem("aug_fixed"), 1)
        U = 2 * H
        scored = Count(sem("scored"), U)
        shift_ready = Count(sem("shift_ready"), U)
        probs_ready = Count(sem("probs_ready"), U)
        probs_turned = Count(sem("probs_turned"), U)
        probs_copied = Count(sem("probs_copied"), U)
        heads_made = Count(sem("heads_made"), U)
        heads_copied = Count(sem("heads_copied"), 6)
        TAIL = 7
        tail_made = Count(sem("tail_made"), 2 * TAIL)
        tail_copied_a = Count(sem("tail_copied_a"), 6)
        tail_copied_v = Count(sem("tail_copied_v"), 8)
        gate_made = Count(sem("gate_made"), 1)
        gate_ready = Count(sem("gate_ready"), 1)
        stores_done = Count(sem("stores_done"), 1)
        raw_loaded = Dmas(sem("raw_loaded"), 1)
        qt_stored = Dmas(sem("qt_stored"), 4)
        aug_loaded = Dmas(sem("aug_loaded"), 8)
        rel_stored = Dmas(sem("rel_stored"), 14)
        pf_loaded = [Dmas(sem(f"pf_loaded{i}"), 2) for i in range(2)]
        stored = Dmas(sem("stored"), 12)
        dve_chain = sem("dve_chain")
        CHAINED = 2 * 2 + 6

        strips = a["x"].rearrange("b c (g i) w -> (b c g) (i w)", i=PATCH)
        qt_rows = t["qt"].rearrange("i (n f) -> i n f", f=TW)
        GROUPS = [(half, w0, min(w0 + 6, GRID)) for half in range(2) for w0 in range(0, GRID, 6)]

        def skew(dram, im, tile, base, run):
            first, rows = (1, 7) if tile == 0 else (T0, 8)
            rn = (first - 1) // SIDE
            at = im * N * TW + first * TW
            if base == 0:
                at += (LREL + 1 - rn) * H
                return bass.AP(dram.tensor, at, [[SIDE * TW - H, rows], [TW, SIDE], [1, run]])
            at += NV * H + (SIDE - 1) * H
            return bass.AP(dram.tensor, at, [[SIDE * TW, rows], [TW - H, SIDE], [1, run]])

        def tail_copy(k):
            im, j = divmod(k, TAIL)
            return (tail_copied_a, 3 * im + j // 2 + 1) if j in (0, 2, 4) else (tail_copied_v, 4 * im + {1: 1, 3: 2, 5: 3, 6: 4}[j])

        block = ctx.enter_context(nc.Block())

        @block.sync
        def _(sp):
            sp.sem_inc(stores_done.sem, 1)
            sp.dma_start(raw[:, :], strips[0:PST, :]).then_inc(raw_loaded.sem, 16)

            def one(it, more):
                if more:
                    sp.wait_ge(pix_ready.sem, pix_ready.now(it))
                    sp.dma_start(raw[:, :], strips[bass.ds(it * PST + PST, PST), :]).then_inc(raw_loaded.sem, 16)
                for q in range(4):
                    im, tile = divmod(q, 2)
                    sp.wait_ge(lin_copied_a.sem, lin_copied_a.now(it, q + 1))
                    sp.sem_inc(t["held"], 1)
                    sp.wait_ge(lin_copied_v.sem, lin_copied_v.now(it, q + 1))
                    sp.dma_start(qt_rows[im, TILE0[tile]:TILE0[tile] + PART[tile], :],
                                 qt[0:PART[tile], q, :]).then_inc(qt_stored.sem, 16)
                sp.wait_ge(qt_stored.sem, qt_stored.now(it))
                for q in range(4):
                    im, tile = divmod(q, 2)
                    p0 = 1 - tile
                    for base, r0, run in ((0, 0, VRUN), (1, ROWS, HRUN)):
                        sp.dma_start(qaug[p0:PART[tile], q, r0:r0 + run // H, :].rearrange("p r h -> p (r h)"),
                                     skew(t["qt"], im, tile, base, run)).then_inc(aug_loaded.sem, 16)
                for im in range(2):
                    sp.wait_ge(heads_copied.sem, heads_copied.now(it, 3 * (im + 1)))
                    for tile in range(2):
                        p0, p1 = 1 - tile, PART[tile]
                        for base, r0, run in ((0, 0, VRUN), (1, ROWS, HRUN)):
                            sp.dma_start(skew(t["pr"], im, tile, base, run),
                                         rel[p0:p1, im, tile, r0:r0 + run // H, :].rearrange("p r h -> p (r h)")).then_inc(rel_stored.sem, 16)
                        sp.dma_start(t["pr"][im].rearrange("(n f) -> n f", f=TW)[TILE0[tile] + p0:TILE0[tile] + p1, 0:H],
                                     rel[p0:p1, im, tile, CLS, :]).then_inc(rel_stored.sem, 16)
                    sp.dma_start(t["pr"][im:im + 1, 0:H], rel[0:1, im, 0, ONE, :]).then_inc(rel_stored.sem, 16)
                    sp.wait_ge(rel_stored.sem, rel_stored.now(it, 7 * (im + 1)))
                    for tile in range(2):
                        sp.dma_start(pf[0:PART[tile], im, tile, :],
                                     t["pr"][im].rearrange("(n f) -> n f", f=TW)[TILE0[tile]:TILE0[tile] + PART[tile], :]
                                     ).then_inc(pf_loaded[im].sem, 16)
                sp.wait_ge(xn_ready.sem, xn_ready.now(it, 2))
                for q in range(4):
                    im, tile = divmod(q, 2)
                    at = it * NT + (im * N + TILE0[tile])
                    sp.dma_start(t["h1"][bass.ds(at, PART[tile]), :], h_sb[0:PART[tile], q, :]).then_inc(stored.sem, 16)
                    sp.dma_start(t["ys"][bass.ds(at + SLOTS, PART[tile]), :], xn[0:PART[tile], q, :]).then_inc(stored.sem, 16)
                sp.wait_ge(gate_ready.sem, gate_ready.now(it))
                for q in range(4):
                    im, tile = divmod(q, 2)
                    at = it * NT + (im * N + TILE0[tile])
                    sp.dma_start(t["lg"][bass.ds(at, PART[tile]), :], lg[0:PART[tile], q, :]).then_inc(stored.sem, 16)
                sp.wait_ge(stored.sem, stored.now(it))
                sp.sem_inc(stores_done.sem, 1)

            with sp.Fori(0, PAIRS - 1) as it:
                one(it, True)
            one(PAIRS - 1, False)

        @block.gpsimd
        def _(pool):
            for c in (pix_ready, biased, token0_set, aug_fixed):
                pool.sem_inc(c.sem, 1)
            with pool.Fori(0, PAIRS) as it:
                pool.wait_ge(raw_loaded.sem, raw_loaded.now(it))
                pool.wait_ge(patch_turned.sem, patch_turned.last(it))
                pool.sem_inc(t["held"], 1)
                pool.tensor_copy(pix[:, :, :].rearrange("p w (i j) -> p i w j", j=PATCH),
                                 raw[:, :].rearrange("p (i w j) -> p i w j", i=PATCH, j=PATCH)).then_inc(pix_ready.sem, 1)
                pool.wait_ge(xn_ready.sem, xn_ready.now(it, 1))
                for q in range(4):
                    last = pool.tensor_tensor(h_sb[:, q, :], h_sb[:, q, :], t["b_proj"][:, :], ALU.add)
                last.then_inc(biased.sem, 1)
                pool.wait_ge(lin_copied_a.sem, lin_copied_a.now(it, 4))
                pool.wait_ge(lin_copied_v.sem, lin_copied_v.now(it, 4))
                pool.sem_inc(t["held"], 1)
                for q in range(4):
                    last = pool.tensor_copy(qaug[:, q, CLS, :], qt[:, q, 0:H])
                for q in (0, 2):
                    last = pool.tensor_copy(qaug[0:1, q, 0:ROWS, :], qt[0:1, q, 0:H].unsqueeze(1).to_broadcast([1, ROWS, H]))
                last.then_inc(token0_set.sem, 1)
                pool.wait_ge(token0_set.sem, token0_set.now(it))
                pool.wait_ge(aug_loaded.sem, aug_loaded.now(it))
                pool.sem_inc(t["held"], 1)
                for q in range(4):
                    last = pool.tensor_copy(qrow[:, q, :, :].rearrange("p h r -> p r h"), qaug[:, q, :, :])
                last.then_inc(aug_fixed.sem, 1)

        @block.scalar
        def _(act):
            for c in (patch_copied_a, std_ready, x_copied_a, lin_copied_a, probs_ready, tail_copied_a):
                act.sem_inc(c.sem, c.per)
            with act.Fori(0, PAIRS) as it:
                for g in (0, 2, 4):
                    half, w0, w1 = GROUPS[g]
                    act.wait_ge(patch_turned.sem, patch_turned.now(it, g + 1))
                    act.copy(pt[:, half, :].rearrange("p (s w) -> p w s", w=GRID)[:, w0:w1, :],
                             ps[:, g, 0:(w1 - w0) * PST].rearrange("p (w s) -> p w s", s=PST)).then_inc(patch_copied_a.sem, 1)

                def norm_step(n):
                    act.wait_ge(var_ready.sem, var_ready.now(it, n + 1))
                    act.activation(std[:, :], mv[:, :, 1], ACT.Sqrt, bias=t["eps"][0:TM, :]).then_inc(std_ready.sem, 1)
                    act.wait_ge(x_turned.sem, x_turned.now(it, 2 * n + 1))
                    act.copy(xt[:, 0, :], ps[0:HD, 4 * n, 0:NT]).then_inc(x_copied_a.sem, 1)

                norm_step(0)
                for j in range(0, NL, 2):
                    act.wait_ge(lin_made.sem, lin_made.now(it, j + 1))
                    bank, (kind, c, n) = (2 + j) % 8, LIN[j]
                    if kind == "qt":
                        last = act.copy(qt[:, c, n * TW // 2:(n + 1) * TW // 2], ps[0:TM, bank, 0:TW // 2])
                    elif kind == "v":
                        last = act.copy(va[:, c, 6 * n:6 * n + 6, 0:DH], ps[0:TM, bank, 0:HW // 2].rearrange("p (h d) -> p h d", d=DH))
                    elif kind == "q":
                        for s in range(2):
                            last = act.mul(qa[0:DH, 2 * c + s, :], ps[DH * s:DH * s + DH, bank, 0:NT], QK_SCALE)
                    elif kind == "k":
                        for s in range(2):
                            last = act.copy(ka[0:DH, 2 * c + s, :], ps[DH * s:DH * s + DH, bank, 0:NT])
                    else:
                        for s in range(4):
                            last = act.copy(qa[DH:DH + AUG, 4 * c + s, :], ps[AUG * s:AUG * s + AUG, bank, 0:NT])
                    last.then_inc(lin_copied_a.sem, 1)
                for u in range(U):
                    act.wait_ge(shift_ready.sem, shift_ready.now(it, u + 1))
                    if u >= 2:
                        act.wait_ge(probs_turned.sem, probs_turned.now(it, u - 1))
                    for tile in range(2):
                        last = act.activation(probs[:, u % 2, tile, :], ps[0:TM, u % 2, tile * N:(tile + 1) * N], ACT.Exp,
                                              bias=shift[:, u % 2, tile:tile + 1])
                    last.then_inc(probs_ready.sem, 1)
                for k in range(2 * TAIL):
                    im, j = divmod(k, TAIL)
                    if j in (0, 2, 4):
                        act.wait_ge(tail_made.sem, tail_made.now(it, k + 1))
                        if j < 3:
                            last = act.copy(ot[:, 2 * j:2 * j + 2, :], ps[:, k % 4, 0:2 * N].rearrange("p (c n) -> p c n", c=2))
                        else:
                            last = act.copy(pft[:, 2 * j - 6:2 * j - 4, :], ps[0:UC, k % 4, 0:2 * N].rearrange("p (c n) -> p c n", c=2))
                        last.then_inc(tail_copied_a.sem, 1)
                norm_step(1)

        @block.vector
        def _(dve):
            for c in (patch_copied_v, embedded, var_ready, xn_ready, x_copied_v, lin_copied_v, shift_ready, probs_copied,
                      heads_copied, tail_copied_v, gate_ready):
                dve.sem_inc(c.sem, c.per)
            with dve.Fori(0, PAIRS) as it:
                link = Chain(dve, dve_chain, it, CHAINED)

                def norm_step(n):
                    for q in range(4):
                        last = dve.bn_stats(stats[:, q, :], h_sb[:, q, :])
                    link(last)
                    dve.sem_inc(t["held"], 1)
                    for q in range(4):
                        last = dve.bn_aggr(mv[:, q, :], stats[:, q, :])
                    last.then_inc(var_ready.sem, 1)
                    dve.wait_ge(std_ready.sem, std_ready.now(it, n + 1))
                    link(dve.reciprocal(rstd[:, :], std[:, :]))
                    for q in range(4):
                        last = dve.tensor_scalar(xn[:, q, :], h_sb[:, q, :], mv[:, q, 0:1], rstd[:, q:q + 1], ALU.subtract, ALU.mult)
                    last.then_inc(xn_ready.sem, 1)
                    dve.wait_ge(x_turned.sem, x_turned.now(it, 2 * n + 2))
                    dve.tensor_copy(xt[:, 1, :], ps[0:HD, 4 * n + 1, 0:NT]).then_inc(x_copied_v.sem, 1)

                for g in (1, 3, 5):
                    half, w0, w1 = GROUPS[g]
                    dve.wait_ge(patch_turned.sem, patch_turned.now(it, g + 1))
                    dve.tensor_copy(pt[:, half, :].rearrange("p (s w) -> p w s", w=GRID)[:, w0:w1, :],
                                    ps[:, g, 0:(w1 - w0) * PST].rearrange("p (w s) -> p w s", s=PST)).then_inc(patch_copied_v.sem, 1)
                dve.wait_ge(stores_done.sem, stores_done.last(it))
                for im in range(2):
                    dve.wait_ge(tok_made.sem, tok_made.now(it, im + 1))
                    dve.tensor_tensor(h_sb[:, 2 * im:2 * im + 2, :], ps[0:TM, 6 + im, 0:2 * D].rearrange("p (q d) -> p q d", q=2),
                                      t["b_tok"][:, :].unsqueeze(1).to_broadcast([TM, 2, D]), ALU.add).then_inc(embedded.sem, 1)
                dve.wait_ge(embedded.sem, embedded.now(it))
                norm_step(0)
                for j in range(1, NL, 2):
                    dve.wait_ge(lin_made.sem, lin_made.now(it, j + 1))
                    bank, (kind, c, n) = (2 + j) % 8, LIN[j]
                    if kind == "qt":
                        last = dve.tensor_copy(qt[:, c, n * TW // 2:(n + 1) * TW // 2], ps[0:TM, bank, 0:TW // 2])
                    elif kind == "v":
                        last = dve.tensor_copy(va[:, c, 6 * n:6 * n + 6, 0:DH], ps[0:TM, bank, 0:HW // 2].rearrange("p (h d) -> p h d", d=DH))
                    elif kind == "q":
                        for s in range(2):
                            last = dve.tensor_scalar(qa[0:DH, 2 * c + s, :], ps[DH * s:DH * s + DH, bank, 0:NT], QK_SCALE, None, ALU.mult)
                    elif kind == "k":
                        for s in range(2):
                            last = dve.tensor_copy(ka[0:DH, 2 * c + s, :], ps[DH * s:DH * s + DH, bank, 0:NT])
                    else:
                        for s in range(4):
                            last = dve.tensor_copy(qa[DH:DH + AUG, 4 * c + s, :], ps[AUG * s:AUG * s + AUG, bank, 0:NT])
                    last.then_inc(lin_copied_v.sem, 1)
                for s in range(U + 5):
                    if s < U:
                        dve.wait_ge(scored.sem, scored.now(it, s + 1))
                        if s >= 2:
                            dve.wait_ge(probs_ready.sem, probs_ready.now(it, s - 1))
                        dve.tensor_reduce(shift[:, s % 2, :], ps[0:TM, s % 2, 0:NT].rearrange("p (q m) -> p q m", q=2), AX_X, ALU.max,
                                          negate=True).then_inc(shift_ready.sem, 1)
                    if 0 <= s - 2 < U:
                        u = s - 2
                        dve.wait_ge(probs_turned.sem, probs_turned.now(it, u + 1))
                        if u >= 2:
                            dve.wait_ge(heads_made.sem, heads_made.now(it, u - 1))
                        dve.tensor_copy(pts[:, u % 2, :, :], ps[0:TM, 2 + u % 2, 0:NT].rearrange("p (q n) -> p q n", q=2)).then_inc(probs_copied.sem, 1)
                    if s >= 7 and (s - 7) % 4 == 0 and (s - 7) // 4 < 6:
                        grp = (s - 7) // 4
                        im, g = divmod(grp, 3)
                        dve.wait_ge(heads_made.sem, heads_made.now(it, 4 * grp + 4))
                        acc = ps[0:TM, 4 + 2 * (grp % 2):6 + 2 * (grp % 2), 0:4 * VW].rearrange("p q (h w) -> p q h w", w=VW)
                        link(dve.reciprocal(rl[:, :, :], acc[:, :, :, VW - 1]))
                        for tile in range(2):
                            dve.tensor_tensor(on[:, im, tile, 4 * g * DH:(4 * g + 4) * DH].rearrange("p (h d) -> p h d", d=DH),
                                              acc[:, tile, :, 0:DH], spread(rl[:, tile, :], DH), ALU.mult)
                            last = dve.tensor_tensor(rel[:, im, tile, :, 4 * g:4 * g + 4].rearrange("p r h -> p h r"),
                                                     acc[:, tile, :, DH:VW], spread(rl[:, tile, :], ONE + 1), ALU.mult)
                        last.then_inc(heads_copied.sem, 1)
                for k in range(2 * TAIL):
                    im, j = divmod(k, TAIL)
                    if j in (0, 2, 4):
                        continue
                    dve.wait_ge(tail_made.sem, tail_made.now(it, k + 1))
                    if j < 3:
                        last = dve.tensor_copy(ot[:, 2 * j:2 * j + 2, :], ps[:, k % 4, 0:2 * N].rearrange("p (c n) -> p c n", c=2))
                    elif j < 6:
                        last = dve.tensor_copy(pft[:, 2 * j - 6:2 * j - 4, :], ps[0:UC, k % 4, 0:2 * N].rearrange("p (c n) -> p c n", c=2))
                    else:
                        if im == 0:
                            dve.wait_ge(biased.sem, biased.now(it))
                        last = dve.tensor_tensor(h_sb[:, 2 * im:2 * im + 2, :], ps[0:TM, k % 4, 0:2 * D].rearrange("p (q d) -> p q d", q=2),
                                                 h_sb[:, 2 * im:2 * im + 2, :], ALU.add)
                    last.then_inc(tail_copied_v.sem, 1)
                dve.wait_ge(tail_copied_v.sem, tail_copied_v.now(it))
                norm_step(1)
                dve.wait_ge(gate_made.sem, gate_made.now(it))
                dve.tensor_tensor(lg[:, :, :], ps[0:TM, 6, 0:4 * NE].rearrange("p (q e) -> p q e", q=4),
                                  t["b_gate"][:, :].unsqueeze(1).to_broadcast([TM, 4, NE]), ALU.add).then_inc(gate_ready.sem, 1)
                link.end()

        @block.tensor
        def _(pe):
            for c in (patch_turned, tok_made, x_turned, lin_made, scored, probs_turned, heads_made, tail_made, gate_made):
                pe.sem_inc(c.sem, c.per)
            with pe.Fori(0, PAIRS) as it:
                def turn_x(n):
                    pe.wait_ge(xn_ready.sem, xn_ready.now(it, n + 1))
                    for c in range(2):
                        for q in range(4):
                            im, tile = divmod(q, 2)
                            m = PART[tile]
                            at = im * N + TILE0[tile]
                            last = pe.transpose(ps[0:HD, 4 * n + c, at:at + m], xn[0:m, q, c * HD:(c + 1) * HD], ident[0:m, 0:m])
                        last.then_inc(x_turned.sem, 1)
                    pe.wait_ge(x_copied_a.sem, x_copied_a.now(it, n + 1))
                    pe.wait_ge(x_copied_v.sem, x_copied_v.now(it, n + 1))

                pe.wait_ge(pix_ready.sem, pix_ready.now(it))
                pe.wait_ge(gate_ready.sem, gate_ready.last(it))
                for g, (half, w0, w1) in enumerate(GROUPS):
                    for w in range(w0, w1):
                        last = pe.transpose(ps[:, g, (w - w0) * PST:(w - w0 + 1) * PST], pix[:, w, 128 * half:128 * half + 128], ident[0:PST, 0:PST])
                    last.then_inc(patch_turned.sem, 1)
                pe.wait_ge(patch_copied_a.sem, patch_copied_a.now(it))
                pe.wait_ge(patch_copied_v.sem, patch_copied_v.now(it))
                for im in range(2):
                    for tile in range(2):
                        at = im * 3 * N + 3 * TILE0[tile]
                        for c in range(6):
                            first = at + c // 2
                            last = pe.matmul(ps[0:TM, 6 + im, tile * D:(tile + 1) * D], pt[:, c % 2, first:first + 3 * (TM - 1) + 1:3],
                                             t["w_tok_t"][:, c, :], start=(c == 0), stop=(c == 5))
                    last.then_inc(tok_made.sem, 1)
                turn_x(0)
                for j, (kind, c, n) in enumerate(LIN):
                    bank = (2 + j) % 8
                    if j >= 8:
                        copied = lin_copied_v if j % 2 else lin_copied_a
                        pe.wait_ge(copied.sem, copied.now(it, (j - 8) // 2 + 1))
                    at = (c // 2) * N + TILE0[c % 2]
                    if kind == "aug" and c == 0:
                        pe.wait_ge(aug_loaded.sem, aug_loaded.now(it))
                        pe.wait_ge(aug_fixed.sem, aug_fixed.now(it))
                    if kind == "aug":
                        for q in range(4):
                            im, tile = divmod(q, 2)
                            m, to = PART[tile], im * N + TILE0[tile]
                            last = pe.transpose(ps[:, bank, to:to + m], qrow[0:m, q, 4 * c:4 * c + 4, :].rearrange("p h r -> p (h r)"),
                                                ident[0:m, 0:m])
                    else:
                        for k in range(2):
                            if kind == "qt":
                                last = pe.matmul(ps[0:TM, bank, 0:TW // 2], xt[:, k, at:at + TM], t["cq"][:, k, n * TW // 2:(n + 1) * TW // 2],
                                                 start=(k == 0), stop=(k == 1))
                            elif kind == "v":
                                last = pe.matmul(ps[0:TM, bank, 0:HW // 2], xt[:, k, at:at + TM], t["wv"][:, k, n * HW // 2:(n + 1) * HW // 2],
                                                 start=(k == 0), stop=(k == 1))
                            else:
                                last = pe.matmul(ps[:, bank, 0:NT], t["w" + kind][:, k, c * 128:(c + 1) * 128], xt[:, k, :],
                                                 start=(k == 0), stop=(k == 1))
                    last.then_inc(lin_made.sem, 1)
                pe.wait_ge(lin_copied_a.sem, lin_copied_a.now(it))
                pe.wait_ge(lin_copied_v.sem, lin_copied_v.now(it))
                for s in range(U + 3):
                    if s < U:
                        im, h = divmod(s, H)
                        if s >= 2:
                            pe.wait_ge(probs_ready.sem, probs_ready.now(it, s - 1))
                        for tile in range(2):
                            at = im * N + TILE0[tile]
                            last = pe.matmul(ps[0:TM, s % 2, tile * N:(tile + 1) * N], qa[:, h, at:at + TM], ka[:, h, im * N:(im + 1) * N],
                                             start=True, stop=True)
                        last.then_inc(scored.sem, 1)
                    if 0 <= s - 2 < U:
                        u = s - 2
                        pe.wait_ge(probs_ready.sem, probs_ready.now(it, u + 1))
                        if u >= 2:
                            pe.wait_ge(probs_copied.sem, probs_copied.now(it, u - 1))
                        for mt in range(2):
                            for tile in range(2):
                                m = PART[tile]
                                last = pe.transpose(ps[0:TM, 2 + u % 2, mt * N + TILE0[tile]:mt * N + TILE0[tile] + m],
                                                    probs[0:m, u % 2, tile, TILE0[mt]:TILE0[mt] + TM], ident[0:m, 0:m])
                        last.then_inc(probs_turned.sem, 1)
                    if 0 <= s - 3 < U:
                        u = s - 3
                        im, h = divmod(u, H)
                        grp = u // 4
                        pe.wait_ge(probs_copied.sem, probs_copied.now(it, u + 1))
                        if u % 4 == 0 and grp >= 2:
                            pe.wait_ge(heads_copied.sem, heads_copied.now(it, grp - 1))
                        for tile in range(2):
                            for mt in range(2):
                                last = pe.matmul(ps[0:TM, 4 + 2 * (grp % 2) + tile, (u % 4) * VW:(u % 4 + 1) * VW],
                                                 pts[0:PART[mt], u % 2, mt, TILE0[tile]:TILE0[tile] + TM],
                                                 va[0:PART[mt], 2 * im + mt, h, :], start=(mt == 0), stop=(mt == 1))
                        last.then_inc(heads_made.sem, 1)
                for k in range(2 * TAIL):
                    im, j = divmod(k, TAIL)
                    if k >= 4:
                        copied, n = tail_copy(k - 4)
                        pe.wait_ge(copied.sem, copied.now(it, n))
                    if j == 0:
                        pe.wait_ge(heads_copied.sem, heads_copied.now(it, 3 * im + 3))
                    if j == 3:
                        pe.wait_ge(pf_loaded[im].sem, pf_loaded[im].now(it))
                    if j < 6:
                        src, w = (on, 128) if j < 3 else (pf, UC)
                        for c in range(2):
                            at = (2 * (j % 3) + c) * w
                            for tile in range(2):
                                m = PART[tile]
                                last = pe.transpose(ps[0:w, k % 4, c * N + TILE0[tile]:c * N + TILE0[tile] + m],
                                                    src[0:m, im, tile, at:at + w], ident[0:m, 0:m])
                    else:
                        pe.wait_ge(tail_copied_a.sem, tail_copied_a.now(it, 3 * im + 3))
                        pe.wait_ge(tail_copied_v.sem, tail_copied_v.now(it, 4 * im + 3))
                        for tile in range(2):
                            n0 = TILE0[tile]
                            for c in range(12):
                                lhs, rhs = (ot[:, c, n0:n0 + TM], t["wp2"][:, c, :]) if c < 6 else (pft[:, c - 6, n0:n0 + TM], t["u_sb"][:, c - 6, :])
                                last = pe.matmul(ps[0:TM, k % 4, tile * D:(tile + 1) * D], lhs, rhs, start=(c == 0), stop=(c == 11))
                    last.then_inc(tail_made.sem, 1)
                turn_x(1)
                for q in range(4):
                    at = (q // 2) * N + TILE0[q % 2]
                    for k in range(2):
                        last = pe.matmul(ps[0:TM, 6, q * NE:(q + 1) * NE], xt[:, k, at:at + TM], t["sw"][:, k, :], start=(k == 0), stop=(k == 1))
                last.then_inc(gate_made.sem, 1)


def constants():
    key = np.zeros((N, ONE + 1), np.float32)
    m = np.arange(1, N)
    key[m, (m - 1) // SIDE] = 1
    key[m, ROWS + (m - 1) % SIDE] = 1
    key[0, CLS] = 1
    key_aug = np.zeros((AUG, 2 * N), np.float32)
    key_aug[:ONE + 1] = np.concatenate([key, key]).T
    key[:, ONE] = 1
    val = np.stack([key[n0:n0 + TM] for n0 in TILE0])
    val_aug = np.ascontiguousarray(np.broadcast_to(val[:, :, None, :], (2, TM, H, ONE + 1)))
    rep = lambda v: np.ascontiguousarray(np.broadcast_to(v.astype(np.float32), (98, v.shape[-1])))
    return {
        "const_ident": np.eye(128, dtype=np.float32), "const_key_aug": key_aug, "const_val_aug": val_aug,
        "const_ones": np.ones((98, 98), np.float32),
        "const_before": np.triu(np.ones((98, 98), np.float32), 1),
        "const_rank": rep(NE - np.arange(NE)), "const_base": rep(CAP * np.arange(NE)),
        "const_own": (SLOTS + np.arange(128)[None, :] * 98 + np.arange(98)[:, None]).astype(np.float32),
    }


def dram(nc, kind="Internal"):
    def d(name, shape, dt=F32, kind=kind):
        return nc.dram_tensor(name, shape, dt, kind=kind).ap()

    return {
        "u": d("u", (TW, D), kind="Internal"),
        "qt": d("qt", (2, N * TW), kind="Internal"),
        "pr": d("pr", (2, N * TW), kind="Internal"),
        "h1": d("h1", (TOK, D)),
        "xs": d("xs", (SLOTS + TOK, D)),
        "ys": d("ys", (SLOTS + TOK, D)),
        "lg": d("lg", (TOK, NE)),
        "h3": d("h3", (TOK, D)),
        "slot": d("slot", (TOK, 1), I32),
        "pm": d("pm", (TOK, 1)),
    }


def keep(nc, ctx, t):
    for name, shape in {
        "eps": [128, 1], "w_tok_t": [128, 6, D], "wq": [HD, 2, HW], "wk": [HD, 2, HW],
        "wv": [HD, 2, HW], "wp2": [128, 6, D], "u_sb": [UC, 6, D], "cq": [HD, 2, TW], "sw": [HD, 2, NE],
        "b_tok": [TM, D], "b_proj": [TM, D], "b_gate": [TM, NE], "ka": [DH + AUG, H, 2 * N], "va": [TM, 4, H, VW],
        "qaug": [TM, 4, AUG, H],
    }.items():
        t[name] = ctx.enter_context(nc.sbuf_tensor("k_" + name, shape, F32))


RP = 98
RQ = TOK // RP
BITS = 28


def phase_route(nc, a, t):
    with ExitStack() as ctx:
        def sb(name, shape, dt=F32):
            return ctx.enter_context(nc.sbuf_tensor("r_" + name, shape, dt))

        def sem(name):
            return semaphore(nc, t, "r_" + name)

        lg = sb("lg", [RP, RQ, NE])
        e = sb("e", [RP, NE, RQ])
        eq = sb("eq", [RP, NE, RQ])
        key = sb("key", [RP, NE, RQ])
        hit = sb("hit", [RP, NE, RQ])
        kept = sb("kept", [RP, NE, RQ])
        before = sb("before", [RP, NE, RQ])
        totals = sb("totals", [RP, NE, RQ])
        ones_row = sb("ones_row", [RP, RQ])
        mx = sb("mx", [RP, RQ])
        sm = sb("sm", [RP, RQ])
        pm = sb("pm", [RP, RQ])
        slot = sb("slot", [RP, RQ])
        has = sb("has", [RP, RQ])
        own = sb("own", [RP, RQ])
        slot_t = sb("slot_t", [RQ, RP])
        pm_t = sb("pm_t", [RQ, RP])
        slot_ti = sb("slot_ti", [RQ, RP], I32)
        slot_i = sb("slot_i", [RP, RQ], I32)
        rank_w = sb("rank_w", [RP, NE])
        base_w = sb("base_w", [RP, NE])
        thr = sb("thr", [RP, NE])
        trial = sb("trial", [RP, NE])
        step = sb("step", [RP, 1])
        cnt = sb("cnt", [RP, NE])
        need = sb("need", [RP, NE])
        ok = sb("ok", [RP, NE])
        ones = sb("ones", [RP, RP])
        lower = sb("lower", [RP, RP])
        ident = t["ident"]
        now = sb("now", [RP, 8], I32)
        xin = sb("xin", [RP, 8, D])
        ps = ctx.enter_context(nc.psum_tensor("r_ps", [128, 8, 512], F32))

        loaded = sem("loaded")
        chain = sem("chain")
        bit_chain = sem("bit_chain")
        counted = sem("counted")
        summed = sem("summed")
        maxed = sem("maxed")
        expd = sem("expd")
        masked = sem("masked")
        ranked = sem("ranked")
        placed = sem("placed")
        slots_turned = sem("slots_turned")
        slots_copied = sem("slots_copied")
        stored = sem("stored")
        x_loaded = [sem(f"x_loaded{i}") for i in range(8)]
        x_sent = [sem(f"x_sent{i}") for i in range(8)]
        picked = sem("picked")
        block = ctx.enter_context(nc.Block())

        @block.sync
        def _(sp):
            for dst, src in ((lg[:, :, :], t["lg"].rearrange("(q p) e -> p q e", p=RP)),
                             (ones[:, :], a["const_ones"]), (lower[:, :], a["const_before"]), (rank_w[:, :], a["const_rank"]),
                             (base_w[:, :], a["const_base"]), (own[:, :], a["const_own"])):
                sp.dma_start(dst, src).then_inc(loaded, 16)
            rows = t["ys"][SLOTS:SLOTS + TOK, :].rearrange("(g p) d -> g p d", p=RP)
            for i in range(8):
                sp.dma_start(xin[:, i, :], rows[i]).then_inc(x_loaded[i], 16)
            sp.wait_ge(slots_copied, 1)
            sp.dma_start(t["slot"].rearrange("(q p) o -> q (p o)", p=RP), slot_ti[:, :]).then_inc(stored, 16)
            sp.dma_start(t["pm"].rearrange("(q p) o -> q (p o)", p=RP), pm_t[:, :]).then_inc(stored, 16)
            with sp.Fori(1, RQ // 8) as n:
                for i in range(8):
                    sp.wait_ge(x_sent[i], 16 * n)
                    sp.sem_inc(t["held"], 1)
                    sp.dma_start(xin[:, i, :], t["ys"][bass.ds(n * (8 * RP) + (SLOTS + i * RP), RP), :]).then_inc(x_loaded[i], 16)
            sp.wait_ge(stored, 32)

        @block.gpsimd
        def _(pool):
            pool.wait_ge(placed, 1)
            def send(n):
                pool.tensor_copy(now[:, :], slot_i[:, bass.ds(n * 8, 8)]).then_inc(picked, 1)
                pool.wait_ge(picked, n + 1)
                for i in range(8):
                    pool.wait_ge(x_loaded[i], n * 16 + 16)
                    pool.sem_inc(t["held"], 1)
                    pool.indirect_dma_start(t["xs"], bass.IndirectOffsetOnAxis(ap=now[:, i:i + 1], axis=0), xin[:, i, :], None
                                            ).then_inc(x_sent[i], 16)

            send(0)
            with pool.Fori(1, RQ // 8) as n:
                for i in range(8):
                    pool.wait_ge(x_sent[i], n * 16)
                pool.sem_inc(t["held"], 1)
                send(n)
            for i in range(8):
                pool.wait_ge(x_sent[i], 16 * (RQ // 8))

        @block.scalar
        def _(act):
            act.wait_ge(maxed, 1)
            act.activation(e[:, :, :], eq[:, :, :], ACT.Exp).then_inc(expd, 1)

        @block.vector
        def _(dve):
            done = [0]

            def link(ins):
                done[0] += 1
                ins.then_inc(chain, 1)
                dve.wait_ge(chain, done[0])

            def by_expert(v):
                return v.unsqueeze(1).to_broadcast([RP, NE, RQ])

            def by_token(v):
                return v.unsqueeze(2).to_broadcast([RP, NE, RQ])

            def sum_e(out, src, op=ALU.add):
                link(dve.tensor_reduce(out, src.rearrange("p e q -> p q e"), AX_X, op))

            dve.wait_ge(loaded, 16 * 6)
            link(dve.memset(ones_row[:, :], 1.0))
            link(dve.memset(thr[:, :], 0.0))
            link(dve.memset(step[:, :], 1.0))
            link(dve.tensor_reduce(mx[:, :], lg[:, :, :], AX_X, ALU.max))
            dve.tensor_tensor(eq[:, :, :], lg[:, :, :].rearrange("p q e -> p e q"), by_expert(mx[:, :]), ALU.subtract).then_inc(maxed, 1)
            dve.wait_ge(expd, 1)
            sum_e(sm[:, :], e[:, :, :])
            link(dve.reciprocal(mx[:, :], sm[:, :]))
            link(dve.tensor_tensor(e[:, :, :], e[:, :, :], by_expert(mx[:, :]), ALU.mult))
            sum_e(pm[:, :], e[:, :, :], ALU.max)
            link(dve.tensor_tensor(eq[:, :, :], e[:, :, :], by_expert(pm[:, :]), ALU.is_equal))
            link(dve.tensor_tensor(eq[:, :, :], eq[:, :, :], by_token(rank_w[:, :]), ALU.mult))
            sum_e(sm[:, :], eq[:, :, :], ALU.max)
            link(dve.tensor_tensor(eq[:, :, :], by_expert(sm[:, :]), by_token(rank_w[:, :]), ALU.is_equal))
            link(dve.tensor_scalar(hit[:, :, :], eq[:, :, :], 1.0, None, ALU.subtract))
            link(dve.tensor_tensor(key[:, :, :], eq[:, :, :], by_expert(pm[:, :]), ALU.mult))
            link(dve.tensor_tensor(key[:, :, :], key[:, :, :], hit[:, :, :], ALU.add))

            def reach(op, bound, ordered):
                ordered(dve.tensor_tensor(hit[:, :, :], key[:, :, :], by_token(bound), op))
                dve.tensor_reduce(cnt[:, :], hit[:, :, :], AX_X, ALU.add).then_inc(counted, 1)

            with dve.Fori(0, BITS) as b:
                bit = Chain(dve, bit_chain, b, 5)
                bit(dve.tensor_scalar(trial[:, :], thr[:, :], step[:, 0:1], None, ALU.add))
                reach(ALU.is_ge, trial[:, :], bit)
                dve.wait_ge(summed, b + 1)
                bit(dve.tensor_scalar(ok[:, :], ps[0:RP, 0, 0:NE], float(CAP), step[:, 0:1], ALU.is_ge, ALU.mult))
                bit(dve.tensor_tensor(thr[:, :], thr[:, :], ok[:, :], ALU.add))
                bit(dve.tensor_scalar(step[:, :], step[:, :], 0.5, None, ALU.mult))
                bit.end()
            reach(ALU.is_gt, thr[:, :], link)
            dve.wait_ge(summed, BITS + 1)
            link(dve.tensor_scalar(need[:, :], ps[0:RP, 0, 0:NE], -1.0, float(CAP), ALU.mult, ALU.add))
            link(dve.tensor_copy(kept[:, :, :], hit[:, :, :]))

            def rank(n):
                dve.wait_ge(ranked, n + 1)
                link(dve.tensor_copy(totals[:, :, :], ps[0:RP, 4:6, :].rearrange("p b (e q) -> p (b e) q", q=RQ)))
                for x in range(NE):
                    link(dve.tensor_tensor_scan(before[:, x, :], ones_row[:, :], totals[:, x, :], 0.0, ALU.mult, ALU.add))
                link(dve.tensor_tensor(before[:, :, :], before[:, :, :], totals[:, :, :], ALU.subtract))
                link(dve.tensor_tensor(before[:, :, :], before[:, :, :], ps[0:RP, 2:4, :].rearrange("p b (e q) -> p (b e) q", q=RQ), ALU.add))

            link(dve.tensor_tensor(hit[:, :, :], key[:, :, :], by_token(thr[:, :]), ALU.is_equal))
            dve.sem_inc(masked, 1)
            rank(0)
            link(dve.tensor_tensor(before[:, :, :], before[:, :, :], by_token(need[:, :]), ALU.is_lt))
            link(dve.tensor_tensor(hit[:, :, :], hit[:, :, :], before[:, :, :], ALU.mult))
            link(dve.tensor_tensor(hit[:, :, :], hit[:, :, :], kept[:, :, :], ALU.add))
            dve.sem_inc(masked, 1)
            rank(1)
            link(dve.tensor_tensor(before[:, :, :], before[:, :, :], by_token(base_w[:, :]), ALU.add))
            link(dve.tensor_tensor(before[:, :, :], before[:, :, :], hit[:, :, :], ALU.mult))
            sum_e(slot[:, :], before[:, :, :])
            sum_e(has[:, :], hit[:, :, :])
            link(dve.tensor_scalar(has[:, :], has[:, :], -1.0, 1.0, ALU.mult, ALU.add))
            link(dve.tensor_tensor(has[:, :], has[:, :], own[:, :], ALU.mult))
            link(dve.tensor_tensor(slot[:, :], slot[:, :], has[:, :], ALU.add))
            dve.tensor_copy(slot_i[:, :], slot[:, :]).then_inc(placed, 1)
            dve.wait_ge(slots_turned, 1)
            dve.tensor_copy(slot_ti[:, :], ps[0:RQ, 1, 0:RP])
            dve.tensor_copy(pm_t[:, :], ps[0:RQ, 1, RP:2 * RP]).then_inc(slots_copied, 1)

        @block.tensor
        def _(pe):
            pe.wait_ge(loaded, 16 * 6)
            with pe.Fori(0, BITS + 1) as b:
                pe.wait_ge(counted, b + 1)
                pe.matmul(ps[0:RP, 0, 0:NE], ones[:, :], cnt[:, :], start=True, stop=True).then_inc(summed, 1)
            for n in range(2):
                pe.wait_ge(masked, n + 1)
                for half in range(2):
                    src = hit[:, 4 * half:4 * half + 4, :].rearrange("p e q -> p (e q)")
                    pe.matmul(ps[0:RP, 2 + half, :], lower[:, :], src, start=True, stop=True)
                    last = pe.matmul(ps[0:RP, 4 + half, :], ones[:, :], src, start=True, stop=True)
                last.then_inc(ranked, 1)
            pe.wait_ge(placed, 1)
            pe.transpose(ps[0:RQ, 1, 0:RP], slot[:, :], ident[0:RP, 0:RP])
            pe.transpose(ps[0:RQ, 1, RP:2 * RP], pm[:, :], ident[0:RP, 0:RP]).then_inc(slots_turned, 1)


CT = CAP // 4
CQ = CT // RP


def phase_experts(nc, a, t):
    with ExitStack() as ctx:
        def sb(name, shape, dt=F32):
            return ctx.enter_context(nc.sbuf_tensor("e_" + name, shape, dt))

        def sem(name):
            return semaphore(nc, t, "e_" + name)

        ident = t["ident"]
        w1 = sb("w1", [HD, 2, FF])
        w2 = sb("w2", [128, FC, D])
        b1 = sb("b1", [128, FC])
        b2 = sb("b2", [RP, D])
        xin = sb("xin", [RP, 2, CQ, D])
        xt = sb("xt", [HD, 2, 2, CT])
        ht = sb("ht", [128, FC, CT])
        y = sb("y", [RP, 2, CQ, D])
        ps = ctx.enter_context(nc.psum_tensor("e_ps", [128, 8, 512], F32))

        w1_loaded = Dmas(sem("w1_loaded"), 2)
        w2_loaded = Dmas(sem("w2_loaded"), 2)
        x_loaded = [Dmas(sem(f"x_loaded{i}"), 2) for i in range(2)]
        stored = [Dmas(sem(f"stored{i}"), 2) for i in range(2)]
        x_turned = Count(sem("x_turned"), 8)
        x_copied_a = Count(sem("x_copied_a"), 4)
        x_copied_v = Count(sem("x_copied_v"), 4)
        up_made = Count(sem("up_made"), 4 * FC)
        gelu_done = Count(sem("gelu_done"), 4 * FC)
        down_made = Count(sem("down_made"), 12)
        y_ready = Count(sem("y_ready"), 12)
        block = ctx.enter_context(nc.Block())

        @block.sync
        def _(sp):
            with sp.Fori(0, NE) as e:
                sp.wait_ge(up_made.sem, up_made.last(e))
                sp.sem_inc(t["held"], 1)
                sp.dma_start(w1[:, :, :].unsqueeze(1), a["L0_ffn_w1"].rearrange("e (c p) n -> p e c n", p=HD)[:, bass.ds(e, 1), :, :]).then_inc(w1_loaded.sem, 16)
                sp.wait_ge(gelu_done.sem, gelu_done.last(e))
                sp.sem_inc(t["held"], 1)
                sp.dma_start(b1[:, :].unsqueeze(1), a["L0_ffn_b1"].rearrange("e (c p) -> p e c", p=128)[:, bass.ds(e, 1), :], allow_slow_non_contiguous=True).then_inc(w1_loaded.sem, 16)

                def load(j):
                    if j < 2:
                        sp.wait_ge(x_turned.sem, x_turned.last(e, 2 * (j + 2) + 2))
                    else:
                        sp.wait_ge(x_turned.sem, x_turned.now(e, 2 * (j - 2) + 2))
                    sp.sem_inc(t["held"], 1)
                    sp.dma_start(xin[:, j % 2, :, :], t["xs"][bass.ds(e * CAP + j * CT, CT), :].rearrange("(q p) d -> p q d", p=RP)
                                 ).then_inc(x_loaded[j % 2].sem, 16)

                load(0)
                sp.wait_ge(down_made.sem, down_made.last(e))
                sp.sem_inc(t["held"], 1)
                sp.dma_start(w2[:, :, :].unsqueeze(1), a["L0_ffn_w2"].rearrange("e (c p) n -> p e c n", p=128)[:, bass.ds(e, 1), :, :]).then_inc(w2_loaded.sem, 16)
                sp.wait_ge(y_ready.sem, y_ready.last(e))
                sp.sem_inc(t["held"], 1)
                sp.dma_start(b2[:, :].unsqueeze(1), a["L0_ffn_b2"][bass.ds(e, 1), :].partition_broadcast(RP)).then_inc(w2_loaded.sem, 16)
                load(1)
                for j in range(4):
                    if j + 2 < 4:
                        load(j + 2)
                    sp.wait_ge(y_ready.sem, y_ready.now(e, 3 * j + 3))
                    sp.sem_inc(t["held"], 1)
                    sp.dma_start(t["ys"][bass.ds(e * CAP + j * CT, CT), :].rearrange("(q p) d -> p q d", p=RP), y[:, j % 2, :, :]
                                 ).then_inc(stored[j % 2].sem, 16)
                for i in range(2):
                    sp.wait_ge(stored[i].sem, stored[i].now(e))
                sp.sem_inc(t["held"], 1)

        @block.scalar
        def _(act):
            for c in (x_copied_a, gelu_done):
                act.sem_inc(c.sem, c.per)
            with act.Fori(0, NE) as e:
                def copy_x(j):
                    act.wait_ge(x_turned.sem, x_turned.now(e, 2 * j + 1))
                    act.copy(xt[:, j % 2, 0, :], ps[0:HD, 0, 0:CT]).then_inc(x_copied_a.sem, 1)

                copy_x(0)
                act.wait_ge(w1_loaded.sem, w1_loaded.now(e))
                for j in range(4):
                    for f in range(FC):
                        act.wait_ge(up_made.sem, up_made.now(e, FC * j + f + 1))
                        act.activation(ht[:, f, :], ps[:, 2 + f, 0:CT], ACT.Gelu, bias=b1[:, f:f + 1]).then_inc(gelu_done.sem, 1)
                    if j < 3:
                        copy_x(j + 1)

        @block.vector
        def _(dve):
            for c in (x_copied_v, y_ready):
                dve.sem_inc(c.sem, c.per)
            with dve.Fori(0, NE) as e:
                def copy_x(j):
                    dve.wait_ge(x_turned.sem, x_turned.now(e, 2 * j + 2))
                    dve.tensor_copy(xt[:, j % 2, 1, :], ps[0:HD, 1, 0:CT]).then_inc(x_copied_v.sem, 1)

                copy_x(0)
                dve.wait_ge(w2_loaded.sem, w2_loaded.now(e))
                for j in range(4):
                    if j < 3:
                        copy_x(j + 1)
                    if j >= 2:
                        dve.wait_ge(stored[j % 2].sem, stored[j % 2].now(e, 1))
                    for b in range(3):
                        n = min(2, CQ - 2 * b)
                        dve.wait_ge(down_made.sem, down_made.now(e, 3 * j + b + 1))
                        dve.tensor_tensor(y[:, j % 2, 2 * b:2 * b + n, :], ps[0:RP, 2 + b, 0:n * D].rearrange("p (q d) -> p q d", q=n),
                                          b2[:, :].unsqueeze(1).to_broadcast([RP, n, D]), ALU.add).then_inc(y_ready.sem, 1)

        @block.tensor
        def _(pe):
            for c in (x_turned, up_made, down_made):
                pe.sem_inc(c.sem, c.per)
            with pe.Fori(0, NE) as e:
                def turn_x(j):
                    pe.wait_ge(x_loaded[j % 2].sem, x_loaded[j % 2].now(e, j // 2 + 1))
                    for c in range(2):
                        for q in range(CQ):
                            last = pe.transpose(ps[0:HD, c, q * RP:(q + 1) * RP], xin[:, j % 2, q, c * HD:(c + 1) * HD], ident[0:RP, 0:RP])
                        last.then_inc(x_turned.sem, 1)

                turn_x(0)
                pe.wait_ge(w1_loaded.sem, w1_loaded.now(e))
                for j in range(4):
                    pe.wait_ge(x_copied_a.sem, x_copied_a.now(e, j + 1))
                    pe.wait_ge(x_copied_v.sem, x_copied_v.now(e, j + 1))
                    for f in range(FC):
                        if f < 3:
                            at = 3 * (j - 1) + f + 1
                            pe.wait_ge(y_ready.sem, y_ready.now(e, at) if j else y_ready.last(e, 9 + f + 1))
                        for c in range(2):
                            last = pe.matmul(ps[:, 2 + f, 0:CT], w1[:, c, f * 128:(f + 1) * 128], xt[:, j % 2, c, :], start=(c == 0), stop=(c == 1))
                        last.then_inc(up_made.sem, 1)
                    if j < 3:
                        turn_x(j + 1)
                    if j == 0:
                        pe.wait_ge(w2_loaded.sem, w2_loaded.now(e))
                    pe.wait_ge(gelu_done.sem, gelu_done.now(e, FC * j + FC))
                    for b in range(3):
                        for q in range(2 * b, min(2 * b + 2, CQ)):
                            for f in range(FC):
                                last = pe.matmul(ps[0:RP, 2 + b, (q % 2) * D:(q % 2 + 1) * D], ht[:, f, q * RP:(q + 1) * RP], w2[:, f, :],
                                                 start=(f == 0), stop=(f == FC - 1))
                        last.then_inc(down_made.sem, 1)


TC = 14
NTC = N // TC
ST = 8 * TC
SQ = 8
HB = B // 2
NB = D // 3
SF = TC * HB
TWO_PI = (6.28125, 1.9350051879882812e-03, 3.019916050561e-07)
ROUND = 1.5 * 2.0 ** 23


NCLS = 6
GT0 = [[0, 1, 0, 0, 1, 0], [0, 1, 0, 0, 0, 1], [0, 0, 1, 0, 1, 0], [0, 0, 1, 0, 0, 1], [0, 0, 0, 1, 1, 0], [0, 0, 0, 1, 0, 1]]
EXPERT_PAIRS = [[(j - 1, k - 1) for j in range(1, 6) for k in range(1, 6) if j != k and row[j] and row[k]] for row in GT0]


class Chunk:

    def __init__(self, i, k):
        self.i, self.k = i, k
        self.tc, self.buf, self.use = i * 4 + k, k % 4, i + k // 4
        self.par, self.turn = k % 2, i * 2 + k // 2

    def __add__(self, d):
        return Chunk(self.i, self.k + d)

    def __sub__(self, d):
        return Chunk(self.i, self.k - d)


def phase_states(nc, a, t, out):
    with ExitStack() as ctx:
        def sb(name, shape, dt=F32):
            return ctx.enter_context(nc.sbuf_tensor("s_" + name, shape, dt))

        def sem(name):
            return semaphore(nc, t, "s_" + name)

        ident = t["ident"]
        wrow = sb("wrow", [NB, 6, D])
        dcol = sb("dcol", [HD, 2])
        wt = sb("wt", [HD, 2, 7, NB])
        bias = sb("bias", [128, 7])
        h = sb("h", [ST, 4, SQ, D])
        slot = sb("slot", [ST, 4, SQ], I32)
        pm = sb("pm", [ST, 4, SQ])
        y = sb("y", [ST, 2, SQ, D])
        xn = sb("xn", [ST, SQ, D])
        stats = sb("stats", [ST, SQ, 6])
        mv = sb("mv", [ST, SQ, 2])
        std = sb("std", [ST, SQ])
        rstd = sb("rstd", [ST, SQ])
        xt = sb("xt", [HD, 2, 2, SF])
        eps = sb("eps", [128, 1])
        biv = sb("biv", [128, 3, SF])
        sq = sb("sq", [128, 3, SF])
        k = sb("k", [128, 3, SF])
        sk = sb("sk", [128, 3, SF])
        qk = sb("qk", [128, 3, SF])
        dec = sb("dec", [128, SF])
        th = sb("th", [128, SF])
        ang = sb("ang", [128, SF])
        rnd = sb("rnd", [128, SF])
        sn = sb("sn", [128, SF])
        sh = sb("sh", [128, SF])
        om = sb("om", [128, SF])
        a0 = sb("a0", [128, SF])
        mat = sb("mat", [128, TC, 9, HB])
        u = sb("u", [128, 2, TC, 3, HB])
        prod = sb("prod", [128, 3, 3, HB])
        sum0 = sb("sum0", [128, 3, HB])
        sum1 = sb("sum1", [128, 3, HB])
        state = sb("state", [128, 2, TC, 3, HB])
        state2 = sb("state2", [128, 3, HB, TC])
        w1 = sb("w1", [HD, 2, FF])
        w2 = sb("w2", [128, FC, D])
        b1 = sb("b1", [128, FC])
        b2 = sb("b2", [ST, D])
        mv2 = sb("mv2", [ST, SQ, 2])
        std2 = sb("std2", [ST, SQ])
        rstd2 = sb("rstd2", [ST, SQ])
        zn = sb("zn", [ST, SQ, D])
        zt = sb("zt", [HD, 2, 2, 4 * ST])
        ht = sb("ht", [128, FC, 4 * ST])
        o = sb("o", [ST, SQ, D])
        ps = ctx.enter_context(nc.psum_tensor("s_ps", [128, 8, 512], F32))

        w_loaded = sem("w_loaded")
        W_LOADS = 12 + 4
        w_turned = sem("w_turned")
        w_copied = sem("w_copied")
        w_ready = sem("w_ready")
        h_loaded = [Dmas(sem(f"h_loaded{i}"), SQ) for i in range(4)]
        s_loaded = [Dmas(sem(f"s_loaded{i}"), 2 * SQ) for i in range(4)]
        y_loaded = [Dmas(sem(f"y_loaded{i}"), SQ) for i in range(2)]
        stored = Dmas(sem("stored"), SQ)
        h3_stored = sem("h3_stored")
        weighted = Count(sem("weighted"), 1)
        h2_ready = Count(sem("h2_ready"), 1)
        var_ready = Count(sem("var_ready"), 1)
        std_ready = Count(sem("std_ready"), 1)
        xn_ready = Count(sem("xn_ready"), 1)
        x_turned = Count(sem("x_turned"), 4)
        x_copied_a = Count(sem("x_copied_a"), 2)
        x_copied_v = Count(sem("x_copied_v"), 2)
        made = Count(sem("made"), 7)
        made_copied = Count(sem("made_copied"), 7)
        squared = Count(sem("squared"), 1)
        norm2_ready = Count(sem("norm2_ready"), 1)
        theta_ready = Count(sem("theta_ready"), 1)
        angle_ready = Count(sem("angle_ready"), 1)
        sines_ready = Count(sem("sines_ready"), 1)
        scanned = Count(sem("scanned"), 1)
        state_sorted = Count(sem("state_sorted"), 1)
        state_turned = Count(sem("state_turned"), 4)
        h3_ready = Count(sem("h3_ready"), 1)
        var2_ready = Count(sem("var2_ready"), 1)
        std2_ready = Count(sem("std2_ready"), 1)
        rstd2_ready = Count(sem("rstd2_ready"), 1)
        zn_ready = Count(sem("zn_ready"), 1)
        biased = Count(sem("biased"), 1)
        STEPS = [("turn", half, c) for half in range(2) for c in range(2)]
        STEPS += [("up", 0, f) for f in range(FC)] + [("down", 0, b) for b in range(2)]
        STEPS += [("up", 1, f) for f in range(FC)] + [("down", 1, b) for b in range(2)]
        NS = len(STEPS)
        ffn_made = Count(sem("ffn_made"), NS)
        ffn_copied = Count(sem("ffn_copied"), NS)
        out_ready = Count(sem("out_ready"), 1)
        stores_done = Count(sem("stores_done"), 1)
        front_chain = sem("front_chain")
        elem_chain = sem("elem_chain")
        scan_chain = sem("scan_chain")
        norm_chain = sem("norm_chain")
        FRONT, ELEM = 2, 16

        def tile_rows(array, g, c):
            v = array.rearrange("(g b n) d -> g b n d", g=SQ, n=N)[g]
            return v[:, bass.ds(c.tc * TC, TC), :]

        def chunks(eng, body):
            body(Chunk(0, 0))
            body(Chunk(0, 1))
            with eng.Fori(0, (NTC - 2) // 4) as i:
                for j in range(4):
                    body(Chunk(i, 2 + j))

        def chunks_ahead(eng, body, more):
            body(Chunk(0, 0), NTC - 1)
            body(Chunk(0, 1), NTC - 2)
            with eng.Fori(0, (NTC - 2) // 4 - 1) as i:
                for j in range(4):
                    body(Chunk(i, 2 + j), more)
            for n in range(NTC - 4, NTC):
                body(Chunk(0, n), NTC - 1 - n)

        def behind(c, d):
            return not isinstance(c.tc, int) or c.tc >= d

        LAST = Chunk(0, NTC - 1)
        block = ctx.enter_context(nc.Block())

        @block.sync
        def _(sp):
            wb = a["L1_attn_W_biv"].rearrange("(k c) d -> c k d", c=3)
            wi = a["L1_attn_W_in"].rearrange("(k c) d -> c k d", c=3)
            for c in range(3):
                sp.dma_start(wrow[:, c, :], wb[c]).then_inc(w_loaded, 16)
                sp.dma_start(wrow[:, 3 + c, :], wi[c]).then_inc(w_loaded, 16)
            def places(c):
                for g in range(SQ):
                    for dst, name in ((slot, "slot"), (pm, "pm")):
                        sp.dma_start(dst[:, c.buf, g:g + 1], tile_rows(t[name], g, c)).then_inc(s_loaded[c.buf].sem, 16)

            places(Chunk(0, 0))
            places(Chunk(0, 1))
            sp.dma_start(dcol[:, :], a["L1_attn_W_decay"].rearrange("o (c p) -> p (o c)", p=HD), allow_slow_non_contiguous=True).then_inc(w_loaded, 16)
            for half in range(2):
                p = slice(half * NB, half * NB + NB)
                sp.dma_start(bias[p, 0:3], a["L1_attn_b_biv"].rearrange("(k c) -> k c", c=3)).then_inc(w_loaded, 16)
                sp.dma_start(bias[p, 3:6], a["L1_attn_b_in"].rearrange("(k c) -> k c", c=3)).then_inc(w_loaded, 16)
            sp.dma_start(bias[:, 6:7], a["L1_attn_b_decay"].partition_broadcast(128)).then_inc(w_loaded, 16)
            sp.dma_start(b1[:, :], a["L1_ffn_moe0_b1"].rearrange("(c p) -> p c", p=128), allow_slow_non_contiguous=True).then_inc(w_loaded, 16)
            for dst, src in ((w1[:, :, :], halves(a["L1_ffn_moe0_W1"])),
                             (w2[:, :, :], a["L1_ffn_moe0_W2"].rearrange("(c p) n -> p c n", p=128)),
                             (b2[:, :], a["L1_ffn_moe0_b2"].partition_broadcast(ST))):
                sp.dma_start(dst, src).then_inc(w_loaded, 16)
            sp.sem_inc(stores_done.sem, 1)

            def load(c):
                for g in range(SQ):
                    sp.dma_start(h[:, c.buf, g, :], tile_rows(t["h1"], g, c)).then_inc(h_loaded[c.buf].sem, 16)

            def body(c, more):
                if more >= 4:
                    sp.wait_ge(h2_ready.sem, h2_ready.now(c.tc))
                    sp.sem_inc(t["held"], 1)
                    places(c + 4)
                if not behind(c, 1):
                    sp.wait_ge(h3_ready.sem, h3_ready.now(0))
                    for g in range(SQ):
                        sp.dma_start(tile_rows(t["h3"], g, c), h[:, 0, g, :]).then_inc(h3_stored, 16)
                sp.wait_ge(out_ready.sem, out_ready.now(c.tc))
                sp.sem_inc(t["held"], 1)
                for g in range(SQ):
                    sp.dma_start(tile_rows(out, g, c), o[:, g, :]).then_inc(stored.sem, 16)
                if more >= 4:
                    load(c + 4)
                sp.wait_ge(stored.sem, stored.now(c.tc))
                sp.sem_inc(stores_done.sem, 1)

            for n in range(2):
                load(Chunk(0, n))
            for n in range(2, 4):
                places(Chunk(0, n))
                load(Chunk(0, n))
            chunks_ahead(sp, body, 4)
            sp.wait_ge(h3_stored, 16 * SQ)

        @block.gpsimd
        def _(pool):
            for c in (weighted, h2_ready, zn_ready, biased, out_ready):
                pool.sem_inc(c.sem, c.per)
            pool.wait_ge(w_loaded, 16 * W_LOADS)

            def gather(c):
                pool.wait_ge(s_loaded[c.buf].sem, s_loaded[c.buf].now(c.use))
                pool.sem_inc(t["held"], 1)
                for g in range(SQ):
                    pool.indirect_dma_start(y[:, c.par, g, :], None, t["ys"], bass.IndirectOffsetOnAxis(ap=slot[:, c.buf, g:g + 1], axis=0)
                                            ).then_inc(y_loaded[c.par].sem, 16)

            def residual(c):
                pool.wait_ge(y_loaded[c.par].sem, y_loaded[c.par].now(c.turn))
                pool.sem_inc(t["held"], 1)
                for g in range(SQ):
                    last = pool.tensor_tensor(y[:, c.par, g, :], y[:, c.par, g, :], pm[:, c.buf, g:g + 1].to_broadcast([ST, D]), ALU.mult)
                last.then_inc(weighted.sem, 1)
                pool.wait_ge(weighted.sem, weighted.now(c.tc))
                pool.wait_ge(h_loaded[c.buf].sem, h_loaded[c.buf].now(c.use))
                pool.sem_inc(t["held"], 1)
                for g in range(SQ):
                    last = pool.tensor_tensor(h[:, c.buf, g, :], h[:, c.buf, g, :], y[:, c.par, g, :], ALU.add)
                last.then_inc(h2_ready.sem, 1)
                pool.wait_ge(h2_ready.sem, h2_ready.now(c.tc))
                pool.sem_inc(t["held"], 1)

            def norm2(c):
                pool.wait_ge(rstd2_ready.sem, rstd2_ready.now(c.tc))
                pool.wait_ge(ffn_made.sem, ffn_made.last(c.tc, 4))
                pool.sem_inc(t["held"], 1)
                for g in range(SQ):
                    last = pool.tensor_scalar(zn[:, g, :], h[:, c.buf, g, :], mv2[:, g, 0:1], rstd2[:, g:g + 1], ALU.subtract, ALU.mult)
                last.then_inc(zn_ready.sem, 1)
                if not behind(c, 1):
                    pool.wait_ge(h3_stored, 16 * SQ)
                for g in range(SQ):
                    last = pool.tensor_tensor(h[:, c.buf, g, :], h[:, c.buf, g, :], b2[:, :], ALU.add)
                last.then_inc(biased.sem, 1)

            def finish(c):
                pool.wait_ge(biased.sem, biased.now(c.tc))
                for half in range(2):
                    at = STEPS.index(("down", half, 1)) + 1
                    pool.wait_ge(ffn_copied.sem, ffn_copied.now(c.tc, at))
                    pool.sem_inc(t["held"], 1)
                    last = pool.tensor_tensor(o[:, 4 * half:4 * half + 4, :], o[:, 4 * half:4 * half + 4, :],
                                              h[:, c.buf, 4 * half:4 * half + 4, :], ALU.add)
                last.then_inc(out_ready.sem, 1)

            def body(c, more):
                if more >= 1:
                    residual(c + 1)
                if more >= 2:
                    gather(c + 2)
                if behind(c, 1):
                    norm2(c - 1)
                if behind(c, 2):
                    finish(c - 2)

            gather(Chunk(0, 0))
            gather(Chunk(0, 1))
            residual(Chunk(0, 0))
            chunks_ahead(pool, body, 4)
            norm2(LAST)
            finish(LAST - 1)
            finish(LAST)

        @block.scalar
        def _(act):
            for c in (std_ready, x_copied_a, made_copied, squared, theta_ready, sines_ready, state_sorted, std2_ready, ffn_copied):
                act.sem_inc(c.sem, c.per)
            act.wait_ge(w_ready, 1)

            def sort_states(c):
                act.wait_ge(scanned.sem, scanned.now(c.tc))
                act.copy(state2[:, :, :, :], state[:, c.par, :, :, :].rearrange("p t c b -> p c b t")).then_inc(state_sorted.sem, 1)

            def ffn(c, steps):
                for s in steps:
                    kind, half, n = STEPS[s]
                    act.wait_ge(ffn_made.sem, ffn_made.now(c.tc, s + 1))
                    src = ps[:, 4 + s % 4, 0:4 * ST]
                    if kind == "turn":
                        last = act.copy(zt[:, half, n, :], src[0:HD, :])
                    elif kind == "up":
                        last = act.activation(ht[:, n, :], src, ACT.Gelu, bias=b1[:, n:n + 1])
                    else:
                        if half == 0 and n == 0:
                            act.wait_ge(stores_done.sem, stores_done.last(c.tc))
                            act.sem_inc(t["held"], 1)
                        g = 4 * half + 2 * n
                        last = act.copy(o[:, g:g + 2, :], ps[0:ST, 4 + s % 4, 0:2 * D].rearrange("p (g d) -> p g d", g=2))
                    last.then_inc(ffn_copied.sem, 1)

            def root2(c):
                act.wait_ge(var2_ready.sem, var2_ready.now(c.tc))
                act.activation(std2[:, :], mv2[:, :, 1], ACT.Sqrt, bias=eps[0:ST, :]).then_inc(std2_ready.sem, 1)

            def body(c):
                tc = c.tc
                act.wait_ge(var_ready.sem, var_ready.now(tc))
                act.activation(std[:, :], mv[:, :, 1], ACT.Sqrt, bias=eps[0:ST, :]).then_inc(std_ready.sem, 1)
                for half in range(2):
                    act.wait_ge(x_turned.sem, x_turned.now(tc, half + 1))
                    act.copy(xt[:, 0, half, :].rearrange("p (t b) -> p t b", b=HB),
                             ps[0:HD, half, 0:SF].rearrange("p (b t) -> p t b", t=TC)).then_inc(x_copied_a.sem, 1)
                for n in range(7):
                    act.wait_ge(made.sem, made.now(tc, n + 1))
                    src = ps[:, n % 4, 0:SF]
                    if n < 3:
                        last = act.activation(biv[:, n, :], src, ACT.Identity, bias=bias[:, n:n + 1])
                    elif n < 6:
                        last = act.activation(u[:, c.par, :, n - 3, :], src.rearrange("p (t b) -> p t b", b=HB), ACT.Identity, bias=bias[:, n:n + 1])
                    else:
                        last = act.activation(dec[:, :], src, ACT.Sigmoid, bias=bias[:, 6:7])
                    last.then_inc(made_copied.sem, 1)
                act.wait_ge(made_copied.sem, made_copied.now(tc))
                act.activation(sq[:, :, :], biv[:, :, :], ACT.Square).then_inc(squared.sem, 1)
                if behind(c, 1):
                    sort_states(c - 1)
                act.wait_ge(norm2_ready.sem, norm2_ready.now(tc))
                act.activation(th[:, :], om[:, :], ACT.Sqrt).then_inc(theta_ready.sem, 1)
                act.wait_ge(angle_ready.sem, angle_ready.now(tc))
                act.activation(sn[:, :], ang[:, :], ACT.Sin)
                act.activation(sh[:, :], ang[:, :], ACT.Sin, scale=0.5).then_inc(sines_ready.sem, 1)
                if behind(c, 2):
                    ffn(c - 2, range(ROOT_AT))
                if behind(c, 1):
                    root2(c - 1)
                if behind(c, 2):
                    ffn(c - 2, range(ROOT_AT, NS))

            ROOT_AT = 14
            chunks(act, body)
            sort_states(LAST)
            ffn(LAST - 1, range(ROOT_AT))
            root2(LAST)
            ffn(LAST - 1, range(ROOT_AT, NS))
            ffn(LAST, range(NS))

        @block.vector
        def _(dve):
            for c in (var_ready, xn_ready, x_copied_v, norm2_ready, angle_ready, scanned, h3_ready, var2_ready, rstd2_ready):
                dve.sem_inc(c.sem, c.per)
            dve.memset(eps[:, :], EPS)
            dve.memset(state[:, 1, TC - 1, :, :], 0.0)
            for c in range(6):
                dve.wait_ge(w_turned, c + 1)
                dve.tensor_copy(wt[:, :, c, :], ps[0:HD, c, 0:2 * NB].rearrange("p (k n) -> p k n", k=2)).then_inc(w_copied, 1)
            dve.wait_ge(w_loaded, 16 * W_LOADS)
            dve.tensor_copy(wt[:, :, 6, :], dcol[:, :].unsqueeze(2).to_broadcast([HD, 2, NB])).then_inc(w_ready, 1)

            def three(v):
                return v.unsqueeze(1).to_broadcast([128, 3, SF])

            def front(c):
                tc = c.tc
                link = Chain(dve, front_chain, tc, FRONT)
                dve.wait_ge(h2_ready.sem, h2_ready.now(tc))
                dve.sem_inc(t["held"], 1)
                for g in range(SQ):
                    last = dve.bn_stats(stats[:, g, :], h[:, c.buf, g, :])
                link(last)
                dve.sem_inc(t["held"], 1)
                for g in range(SQ):
                    last = dve.bn_aggr(mv[:, g, :], stats[:, g, :])
                last.then_inc(var_ready.sem, 1)
                dve.wait_ge(std_ready.sem, std_ready.now(tc))
                link(dve.reciprocal(rstd[:, :], std[:, :]))
                for g in range(SQ):
                    last = dve.tensor_scalar(xn[:, g, :], h[:, c.buf, g, :], mv[:, g, 0:1], rstd[:, g:g + 1], ALU.subtract, ALU.mult)
                last.then_inc(xn_ready.sem, 1)
                for half in range(2):
                    dve.wait_ge(x_turned.sem, x_turned.now(tc, 3 + half))
                    dve.tensor_copy(xt[:, 1, half, :].rearrange("p (t b) -> p t b", b=HB),
                                    ps[0:HD, 2 + half, 0:SF].rearrange("p (b t) -> p t b", t=TC)).then_inc(x_copied_v.sem, 1)
                link.end()

            def norm2(c):
                link = Chain(dve, norm_chain, c.tc, 1)
                dve.wait_ge(h3_ready.sem, h3_ready.now(c.tc))
                dve.wait_ge(zn_ready.sem, zn_ready.last(c.tc))
                dve.sem_inc(t["held"], 1)
                for g in range(SQ):
                    last = dve.bn_stats(stats[:, g, :], h[:, c.buf, g, :])
                link(last)
                dve.sem_inc(t["held"], 1)
                for g in range(SQ):
                    last = dve.bn_aggr(mv2[:, g, :], stats[:, g, :])
                last.then_inc(var2_ready.sem, 1)
                dve.wait_ge(std2_ready.sem, std2_ready.now(c.tc))
                dve.reciprocal(rstd2[:, :], std2[:, :]).then_inc(rstd2_ready.sem, 1)
                link.end()

            def scan(c):
                link = Chain(dve, scan_chain, c.tc, 3 * TC)
                for s in range(TC):
                    old = state[:, c.par, s - 1, :, :] if s else state[:, 1 - c.par, TC - 1, :, :]
                    link(dve.tensor_tensor(prod[:, :, :, :].rearrange("p i j b -> p i (j b)"),
                                           mat[:, s, :, :].rearrange("p (i j) b -> p i (j b)", i=3),
                                           old.rearrange("p j b -> p (j b)").unsqueeze(1).to_broadcast([128, 3, 3 * HB]), ALU.mult))
                    dve.tensor_tensor(sum0[:, :, :], prod[:, :, 0, :], prod[:, :, 1, :], ALU.add)
                    link(dve.tensor_tensor(sum1[:, :, :], prod[:, :, 2, :], u[:, c.par, s, :, :], ALU.add))
                    link(dve.tensor_tensor(state[:, c.par, s, :, :], sum0[:, :, :], sum1[:, :, :], ALU.add))
                link.end()
                dve.sem_inc(scanned.sem, 1)

            def elem(tc):
                link = Chain(dve, elem_chain, tc, ELEM)
                dve.wait_ge(squared.sem, squared.now(tc))
                link(dve.tensor_tensor(om[:, :], sq[:, 0, :], sq[:, 1, :], ALU.add))
                dve.scalar_tensor_tensor(om[:, :], sq[:, 2, :], 1e-32, om[:, :], ALU.max, ALU.add).then_inc(norm2_ready.sem, 1)
                dve.wait_ge(theta_ready.sem, theta_ready.now(tc))
                link(dve.tensor_scalar(rnd[:, :], th[:, :], 1.0 / (2.0 * np.pi), ROUND, ALU.mult, ALU.add))
                link(dve.tensor_scalar(rnd[:, :], rnd[:, :], ROUND, None, ALU.subtract))
                src = th
                for part in TWO_PI:
                    link(dve.scalar_tensor_tensor(ang[:, :], rnd[:, :], -part, src[:, :], ALU.mult, ALU.add))
                    src = ang
                dve.tensor_scalar(ang[:, :], ang[:, :], 3.1415925, -3.1415925, ALU.min, ALU.max).then_inc(angle_ready.sem, 1)
                link(dve.tensor_scalar(th[:, :], th[:, :], 1e-8, None, ALU.max))
                link(dve.reciprocal(rnd[:, :], th[:, :]))
                dve.tensor_tensor(k[:, :, :], biv[:, :, :], three(rnd[:, :]), ALU.mult)
                dve.wait_ge(sines_ready.sem, sines_ready.now(tc))
                link(dve.scalar_tensor_tensor(om[:, :], sh[:, :], 2.0, sh[:, :], ALU.mult, ALU.mult))
                link(dve.tensor_tensor(om[:, :], om[:, :], dec[:, :], ALU.mult))
                dve.tensor_tensor(a0[:, :], dec[:, :], om[:, :], ALU.subtract)
                link(dve.tensor_tensor(sn[:, :], sn[:, :], dec[:, :], ALU.mult))
                dve.tensor_tensor(sk[:, :, :], k[:, :, :], three(sn[:, :]), ALU.mult)
                link(dve.tensor_tensor(qk[:, :, :], k[:, :, :], three(om[:, :]), ALU.mult))

                def rows(v, n):
                    return v.rearrange("p c (t b) -> p c t b", b=HB) if n > 1 else v.rearrange("p (t b) -> p t b", b=HB)

                link(dve.tensor_tensor(sq[:, :, :], qk[:, :, :], k[:, :, :], ALU.mult))
                link(dve.tensor_tensor(mat[:, :, 0:9:4, :].rearrange("p t c b -> p c t b"), rows(sq[:, :, :], 3), rows(three(a0[:, :]), 3), ALU.add))
                dve.tensor_tensor(sq[:, 0, :], qk[:, 0, :], k[:, 1, :], ALU.mult)
                dve.tensor_tensor(sq[:, 1, :], qk[:, 0, :], k[:, 2, :], ALU.mult)
                link(dve.tensor_tensor(sq[:, 2, :], qk[:, 1, :], k[:, 2, :], ALU.mult))
                for cell, p, c, op in ((1, 0, 2, ALU.subtract), (3, 0, 2, ALU.add), (2, 1, 1, ALU.add), (6, 1, 1, ALU.subtract),
                                       (5, 2, 0, ALU.subtract), (7, 2, 0, ALU.add)):
                    last = dve.tensor_tensor(mat[:, :, cell, :], rows(sq[:, p, :], 1), rows(sk[:, c, :], 1), op)
                link(last)
                link.end()

            def add(c):
                for g in range(4):
                    dve.wait_ge(state_turned.sem, state_turned.now(c.tc, g + 1))
                    for half in range(2):
                        v = h[:, c.buf, 4 * half + g, :].rearrange("p (k c) -> p k c", c=3)
                        last = dve.tensor_tensor(v, ps[0:ST, g, 0:3 * 128].rearrange("p (c h k) -> p h k c", c=3, h=2)[:, half, :, :], v, ALU.add)
                last.then_inc(h3_ready.sem, 1)

            def body(c):
                front(c)
                if behind(c, 1):
                    scan(c - 1)
                elem(c.tc)
                if behind(c, 1):
                    add(c - 1)
                    norm2(c - 1)

            chunks(dve, body)
            scan(LAST)
            add(LAST)
            norm2(LAST)

        @block.tensor
        def _(pe):
            for c in (x_turned, made, state_turned, ffn_made):
                pe.sem_inc(c.sem, c.per)
            pe.wait_ge(w_loaded, 16 * W_LOADS)
            for c in range(6):
                for n in range(2):
                    last = pe.transpose(ps[0:HD, c, n * NB:(n + 1) * NB], wrow[:, c, n * HD:(n + 1) * HD], ident[0:NB, 0:NB])
                last.then_inc(w_turned, 1)
            pe.wait_ge(w_copied, 6)
            pe.wait_ge(w_ready, 1)

            def turn_states(c):
                pe.wait_ge(state_sorted.sem, state_sorted.now(c.tc))
                for g in range(4):
                    for n in range(3):
                        last = pe.transpose(ps[0:ST, g, n * 128:(n + 1) * 128],
                                            state2[:, n, 8 * g:8 * g + 8, :].rearrange("p b t -> p (b t)"), ident[:, :])
                    last.then_inc(state_turned.sem, 1)

            def ffn(c):
                for s, (kind, half, n) in enumerate(STEPS):
                    need = s - 3
                    if kind == "up":
                        need = max(need, 2 * half + 2)
                    elif kind == "down":
                        need = max(need, STEPS.index(("up", half, FC - 1)) + 1)
                    if s == 0:
                        pe.wait_ge(zn_ready.sem, zn_ready.now(c.tc))
                        pe.wait_ge(ffn_copied.sem, ffn_copied.last(c.tc))
                    elif need > 0:
                        pe.wait_ge(ffn_copied.sem, ffn_copied.now(c.tc, need))
                    bank = 4 + s % 4
                    if kind == "turn":
                        for g in range(4):
                            last = pe.transpose(ps[0:HD, bank, g * ST:(g + 1) * ST], zn[:, 4 * half + g, n * HD:(n + 1) * HD], ident[0:ST, 0:ST])
                    elif kind == "up":
                        for q in range(2):
                            last = pe.matmul(ps[:, bank, 0:4 * ST], w1[:, q, n * 128:(n + 1) * 128], zt[:, half, q, :], start=(q == 0), stop=(q == 1))
                    else:
                        for g in range(2):
                            at = (2 * n + g) * ST
                            for f in range(FC):
                                last = pe.matmul(ps[0:ST, bank, g * D:(g + 1) * D], ht[:, f, at:at + ST], w2[:, f, :], start=(f == 0), stop=(f == FC - 1))
                    last.then_inc(ffn_made.sem, 1)

            def body(c):
                tc = c.tc
                pe.wait_ge(xn_ready.sem, xn_ready.now(tc))
                pe.wait_ge(h3_ready.sem, h3_ready.last(tc - 1) if behind(c, 1) else h3_ready.per)
                pe.sem_inc(t["held"], 1)
                for n in range(2):
                    for half in range(2):
                        for g in range(4):
                            last = pe.transpose(ps[0:HD, 2 * n + half, g * ST:(g + 1) * ST], xn[:, 4 * half + g, n * HD:(n + 1) * HD], ident[0:ST, 0:ST])
                        last.then_inc(x_turned.sem, 1)
                pe.wait_ge(x_copied_a.sem, x_copied_a.now(tc))
                pe.wait_ge(x_copied_v.sem, x_copied_v.now(tc))
                for comp in range(7):
                    if comp >= 4:
                        pe.wait_ge(made_copied.sem, made_copied.now(tc, comp - 3))
                    for half in range(2):
                        for n in range(2):
                            last = pe.matmul(ps[half * NB:(half + 1) * NB, comp % 4, 0:SF], wt[:, n, comp, :], xt[:, n, half, :],
                                             start=(n == 0), stop=(n == 1))
                    last.then_inc(made.sem, 1)
                if behind(c, 1):
                    pe.wait_ge(made_copied.sem, made_copied.now(tc))
                    turn_states(c - 1)
                if behind(c, 2):
                    ffn(c - 2)

            chunks(pe, body)
            turn_states(LAST)
            ffn(LAST - 1)
            ffn(LAST)


def phase_first(nc, a, t, out):
    with ExitStack() as ctx:
        def sb(name, shape, dt=F32):
            return ctx.enter_context(nc.sbuf_tensor("f_" + name, shape, dt))

        def sem(name):
            return semaphore(nc, t, "f_" + name)

        NA = 5
        users = [[(i, s) for i in range(NCLS) for s in range(2) if EXPERT_PAIRS[i][s][0] == x] for x in range(NA)]
        place, n = {}, 0
        for x in range(NA):
            for key in users[x]:
                place[key] = n
                n += 1
        ident = t["ident"]
        w1 = sb("w1", [HD, NA, 2, FF])
        w2 = sb("w2", [128, NA, FC, D])
        b1 = sb("b1", [128, NA, FC])
        b2 = sb("b2", [B, NA, D])
        gw = sb("gw", [HD, NCLS, 2, 2])
        eps = sb("eps", [128, 1])
        h = sb("h", [B, NCLS, D])
        xn = sb("xn", [B, NCLS, D])
        stats = sb("stats", [B, NCLS, 6])
        mv = sb("mv", [B, NCLS, 2])
        std = sb("std", [B, NCLS])
        rstd = sb("rstd", [B, NCLS])
        xt = sb("xt", [HD, 2, NCLS * B])
        ht = sb("ht", [128, FC, 2 * NCLS * B])
        lg = sb("lg", [B, NCLS, 2])
        g = sb("g", [B, NCLS, 2])
        mask = sb("mask", [B, NCLS, 2])
        one = sb("one", [B, NCLS])
        e0 = sb("e0", [B, NCLS, 2, D])
        ps = ctx.enter_context(nc.psum_tensor("f_ps", [128, 8, 512], F32))

        loaded = sem("loaded")
        late = sem("late")
        chain = sem("chain")
        eps_set = sem("eps_set")
        var_ready = sem("var_ready")
        std_ready = sem("std_ready")
        xn_ready = sem("xn_ready")
        x_turned = sem("x_turned")
        x_copied = sem("x_copied")
        gate_made = sem("gate_made")
        gate_in = sem("gate_in")
        gate_exp = sem("gate_exp")
        up_made = sem("up_made")
        gelu_done = sem("gelu_done")
        down_made = sem("down_made")
        down_copied = sem("down_copied")
        y_ready = sem("y_ready")
        stored = sem("stored")
        block = ctx.enter_context(nc.Block())
        rows = t["h3"].rearrange("(b n) d -> b n d", n=N)[:, 0:NCLS, :]

        @block.sync
        def _(sp):
            for dst, src in ((h[:, :, :], rows),
                             (gw[:, :, 0, :], a["L1_ffn_G_W"].rearrange("i (c p) o -> c p i o", p=HD)[0]),
                             (gw[:, :, 1, :], a["L1_ffn_G_W"].rearrange("i (c p) o -> c p i o", p=HD)[1])):
                sp.dma_start(dst, src).then_inc(loaded, 16)
            for x in range(NA):
                sp.dma_start(w1[:, x, :, :], halves(a["L1_ffn_A1_W"][x])).then_inc(late, 16)
                sp.dma_start(b1[:, x, :], a["L1_ffn_A1_b"][x].rearrange("(c p) -> p c", p=128), allow_slow_non_contiguous=True).then_inc(late, 16)
                sp.dma_start(w2[:, x, :, :], a["L1_ffn_A2_W"][x].rearrange("(c p) n -> p c n", p=128)).then_inc(late, 16)
                sp.dma_start(b2[:, x, :], a["L1_ffn_A2_b"][x].partition_broadcast(B)).then_inc(late, 16)
            sp.wait_ge(y_ready, 1)
            sp.dma_start(out.rearrange("(b n) d -> b n d", n=N)[:, 0:NCLS, :], h[:, :, :]).then_inc(stored, 16)
            sp.wait_ge(stored, 16)

        @block.gpsimd
        def _(pool):
            pool.memset(eps[:, :], EPS).then_inc(eps_set, 1)

        @block.scalar
        def _(act):
            act.wait_ge(eps_set, 1)
            act.wait_ge(var_ready, 1)
            act.activation(std[:, :], mv[:, :, 1], ACT.Sqrt, bias=eps[0:B, :]).then_inc(std_ready, 1)
            act.wait_ge(gate_in, 1)
            act.activation(g[:, :, :], lg[:, :, :], ACT.Exp).then_inc(gate_exp, 1)
            act.wait_ge(late, 16 * 4 * NA)
            n = 0
            for x in range(NA):
                lo = place[users[x][0]] * B
                for f in range(FC):
                    act.wait_ge(up_made, n + 1)
                    w = len(users[x]) * B
                    act.activation(ht[:, f, lo:lo + w], ps[:, 3 + n % 2, 0:w], ACT.Gelu, bias=b1[:, x, f:f + 1]).then_inc(gelu_done, 1)
                    n += 1

        @block.vector
        def _(dve):
            done = [0]

            def link(ins):
                done[0] += 1
                ins.then_inc(chain, 1)
                dve.wait_ge(chain, done[0])

            dve.wait_ge(loaded, 16 * 3)
            for i in range(NCLS):
                last = dve.bn_stats(stats[:, i, :], h[:, i, :])
            link(last)
            for i in range(NCLS):
                last = dve.bn_aggr(mv[:, i, :], stats[:, i, :])
            last.then_inc(var_ready, 1)
            dve.wait_ge(std_ready, 1)
            link(dve.reciprocal(rstd[:, :], std[:, :]))
            for i in range(NCLS):
                last = dve.tensor_scalar(xn[:, i, :], h[:, i, :], mv[:, i, 0:1], rstd[:, i:i + 1], ALU.subtract, ALU.mult)
            last.then_inc(xn_ready, 1)
            for c in range(2):
                dve.wait_ge(x_turned, c + 1)
                dve.tensor_copy(xt[:, c, :], ps[0:HD, c, 0:NCLS * B]).then_inc(x_copied, 1)
            dve.wait_ge(gate_made, 1)
            link(dve.tensor_copy(lg[:, :, :], ps[0:B, 2, 0:2 * NCLS].rearrange("p (i o) -> p i o", o=2)))
            link(dve.tensor_reduce(one[:, :], lg[:, :, :], AX_X, ALU.max))
            dve.tensor_tensor(lg[:, :, :], lg[:, :, :], spread(one[:, :], 2), ALU.subtract).then_inc(gate_in, 1)
            dve.wait_ge(gate_exp, 1)
            link(dve.tensor_reduce(one[:, :], g[:, :, :], AX_X, ALU.add))
            link(dve.reciprocal(one[:, :], one[:, :]))
            link(dve.tensor_tensor(g[:, :, :], g[:, :, :], spread(one[:, :], 2), ALU.mult))
            link(dve.tensor_reduce(one[:, :], g[:, :, :], AX_X, ALU.min))
            link(dve.tensor_tensor(mask[:, :, :], g[:, :, :], spread(one[:, :], 2), ALU.is_gt))
            link(dve.tensor_tensor(g[:, :, :], g[:, :, :], mask[:, :, :], ALU.mult))
            link(dve.tensor_reduce(one[:, :], g[:, :, :], AX_X, ALU.add))
            link(dve.tensor_scalar(one[:, :], one[:, :], 1e-6, None, ALU.max))
            link(dve.reciprocal(one[:, :], one[:, :]))
            link(dve.tensor_tensor(g[:, :, :], g[:, :, :], spread(one[:, :], 2), ALU.mult))
            for i in range(NCLS):
                dve.wait_ge(down_made, i + 1)
                for s in range(2):
                    last = dve.tensor_tensor(e0[:, i, s, :], ps[0:B, 5 + i % 3, s * D:(s + 1) * D], b2[:, EXPERT_PAIRS[i][s][1], :], ALU.add)
                last.then_inc(down_copied, 1)
                dve.wait_ge(down_copied, i + 1)
                for s in range(2):
                    link(dve.scalar_tensor_tensor(h[:, i, :], e0[:, i, s, :], g[:, i, s:s + 1], h[:, i, :], ALU.mult, ALU.add))
            dve.sem_inc(y_ready, 1)

        @block.tensor
        def _(pe):
            pe.wait_ge(xn_ready, 1)
            for c in range(2):
                for i in range(NCLS):
                    last = pe.transpose(ps[0:HD, c, i * B:(i + 1) * B], xn[:, i, c * HD:(c + 1) * HD], ident[0:B, 0:B])
                last.then_inc(x_turned, 1)
            pe.wait_ge(x_copied, 2)
            for i in range(NCLS):
                for c in range(2):
                    last = pe.matmul(ps[0:B, 2, 2 * i:2 * i + 2], xt[:, c, i * B:(i + 1) * B], gw[:, i, c, :], start=(c == 0), stop=(c == 1))
            last.then_inc(gate_made, 1)
            pe.wait_ge(late, 16 * 4 * NA)
            n = 0
            for x in range(NA):
                tokens = [i for i, _ in users[x]]
                step = tokens[1] - tokens[0]
                assert tokens == list(range(tokens[0], tokens[-1] + 1, step))
                for f in range(FC):
                    if n >= 2:
                        pe.wait_ge(gelu_done, n - 1)
                    for c in range(2):
                        cols = xt[:, c, :].rearrange("p (i b) -> p i b", b=B)[:, tokens[0]:tokens[-1] + 1:step, :]
                        last = pe.matmul(ps[:, 3 + n % 2, 0:len(tokens) * B].rearrange("p (i b) -> p i b", b=B), w1[:, x, c, f * 128:(f + 1) * 128], cols,
                                         start=(c == 0), stop=(c == 1))
                    last.then_inc(up_made, 1)
                    n += 1
            pe.wait_ge(gelu_done, NA * FC)
            for i in range(NCLS):
                if i >= 3:
                    pe.wait_ge(down_copied, i - 2)
                for s in range(2):
                    at = place[(i, s)] * B
                    for f in range(FC):
                        last = pe.matmul(ps[0:B, 5 + i % 3, s * D:(s + 1) * D], ht[:, f, at:at + B], w2[:, EXPERT_PAIRS[i][s][1], f, :],
                                         start=(f == 0), stop=(f == FC - 1))
                last.then_inc(down_made, 1)


def vit_tower(nc, a, out):
    t = dram(nc)
    t["held"] = nc.alloc_semaphore("held")
    t["in_use"] = []
    out = out.rearrange("b n d -> (b n) d")
    with nc.sbuf_tensor("ident", [128, 128], F32) as ident:
        t["ident"] = ident
        with ExitStack() as ctx:
            keep(nc, ctx, t)
            phase_setup(nc, a, t)
            clear(nc, t)
            phase_tokens(nc, a, t)
        clear(nc, t)
        phase_route(nc, a, t)
        clear(nc, t)
        phase_experts(nc, a, t)
        clear(nc, t)
        phase_states(nc, a, t, out)
        clear(nc, t)
        phase_first(nc, a, t, out)


def kernel(**inputs):
    import concourse.bacc as bacc
    from concourse.bass_utils import run_bass_kernel_spmd

    nc = bacc.Bacc("TRN2", target_bir_lowering=False, num_devices=1)
    arrays = {k: np.ascontiguousarray(v) for k, v in inputs.items() if k != "L1_ffn_mids"}
    arrays.update(constants())
    a = {k: nc.dram_tensor("in_" + k, v.shape, mybir.dt.from_np(v.dtype), kind="ExternalInput").ap() for k, v in arrays.items()}
    out = nc.dram_tensor("out", (B, N, D), F32, kind="ExternalOutput").ap()
    vit_tower(nc, a, out)
    r = run_bass_kernel_spmd(nc, [{"in_" + k: v for k, v in arrays.items()}], core_ids=[0])
    return r.results[0]["out"]
```

```python
from contextlib import ExitStack

import numpy as np

import concourse.bass as bass
from concourse import mybir

F32 = mybir.dt.float32
F32R = mybir.dt.float32r
I32 = mybir.dt.int32
U32 = mybir.dt.uint32
ALU = mybir.AluOpType
ACT = mybir.ActivationFunctionType
AX_X = mybir.AxisListType.X

B = 64
C_IN, IMG, PATCH = 3, 224, 16
GRID = IMG // PATCH
N = GRID * GRID
D = 192
HD = D // 2
TOK = B * N
H, DH = 12, 64
HW = H * DH
SIDE = 13
ROWS = 15
LREL = 14
CAP = int(1.25 * TOK / 8)
NE = 8
FF = 768
FC = FF // 128
SLOTS = NE * CAP
EPS = 1e-5
QK_SCALE = DH ** -0.5

NV = 2 * LREL + 2
NHR = 2 * SIDE - 1
TR = NV + NHR
TW = TR * H
VRUN, HRUN = ROWS * H, SIDE * H
AUG = 32
CLS = ROWS + SIDE
ONE = CLS + 1
VW = DH + ONE + 1
UC = TW // 6

PAIRS = B // 2
TM = 104
T0 = N - TM
SPI = C_IN * GRID
PST = 2 * SPI
TILE0 = [0, T0]
PART = [T0, TM]


class Count:

    def __init__(self, sem, per):
        self.sem, self.per = sem, per

    def now(self, it, k=None):
        return it * self.per + self.per + (self.per if k is None else k)

    def last(self, it, k=None):
        return it * self.per + (self.per if k is None else k)


class Dmas:

    def __init__(self, sem, per):
        self.sem, self.per = sem, per

    def now(self, it, k=None):
        return (it * self.per + (self.per if k is None else k)) * 16


def semaphore(nc, t, name):
    t["in_use"].append(nc.alloc_semaphore(name))
    return t["in_use"][-1]


def clear(nc, t):
    nc.clear_and_free_semaphores(t["in_use"])
    t["in_use"] = []
    nc.all_engine_barrier()


def halves(w):
    return w.rearrange("(c p) n -> p c n", p=HD)


def whole(ap):
    return ap.bitcast(F32)


def parts(ap):
    return ap.bitcast(F32R)


WIDTH_PASSES = [(0, 128, 0), (0, 128, 1), (1, 128, 0), (1, 64, 1), (2, 128, 0)]


def load_blocks(eng, dst, w, done):
    for rows, block, to in ((0, 0, slice(0, 128)), (128, 1, slice(0, 64)), (0, 1, slice(64, 128)), (64, 2, slice(0, 128))):
        eng.dma_start(dst[to, block, :], w[rows:rows + to.stop - to.start, :]).then_inc(done, 16)


def width_product(pe, out, weights, cols, x, by_token):
    n = len(WIDTH_PASSES)
    for k, (block, rows, part) in enumerate(WIDTH_PASSES):
        w, v = weights[part][0:rows, block, cols], x(block, rows)
        last = pe.matmul(out, v if by_token else w, w if by_token else v, start=(k == 0), stop=(k == n - 1))
    return last


def hidden_product(pe, out, x, tokens, w, chunks):
    n = 0
    for c in range(chunks):
        for p, q in ((0, 0), (0, 1), (1, 0)):
            last = pe.matmul(out, x[p][:, c, tokens], w[q][:, c, :], start=(n == 0), stop=(n == 3 * chunks - 1))
            n += 1
    return last


def phase_setup(nc, a, t):
    with ExitStack() as ctx:
        def sb(name, shape, dt=F32):
            return ctx.enter_context(nc.sbuf_tensor(name, shape, dt))

        def sem(name):
            return semaphore(nc, t, name)

        w_tok = sb("su_w_tok", [HD, 2, 4 * D])
        wp_h = sb("su_wp_h", [DH, H, D])
        tab = sb("su_tab", [TR, 2, DH])
        tab0 = sb("su_tab0", [1, 2, DH])
        tab_t = sb("su_tab_t", [DH, 2, TR])
        wq = sb("su_wq", [HD, 2, HW])
        wq_t = sb("su_wq_t", [DH, 2, 2 * D])
        raw = {"wq": sb("su_raw_q", [128, 3, HW]), "wk": sb("su_raw_k", [128, 3, HW]), "wv": sb("su_raw_v", [128, 3, HW]),
               "cq": sb("su_raw_cq", [128, 3, TW])}
        u_h = sb("su_u_h", [TR, 2, D])
        raw_sw = sb("su_raw_sw", [128, 3, NE])
        zero = sb("su_zero", [120, 1536])
        ps = ctx.enter_context(nc.psum_tensor("su_ps", [128, 8, 512], F32))

        loaded = sem("su_loaded")
        added = sem("su_added")
        tables_turned = sem("su_tables_turned")
        tables_copied = sem("su_tables_copied")
        tok_turned = sem("su_tok_turned")
        tok_copied = sem("su_tok_copied")
        wq_turned = sem("su_wq_turned")
        wq_copied = sem("su_wq_copied")
        cq_made = sem("su_cq_made")
        cq_copied = sem("su_cq_copied")
        u_made = sem("su_u_made")
        u_copied = sem("su_u_copied")
        u_stored = [sem(f"su_u_stored{i}") for i in range(2)]
        u_loaded = sem("su_u_loaded")
        cleared = sem("su_cleared")
        zeroed = sem("su_zeroed")
        aug_cleared = sem("su_aug_cleared")
        masked = sem("su_masked")

        u_dram = t["u"].rearrange("(r h) e -> r h e", h=H)

        block = ctx.enter_context(nc.Block())

        @block.sync
        def _(sp):
            loads = [(t["ident"][:, :], a["const_ident"]), (w_tok[:, :, :], halves(a["L0_tok_W"])),
                     (wq[:, :, :], halves(a["L0_attn_Wq"])),
                     (t["wp2"][:, :, :], a["L0_attn_Wp"].rearrange("(c p) n -> p c n", p=128)),
                     (wp_h[:, :, :], a["L0_attn_Wp"].rearrange("(h p) n -> p h n", p=DH)),
                     (t["b_tok"][:, :], a["L0_tok_b"].partition_broadcast(TM)),
                     (t["b_proj"][:, :], a["L0_attn_bp"].partition_broadcast(TM)),
                     (t["b_gate"][:, :], a["L0_ffn_switch_b"].partition_broadcast(TM))]
            for k, (v, h) in enumerate((("tvk", "thk"), ("tvv", "thv"))):
                loads += [(tab[0:NV, k, :], a["L0_attn_" + v]),
                          (tab[NV:TR, k, :], a["L0_attn_" + h][LREL + 2 - SIDE:LREL + 1 + SIDE, :]),
                          (tab0[0:1, k, :], a["L0_attn_" + h][0:1, :])]
            for h in range(H):
                loads.append((t["ka"][DH:DH + AUG, h, :], a["const_key_aug"][:, 0:N]))
            for q in range(4):
                loads.append((t["va"][:, q, :, DH:VW], a["const_val_aug"][q % 2]))
            for dst, src in loads:
                sp.dma_start(dst, src).then_inc(loaded, 16)
            for name in ("wq", "wk", "wv"):
                load_blocks(sp, raw[name], a["L0_attn_W" + name[1]], loaded)
            load_blocks(sp, raw_sw, a["L0_ffn_switch_w"], loaded)
            sp.wait_ge(cleared, 1)
            rows = 960
            xs = t["xs"]
            n_big = SLOTS // rows
            for r in range(n_big):
                sp.dma_start(xs[r * rows:(r + 1) * rows, :].rearrange("(p r) d -> p (r d)", p=120),
                             zero[:, :]).then_inc(zeroed, 16)
            left = SLOTS - n_big * rows
            sp.dma_start(xs[n_big * rows:SLOTS, :].rearrange("(p r) d -> p (r d)", p=40),
                         zero[0:40, 0:left // 40 * D]).then_inc(zeroed, 16)
            for i in range(2):
                for j in range(2):
                    sp.dma_start(t["pr"][i, j * 98 * TW:(j + 1) * 98 * TW].rearrange("(p f) -> p f", p=98),
                                 zero[0:98, 0:TW]).then_inc(zeroed, 16)
            for h in range(H):
                sp.wait_ge(u_copied, h + 1)
                sp.dma_start(u_dram[:, h, :], u_h[:, h % 2, :]).then_inc(u_stored[h % 2], 16)
            for i in range(2):
                sp.wait_ge(u_stored[i], 16 * H // 2)
            sp.dma_start(t["u_sb"][:, :, :], t["u"].rearrange("(c p) e -> p c e", p=UC)).then_inc(u_loaded, 16)
            sp.wait_ge(u_loaded, 16)
            sp.wait_ge(zeroed, 16 * (n_big + 5))

        @block.gpsimd
        def _(pool):
            pool.memset(zero[:, :], 0.0).then_inc(cleared, 1)
            pool.memset(t["eps"][:, :], EPS)
            pool.memset(t["qaug"][:, :, :, :], 0.0).then_inc(aug_cleared, 1)
            pool.wait_ge(aug_cleared, 1)

        n_loads = 8 + 6 + H + 4 + 4 * 4

        @block.vector
        def _(dve):
            dve.wait_ge(loaded, 16 * n_loads)
            dve.memset(t["ka"][DH + AUG:128, :, :], 0.0)
            dve.tensor_copy(t["ident_r"][:, :], t["ident"][:, :])
            dve.tensor_copy(t["sw_hi"][:, :, :], raw_sw[:, :, :]).then_inc(masked, 1)
            dve.wait_ge(masked, 1)
            dve.tensor_tensor(t["sw_lo"][:, :, :], raw_sw[:, 0:2, :], whole(t["sw_hi"][:, 0:2, :]), ALU.subtract)
            dve.tensor_tensor(tab[0:1, :, :], tab[0:1, :, :], tab0[:, :, :], ALU.add).then_inc(added, 1)
            dve.wait_ge(tables_turned, 1)
            dve.tensor_copy(tab_t[:, :, :], ps[0:DH, 0, 0:2 * TR].rearrange("p (k r) -> p k r", k=2)).then_inc(tables_copied, 1)
            for c in range(6):
                dve.wait_ge(tok_turned, c + 1)
                dve.tensor_copy(t["w_tok_t"][:, c, :], ps[:, 1 + c % 3, 0:D]).then_inc(tok_copied, 1)
            for h in range(H):
                dve.wait_ge(wq_turned, h + 1)
                if h >= 2:
                    dve.wait_ge(cq_made, h - 1)
                dve.tensor_copy(wq_t[:, h % 2, :].rearrange("p (n d) -> p n d", n=2),
                                ps[0:DH, 4 + h % 2, 0:D].unsqueeze(1).to_broadcast([DH, 2, D])).then_inc(wq_copied, 1)
            for h in range(H):
                dve.wait_ge(u_made, h + 1)
                if h >= 2:
                    dve.wait_ge(u_stored[h % 2], 16 * (h // 2))
                dve.tensor_copy(u_h[:, h % 2, :], ps[0:TR, 1 + h % 2, 0:D]).then_inc(u_copied, 1)
            dve.wait_ge(cq_copied, H)
            for name, v in raw.items():
                last = dve.tensor_copy(t[name + "_hi"][:, :, :], v[:, :, :])
            last.then_inc(masked, 1)
            dve.wait_ge(masked, 2)
            for name, v in raw.items():
                last = dve.tensor_tensor(t[name + "_lo"][:, :, :], v[:, 0:2, :], whole(t[name + "_hi"][:, 0:2, :]), ALU.subtract)
            last.then_inc(masked, 1)
            dve.wait_ge(masked, 2)

        @block.scalar
        def _(act):
            for h in range(H):
                act.wait_ge(cq_made, h + 1)
                act.mul(raw["cq"].rearrange("p c (r h) -> p c r h", h=H)[:, :, :, h],
                        ps[:, 6 + h % 2, 0:3 * TR].rearrange("p (c r) -> p c r", c=3), QK_SCALE).then_inc(cq_copied, 1)
            act.wait_ge(cq_copied, H)

        @block.tensor
        def _(pe):
            ident = t["ident"]
            pe.wait_ge(loaded, 16 * n_loads)
            pe.wait_ge(added, 1)
            for k in range(2):
                last = pe.transpose(ps[0:DH, 0, k * TR:(k + 1) * TR], tab[:, k, :], ident[0:TR, 0:TR])
            last.then_inc(tables_turned, 1)
            for c in range(6):
                if c >= 3:
                    pe.wait_ge(tok_copied, c - 2)
                for k in range(2):
                    last = pe.transpose(ps[:, 1 + c % 3, k * HD:(k + 1) * HD], w_tok[:, k, c * 128:(c + 1) * 128],
                                        ident[0:HD, 0:HD])
                last.then_inc(tok_turned, 1)
            pe.wait_ge(tables_copied, 1)
            for h in range(H):
                if h >= 2:
                    pe.wait_ge(wq_copied, h - 1)
                for k in range(2):
                    last = pe.transpose(ps[0:DH, 4 + h % 2, k * HD:(k + 1) * HD],
                                        wq[:, k, h * DH:(h + 1) * DH], ident[0:HD, 0:HD])
                last.then_inc(wq_turned, 1)
                pe.wait_ge(wq_copied, h + 1)
                if h >= 2:
                    pe.wait_ge(cq_copied, h - 1)
                for k in range(3):
                    last = pe.matmul(ps[:, 6 + h % 2, k * TR:(k + 1) * TR], wq_t[:, h % 2, k * 128:(k + 1) * 128],
                                     tab_t[:, 0, :], start=True, stop=True)
                last.then_inc(cq_made, 1)
            pe.wait_ge(tok_copied, 6)
            for h in range(H):
                if h >= 2:
                    pe.wait_ge(u_copied, h - 1)
                pe.matmul(ps[0:TR, 1 + h % 2, 0:D], tab_t[:, 1, :], wp_h[:, h, :], start=True, stop=True).then_inc(u_made, 1)


class Chain:

    def __init__(self, eng, sem, it, per):
        self.eng, self.sem, self.it, self.per, self.k = eng, sem, it, per, 0

    def __call__(self, instruction):
        self.k += 1
        instruction.then_inc(self.sem, 1)
        self.eng.wait_ge(self.sem, self.it * self.per + self.k)

    def end(self):
        assert self.k == self.per, self.k


def spread(ap, n):
    return ap.unsqueeze(2).to_broadcast([ap.shape[0], ap.shape[1], n])


def phase_tokens(nc, a, t):
    with ExitStack() as ctx:
        def sb(name, shape, dt=F32):
            return ctx.enter_context(nc.sbuf_tensor("a_" + name, shape, dt))

        def sem(name):
            return semaphore(nc, t, "a_" + name)

        NT = 2 * N
        strip = sb("strip", [128, PATCH * IMG])
        raw = strip[0:PST, :]
        mem = sb("mem", [TM, 4 * HW + 2 * N])
        pix = sb("pix", [PST, GRID, PATCH * PATCH])
        pt = sb("pt", [128, 2, PST * GRID])
        h_sb = sb("h", [TM, 4, D])
        soft = sb("soft", [TM, 4 * N])
        xf = soft[:, 0:4 * D].rearrange("p (q d) -> p q d", q=4)
        xn = sb("xn", [TM, 4, 2 * D], F32R)
        stats = sb("stats", [TM, 4, 6])
        mv = sb("mv", [TM, 4, 2])
        std = sb("std", [TM, 4])
        rstd = sb("rstd", [TM, 4])
        xt = sb("xt", [128, 3, NT], F32R)
        qt = sb("qt", [TM, 4, TW])
        qa = sb("qa", [128, H, N])
        qrow = sb("qrow", [TM, 4, H, AUG])
        probs = soft[:, :].rearrange("p (u t n) -> p u t n", u=2, t=2)
        pts = [mem[:, 4 * HW:4 * HW + 2 * N].rearrange("p (t n) -> p t n", t=2), sb("pts", [TM, 2, N])]
        shift = sb("shift", [TM, 2, 2])
        rl = sb("rl", [TM, 2, 4])
        on = mem[:, 0:4 * HW].rearrange("p (i t d) -> p i t d", i=2, t=2)
        rel = qrow[:, :, :, :].rearrange("p q h r -> p (q h r)")[:, 0:4 * (ONE + 1) * H].rearrange("p (i t r h) -> p i t r h", i=2, t=2, h=H)
        pf = qt[:, :, :].rearrange("p (i t) f -> p i t f", i=2)
        ot = strip[:, 0:6 * N].rearrange("p (c n) -> p c n", c=6)
        pft = strip[0:UC, 6 * N:12 * N].rearrange("p (c n) -> p c n", c=6)
        lg = sb("lg", [TM, 4, NE])
        ka, va, qaug, ident = t["ka"], t["va"], t["qaug"], t["ident"]
        ps = ctx.enter_context(nc.psum_tensor("a_ps", [128, 8, 512], F32))

        patch_turned = Count(sem("patch_turned"), 6)
        patch_copied_a = Count(sem("patch_copied_a"), 3)
        patch_copied_v = Count(sem("patch_copied_v"), 3)
        tok_made = Count(sem("tok_made"), 2)
        embedded = Count(sem("embedded"), 2)
        var_ready = Count(sem("var_ready"), 2)
        std_ready = Count(sem("std_ready"), 2)
        xn_ready = Count(sem("xn_ready"), 2)
        x_turned = Count(sem("x_turned"), 6)
        x_copied_a = Count(sem("x_copied_a"), 5)
        x_copied_v = Count(sem("x_copied_v"), 1)
        LIN = [("qt", q, n) for q in range(4) for n in range(2)]
        LIN += [("v", q, n) for q in range(4) for n in range(2)]
        for im in range(2):
            LIN += [(kind, c, im) for c in range(6) for kind in ("q", "k")]
            LIN += [("aug", g, im) for g in range(3)]
        NL = len(LIN)
        NL0 = NL - 15
        LIN_IMAGE = [range(NL0), range(NL0, NL)]

        def lin_bank(j):
            return (j - NL0) % 4 if j >= NL0 else 4 if j == NL0 - 1 else (2 + j) % 8
        lin_made = Count(sem("lin_made"), NL)
        lin_copied_a = Count(sem("lin_copied_a"), (NL + 1) // 2)
        lin_copied_v = Count(sem("lin_copied_v"), NL // 2)
        pix_ready = Count(sem("pix_ready"), 2)
        biased = Count(sem("biased"), 1)
        token0_set = Count(sem("token0_set"), 1)
        aug_fixed = Count(sem("aug_fixed"), 1)
        aug_fixed_a = Count(sem("aug_fixed_a"), 1)
        U = 2 * H
        scored = Count(sem("scored"), U)
        shift_ready = Count(sem("shift_ready"), U)
        probs_ready = Count(sem("probs_ready"), U)
        probs_turned = Count(sem("probs_turned"), U)
        probs_copied = Count(sem("probs_copied"), U)
        heads_made = Count(sem("heads_made"), U)
        heads_copied = Count(sem("heads_copied"), 6)
        TAIL = 7
        tail_made = Count(sem("tail_made"), 2 * TAIL)
        tail_copied_a = Count(sem("tail_copied_a"), 6)
        tail_copied_v = Count(sem("tail_copied_v"), 8)
        gate_made = Count(sem("gate_made"), 1)
        gate_ready = Count(sem("gate_ready"), 1)
        stores_done = Count(sem("stores_done"), 3)
        raw_loaded = Dmas(sem("raw_loaded"), 1)
        qt_stored = Dmas(sem("qt_stored"), 4)
        aug_loaded = Dmas(sem("aug_loaded"), 8)
        rel_stored = Dmas(sem("rel_stored"), 14)
        pf_loaded = [Dmas(sem(f"pf_loaded{i}"), 2) for i in range(2)]
        h_stored = Dmas(sem("h_stored"), 4)
        norm_stored = Dmas(sem("norm_stored"), 4)
        lg_stored = Dmas(sem("lg_stored"), 4)
        dve_chain = sem("dve_chain")
        norm_chain = [sem("norm_chain0"), sem("norm_chain1")]

        strips = a["x"].rearrange("b c (g i) w -> (b c g) (i w)", i=PATCH)
        qt_rows = t["qt"].rearrange("i (n f) -> i n f", f=TW)
        GROUPS = [(half, w0, min(w0 + 6, GRID)) for half in range(2) for w0 in range(0, GRID, 6)]
        PATCH_BANK = (4, 5, 6, 7, 2, 3)

        def skew(dram, im, tile, base, run):
            first, rows = (1, 7) if tile == 0 else (T0, 8)
            rn = (first - 1) // SIDE
            at = im * N * TW + first * TW
            if base == 0:
                at += (LREL + 1 - rn) * H
                return bass.AP(dram.tensor, at, [[SIDE * TW - H, rows], [TW, SIDE], [1, run]])
            at += NV * H + (SIDE - 1) * H
            return bass.AP(dram.tensor, at, [[SIDE * TW, rows], [TW - H, SIDE], [1, run]])

        def tail_copy(k):
            im, j = divmod(k, TAIL)
            return (tail_copied_a, 3 * im + j // 2 + 1) if j in (0, 2, 4) else (tail_copied_v, 4 * im + {1: 1, 3: 2, 5: 3, 6: 4}[j])

        block = ctx.enter_context(nc.Block())

        @block.sync
        def _(sp):
            sp.sem_inc(stores_done.sem, stores_done.per)

            def one(it):
                for q in range(4):
                    im, tile = divmod(q, 2)
                    sp.wait_ge(lin_copied_a.sem, lin_copied_a.now(it, q + 1))
                    sp.sem_inc(t["held"], 1)
                    sp.wait_ge(lin_copied_v.sem, lin_copied_v.now(it, q + 1))
                    sp.dma_start(qt_rows[im, TILE0[tile]:TILE0[tile] + PART[tile], :],
                                 qt[0:PART[tile], q, :]).then_inc(qt_stored.sem, 16)
                sp.wait_ge(qt_stored.sem, qt_stored.now(it))
                for q in range(4):
                    im, tile = divmod(q, 2)
                    p0 = 1 - tile
                    for base, r0, run in ((0, 0, VRUN), (1, ROWS, HRUN)):
                        sp.dma_start(qaug[p0:PART[tile], q, r0:r0 + run // H, :].rearrange("p r h -> p (r h)"),
                                     skew(t["qt"], im, tile, base, run)).then_inc(aug_loaded.sem, 16)
                for im in range(2):
                    sp.wait_ge(heads_copied.sem, heads_copied.now(it, 3 * (im + 1)))
                    for tile in range(2):
                        p0, p1 = 1 - tile, PART[tile]
                        for base, r0, run in ((0, 0, VRUN), (1, ROWS, HRUN)):
                            sp.dma_start(skew(t["pr"], im, tile, base, run),
                                         rel[p0:p1, im, tile, r0:r0 + run // H, :].rearrange("p r h -> p (r h)")).then_inc(rel_stored.sem, 16)
                        sp.dma_start(t["pr"][im].rearrange("(n f) -> n f", f=TW)[TILE0[tile] + p0:TILE0[tile] + p1, 0:H],
                                     rel[p0:p1, im, tile, CLS, :]).then_inc(rel_stored.sem, 16)
                    sp.dma_start(t["pr"][im:im + 1, 0:H], rel[0:1, im, 0, ONE, :]).then_inc(rel_stored.sem, 16)
                    sp.wait_ge(rel_stored.sem, rel_stored.now(it, 7 * (im + 1)))
                    for tile in range(2):
                        sp.dma_start(pf[0:PART[tile], im, tile, :],
                                     t["pr"][im].rearrange("(n f) -> n f", f=TW)[TILE0[tile]:TILE0[tile] + PART[tile], :]
                                     ).then_inc(pf_loaded[im].sem, 16)
                sp.wait_ge(tail_copied_v.sem, tail_copied_v.now(it))
                for q in range(4):
                    im, tile = divmod(q, 2)
                    at = it * NT + (im * N + TILE0[tile])
                    sp.dma_start(t["h1"][bass.ds(at, PART[tile]), :], h_sb[0:PART[tile], q, :]).then_inc(h_stored.sem, 16)
                sp.wait_ge(h_stored.sem, h_stored.now(it))
                sp.sem_inc(stores_done.sem, 1)
                sp.wait_ge(xn_ready.sem, xn_ready.now(it, 2))
                for q in range(4):
                    im, tile = divmod(q, 2)
                    at = it * NT + (im * N + TILE0[tile])
                    sp.dma_start(t["ys"][bass.ds(at + SLOTS, PART[tile]), :], xf[0:PART[tile], q, :]).then_inc(norm_stored.sem, 16)
                sp.wait_ge(norm_stored.sem, norm_stored.now(it))
                sp.sem_inc(stores_done.sem, 1)
                sp.wait_ge(gate_ready.sem, gate_ready.now(it))
                for q in range(4):
                    im, tile = divmod(q, 2)
                    at = it * NT + (im * N + TILE0[tile])
                    sp.dma_start(t["lg"][bass.ds(at, PART[tile]), :], lg[0:PART[tile], q, :]).then_inc(lg_stored.sem, 16)
                sp.wait_ge(lg_stored.sem, lg_stored.now(it))
                sp.sem_inc(stores_done.sem, 1)

            with sp.Fori(0, PAIRS) as it:
                one(it)

        @block.gpsimd
        def _(pool):
            for c in (pix_ready, biased, token0_set, aug_fixed):
                pool.sem_inc(c.sem, c.per)
            with pool.Fori(0, PAIRS) as it:
                pool.wait_ge(pix_ready.sem, pix_ready.last(it))
                pool.sem_inc(t["held"], 1)
                pool.dma_start(raw[:, :], strips[bass.ds(it * PST, PST), :]).then_inc(raw_loaded.sem, 16)
                pool.wait_ge(patch_turned.sem, patch_turned.last(it))
                pool.wait_ge(raw_loaded.sem, raw_loaded.now(it))
                pool.sem_inc(t["held"], 1)
                for half in range(2):
                    pool.tensor_copy(pix[:, :, half * 128:half * 128 + 128].rearrange("p w (i j) -> p i w j", j=PATCH),
                                     raw[:, half * 8 * IMG:(half + 1) * 8 * IMG].rearrange("p (i w j) -> p i w j", i=PATCH // 2, j=PATCH)
                                     ).then_inc(pix_ready.sem, 1)
                pool.wait_ge(xn_ready.sem, xn_ready.now(it, 1))
                for q in range(4):
                    last = pool.tensor_tensor(h_sb[:, q, :], h_sb[:, q, :], t["b_proj"][:, :], ALU.add)
                last.then_inc(biased.sem, 1)
                pool.wait_ge(lin_copied_a.sem, lin_copied_a.now(it, 4))
                pool.wait_ge(lin_copied_v.sem, lin_copied_v.now(it, 4))
                pool.sem_inc(t["held"], 1)
                for q in range(4):
                    last = pool.tensor_copy(qaug[:, q, CLS, :], qt[:, q, 0:H])
                for q in (0, 2):
                    last = pool.tensor_copy(qaug[0:1, q, 0:ROWS, :], qt[0:1, q, 0:H].unsqueeze(1).to_broadcast([1, ROWS, H]))
                last.then_inc(token0_set.sem, 1)
                pool.wait_ge(token0_set.sem, token0_set.now(it))
                pool.wait_ge(aug_loaded.sem, aug_loaded.now(it))
                pool.sem_inc(t["held"], 1)
                for q in range(1):
                    last = pool.tensor_copy(qrow[:, q, :, :].rearrange("p h r -> p r h"), qaug[:, q, :, :])
                last.then_inc(aug_fixed.sem, 1)

        @block.scalar
        def _(act):
            for c in (patch_copied_a, std_ready, x_copied_a, lin_copied_a, aug_fixed_a, probs_ready, tail_copied_a):
                act.sem_inc(c.sem, c.per)

            def patches(it):
                for g in (0, 2, 4):
                    half, w0, w1 = GROUPS[g]
                    act.wait_ge(patch_turned.sem, patch_turned.now(it, g + 1))
                    act.copy(pt[:, half, :].rearrange("p (s w) -> p w s", w=GRID)[:, w0:w1, :],
                             ps[:, PATCH_BANK[g], 0:(w1 - w0) * PST].rearrange("p (w s) -> p w s", s=PST)).then_inc(patch_copied_a.sem, 1)

            def root(it, n):
                act.wait_ge(var_ready.sem, var_ready.now(it, n + 1))
                act.activation(std[:, :], mv[:, :, 1], ACT.Sqrt, bias=t["eps"][0:TM, :]).then_inc(std_ready.sem, 1)

            def copy_x(it, n):
                if n == 0:
                    for c in (0, 2):
                        act.wait_ge(x_turned.sem, x_turned.now(it, c + 1))
                        act.copy(xt[:, c, :], ps[:, c, 0:NT]).then_inc(x_copied_a.sem, 1)
                else:
                    for c in range(3):
                        act.wait_ge(x_turned.sem, x_turned.now(it, 4 + c))
                        act.copy(xt[:, c, :], ps[:, 3 + c, 0:NT]).then_inc(x_copied_a.sem, 1)

            def pair(it, more):
                def lins(im):
                    for j in LIN_IMAGE[im]:
                        if j % 2:
                            continue
                        act.wait_ge(lin_made.sem, lin_made.now(it, j + 1))
                        bank, (kind, c, n) = lin_bank(j), LIN[j]
                        if kind == "qt":
                            last = act.copy(qt[:, c, n * TW // 2:(n + 1) * TW // 2], ps[0:TM, bank, 0:TW // 2])
                        elif kind == "v":
                            last = act.copy(va[:, c, 6 * n:6 * n + 6, 0:DH], ps[0:TM, bank, 0:HW // 2].rearrange("p (h d) -> p h d", d=DH))
                        elif kind == "q":
                            for s in range(2):
                                last = act.mul(qa[0:DH, 2 * c + s, :], ps[DH * s:DH * s + DH, bank, 0:N], QK_SCALE)
                        elif kind == "k":
                            for s in range(2):
                                last = act.copy(ka[0:DH, 2 * c + s, :], ps[DH * s:DH * s + DH, bank, 0:N])
                        else:
                            for s in range(4):
                                last = act.copy(qa[DH:DH + AUG, 4 * c + s, :], ps[AUG * s:AUG * s + AUG, bank, 0:N])
                        last.then_inc(lin_copied_a.sem, 1)
                        if j == 24:
                            act.wait_ge(aug_loaded.sem, aug_loaded.now(it))
                            act.wait_ge(token0_set.sem, token0_set.now(it))
                            for q in range(1, 4):
                                last = act.copy(qrow[:, q, :, :].rearrange("p h r -> p r h"), qaug[:, q, :, :])
                            last.then_inc(aug_fixed_a.sem, 1)

                def softmax(im):
                    for u in range(im * H, im * H + H):
                        act.wait_ge(shift_ready.sem, shift_ready.now(it, u + 1))
                        if u >= 2:
                            act.wait_ge(probs_turned.sem, probs_turned.now(it, u - 1))
                        for tile in range(2):
                            last = act.activation(probs[:, u % 2, tile, :], ps[0:TM, u % 2, tile * N:(tile + 1) * N], ACT.Exp,
                                                  bias=shift[:, u % 2, tile:tile + 1])
                        last.then_inc(probs_ready.sem, 1)

                for im in range(2):
                    lins(im)
                    softmax(im)
                if more:
                    act.wait_ge(pix_ready.sem, pix_ready.now(it + 1))
                for k in range(2 * TAIL):
                    im, j = divmod(k, TAIL)
                    if j in (0, 2, 4):
                        act.wait_ge(tail_made.sem, tail_made.now(it, k + 1))
                        if j < 3:
                            last = act.copy(ot[:, 2 * j:2 * j + 2, :], ps[:, k % 4, 0:2 * N].rearrange("p (c n) -> p c n", c=2))
                        else:
                            last = act.copy(pft[:, 2 * j - 6:2 * j - 4, :], ps[0:UC, k % 4, 0:2 * N].rearrange("p (c n) -> p c n", c=2))
                        last.then_inc(tail_copied_a.sem, 1)
                if more:
                    patches(it + 1)
                root(it, 1)
                copy_x(it, 1)
                if more:
                    root(it + 1, 0)
                    copy_x(it + 1, 0)

            patches(0)
            root(0, 0)
            copy_x(0, 0)
            with act.Fori(0, PAIRS - 1) as it:
                pair(it, True)
            pair(PAIRS - 1, False)

        @block.vector
        def _(dve):
            for c in (patch_copied_v, embedded, var_ready, xn_ready, x_copied_v, lin_copied_v, shift_ready, probs_copied,
                      heads_copied, tail_copied_v, gate_ready):
                dve.sem_inc(c.sem, c.per)

            def norm(it, n):
                link = Chain(dve, norm_chain[n], it, 4)
                for q in range(2 - 2 * n, 4):
                    last = dve.bn_stats(stats[:, q, :], h_sb[:, q, :])
                link(last)
                dve.sem_inc(t["held"], 1)
                for q in range(4):
                    last = dve.bn_aggr(mv[:, q, :], stats[:, q, :])
                last.then_inc(var_ready.sem, 1)
                dve.wait_ge(std_ready.sem, std_ready.now(it, n + 1))
                link(dve.reciprocal(rstd[:, :], std[:, :]))
                if n == 0:
                    dve.wait_ge(x_turned.sem, x_turned.last(it))
                    dve.wait_ge(stores_done.sem, stores_done.last(it, 2))
                for q in range(4):
                    last = dve.tensor_scalar(xf[:, q, :], h_sb[:, q, :], mv[:, q, 0:1], rstd[:, q:q + 1], ALU.subtract, ALU.mult)
                link(last)
                link(dve.tensor_copy(xn[:, :, 0:D], xf[:, :, :]))
                dve.tensor_tensor(xn[:, :, D:2 * D], xf[:, :, :], whole(xn[:, :, 0:D]), ALU.subtract).then_inc(xn_ready.sem, 1)
                link.end()

            def copy_x(it):
                dve.wait_ge(x_turned.sem, x_turned.now(it, 2))
                dve.tensor_copy(xt[:, 1, :], ps[:, 1, 0:NT]).then_inc(x_copied_v.sem, 1)

            def patches(it):
                for g in (1, 3, 5):
                    half, w0, w1 = GROUPS[g]
                    dve.wait_ge(patch_turned.sem, patch_turned.now(it, g + 1))
                    dve.tensor_copy(pt[:, half, :].rearrange("p (s w) -> p w s", w=GRID)[:, w0:w1, :],
                                    ps[:, PATCH_BANK[g], 0:(w1 - w0) * PST].rearrange("p (w s) -> p w s", s=PST)).then_inc(patch_copied_v.sem, 1)

            def embed(it, stores):
                dve.wait_ge(stores_done.sem, stores)
                for im in range(2):
                    dve.wait_ge(tok_made.sem, tok_made.now(it, im + 1))
                    dve.tensor_tensor(h_sb[:, 2 * im:2 * im + 2, :], ps[0:TM, im, 0:2 * D].rearrange("p (q d) -> p q d", q=2),
                                      t["b_tok"][:, :].unsqueeze(1).to_broadcast([TM, 2, D]), ALU.add).then_inc(embedded.sem, 1)
                    dve.wait_ge(embedded.sem, embedded.now(it, im + 1))
                    if im == 0:
                        for q in range(2):
                            dve.bn_stats(stats[:, q, :], h_sb[:, q, :])

            def pair(it, more):
                link = Chain(dve, dve_chain, it, 6)
                def lins(im):
                    for j in LIN_IMAGE[im]:
                        bank, (kind, c, n) = lin_bank(j), LIN[j]
                        if j % 2:
                            dve.wait_ge(lin_made.sem, lin_made.now(it, j + 1))
                            if kind == "qt":
                                last = dve.tensor_copy(qt[:, c, n * TW // 2:(n + 1) * TW // 2], ps[0:TM, bank, 0:TW // 2])
                            elif kind == "v":
                                last = dve.tensor_copy(va[:, c, 6 * n:6 * n + 6, 0:DH], ps[0:TM, bank, 0:HW // 2].rearrange("p (h d) -> p h d", d=DH))
                            elif kind == "q":
                                for s in range(2):
                                    last = dve.tensor_scalar(qa[0:DH, 2 * c + s, :], ps[DH * s:DH * s + DH, bank, 0:N], QK_SCALE, None, ALU.mult)
                            elif kind == "k":
                                for s in range(2):
                                    last = dve.tensor_copy(ka[0:DH, 2 * c + s, :], ps[DH * s:DH * s + DH, bank, 0:N])
                            else:
                                for s in range(4):
                                    last = dve.tensor_copy(qa[DH:DH + AUG, 4 * c + s, :], ps[AUG * s:AUG * s + AUG, bank, 0:N])
                            last.then_inc(lin_copied_v.sem, 1)

                def heads(im):
                    for step in range(H + 5):
                        if step < H:
                            u = im * H + step
                            dve.wait_ge(scored.sem, scored.now(it, u + 1))
                            if u >= 2:
                                dve.wait_ge(probs_ready.sem, probs_ready.now(it, u - 1))
                            dve.tensor_reduce(shift[:, u % 2, :], ps[0:TM, u % 2, 0:NT].rearrange("p (q m) -> p q m", q=2), AX_X, ALU.max,
                                              negate=True).then_inc(shift_ready.sem, 1)
                        if 0 <= step - 2 < H:
                            u = im * H + step - 2
                            dve.wait_ge(probs_turned.sem, probs_turned.now(it, u + 1))
                            if u >= 2:
                                dve.wait_ge(heads_made.sem, heads_made.now(it, u - 1))
                            dve.tensor_copy(pts[u % 2][:, :, :], ps[0:TM, 2 + u % 2, 0:NT].rearrange("p (q n) -> p q n", q=2)).then_inc(probs_copied.sem, 1)
                        if step >= 7 and (step - 7) % 4 == 0 and (step - 7) // 4 < 3:
                            g = (step - 7) // 4
                            grp = 3 * im + g
                            dve.wait_ge(heads_made.sem, heads_made.now(it, 4 * grp + 4))
                            acc = ps[0:TM, 4 + 2 * (grp % 2):6 + 2 * (grp % 2), 0:4 * VW].rearrange("p q (h w) -> p q h w", w=VW)
                            link(dve.reciprocal(rl[:, :, :], acc[:, :, :, VW - 1]))
                            for tile in range(2):
                                dve.tensor_tensor(on[:, im, tile, 4 * g * DH:(4 * g + 4) * DH].rearrange("p (h d) -> p h d", d=DH),
                                                  acc[:, tile, :, 0:DH], spread(rl[:, tile, :], DH), ALU.mult)
                                last = dve.tensor_tensor(rel[:, im, tile, :, 4 * g:4 * g + 4].rearrange("p r h -> p h r"),
                                                         acc[:, tile, :, DH:VW], spread(rl[:, tile, :], ONE + 1), ALU.mult)
                            last.then_inc(heads_copied.sem, 1)

                for im in range(2):
                    lins(im)
                    heads(im)
                if more:
                    dve.wait_ge(pix_ready.sem, pix_ready.now(it + 1))
                for k in range(2 * TAIL):
                    im, j = divmod(k, TAIL)
                    if j in (0, 2, 4):
                        continue
                    if more and k == 2 * TAIL - 1:
                        patches(it + 1)
                    dve.wait_ge(tail_made.sem, tail_made.now(it, k + 1))
                    if j < 3:
                        last = dve.tensor_copy(ot[:, 2 * j:2 * j + 2, :], ps[:, k % 4, 0:2 * N].rearrange("p (c n) -> p c n", c=2))
                    elif j < 6:
                        last = dve.tensor_copy(pft[:, 2 * j - 6:2 * j - 4, :], ps[0:UC, k % 4, 0:2 * N].rearrange("p (c n) -> p c n", c=2))
                    else:
                        if im == 0:
                            dve.wait_ge(biased.sem, biased.now(it))
                        last = dve.tensor_tensor(h_sb[:, 2 * im:2 * im + 2, :], ps[0:TM, k % 4, 0:2 * D].rearrange("p (q d) -> p q d", q=2),
                                                 h_sb[:, 2 * im:2 * im + 2, :], ALU.add)
                    last.then_inc(tail_copied_v.sem, 1)
                dve.wait_ge(tail_copied_v.sem, tail_copied_v.now(it))
                norm(it, 1)
                if more:
                    embed(it + 1, stores_done.now(it, 1))
                    norm(it + 1, 0)
                dve.wait_ge(stores_done.sem, stores_done.last(it))
                dve.wait_ge(gate_made.sem, gate_made.now(it))
                dve.tensor_tensor(lg[:, :, :], ps[0:TM, 6, 0:4 * NE].rearrange("p (q e) -> p q e", q=4),
                                  t["b_gate"][:, :].unsqueeze(1).to_broadcast([TM, 4, NE]), ALU.add).then_inc(gate_ready.sem, 1)
                if more:
                    copy_x(it + 1)
                link.end()

            dve.memset(qa[DH + AUG:128, :, :], 0.0)
            patches(0)
            embed(0, stores_done.per)
            norm(0, 0)
            copy_x(0)
            with dve.Fori(0, PAIRS - 1) as it:
                pair(it, True)
            pair(PAIRS - 1, False)

        @block.tensor
        def _(pe):
            for c in (patch_turned, tok_made, x_turned, lin_made, scored, probs_turned, heads_made, tail_made, gate_made):
                pe.sem_inc(c.sem, c.per)

            def turn_x(it, n):
                pe.wait_ge(xn_ready.sem, xn_ready.now(it, n + 1))
                for c in range(3):
                    for q in range(4):
                        im, tile = divmod(q, 2)
                        m = PART[tile]
                        at = im * N + TILE0[tile]
                        last = pe.transpose(parts(ps[:, 3 * n + c, at:at + m]), xn[0:m, q, c * 128:(c + 1) * 128], t["ident_r"][0:m, 0:m])
                    last.then_inc(x_turned.sem, 1)
                pe.wait_ge(x_copied_a.sem, x_copied_a.now(it, 3 * n + 2))
                if n == 0:
                    pe.wait_ge(x_copied_v.sem, x_copied_v.now(it))

            def turn_patches(it):
                for g, (half, w0, w1) in enumerate(GROUPS):
                    pe.wait_ge(pix_ready.sem, pix_ready.now(it, half + 1))
                    for w in range(w0, w1):
                        last = pe.transpose(ps[:, PATCH_BANK[g], (w - w0) * PST:(w - w0 + 1) * PST], pix[:, w, 128 * half:128 * half + 128], ident[0:PST, 0:PST])
                    last.then_inc(patch_turned.sem, 1)

            def tokens(it):
                pe.wait_ge(patch_copied_a.sem, patch_copied_a.now(it))
                pe.wait_ge(patch_copied_v.sem, patch_copied_v.now(it))
                for im in range(2):
                    for tile in range(2):
                        at = im * 3 * N + 3 * TILE0[tile]
                        for c in range(6):
                            first = at + c // 2
                            last = pe.matmul(ps[0:TM, im, tile * D:(tile + 1) * D], pt[:, c % 2, first:first + 3 * (TM - 1) + 1:3],
                                             t["w_tok_t"][:, c, :], start=(c == 0), stop=(c == 5))
                    last.then_inc(tok_made.sem, 1)

            def pair(it, more):
                def lins(of):
                    for j in LIN_IMAGE[of]:
                        bank, (kind, c, n) = lin_bank(j), LIN[j]
                        before = j - 4 if j >= NL0 - 1 else j - 8
                        if j < NL0 and before >= 0 or before >= NL0:
                            copied = lin_copied_v if before % 2 else lin_copied_a
                            pe.wait_ge(copied.sem, copied.now(it, before // 2 + 1))
                        elif j in (NL0, NL0 + 1):
                            pe.wait_ge(probs_ready.sem, probs_ready.now(it, H))
                        elif j in (NL0 + 2, NL0 + 3):
                            pe.wait_ge(probs_copied.sem, probs_copied.now(it, H))
                        if j == 4:
                            pe.wait_ge(gate_ready.sem, gate_ready.last(it))
                        if kind == "aug" and c == 0:
                            pe.wait_ge(aug_loaded.sem, aug_loaded.now(it))
                            pe.wait_ge(aug_fixed.sem, aug_fixed.now(it))
                            pe.wait_ge(aug_fixed_a.sem, aug_fixed_a.now(it))
                        if kind == "aug":
                            for tile in range(2):
                                m, to = PART[tile], TILE0[tile]
                                last = pe.transpose(ps[:, bank, to:to + m], qrow[0:m, 2 * n + tile, 4 * c:4 * c + 4, :].rearrange("p h r -> p (h r)"),
                                                    ident[0:m, 0:m])
                        elif kind in ("qt", "v"):
                            at = (c // 2) * N + TILE0[c % 2]
                            name, w = ("cq", TW // 2) if kind == "qt" else ("wv", HW // 2)
                            last = width_product(pe, ps[0:TM, bank, 0:w], (t[name + "_hi"], t[name + "_lo"]), slice(n * w, (n + 1) * w),
                                                 lambda block, rows: xt[0:rows, block, at:at + TM], True)
                        else:
                            last = width_product(pe, ps[:, bank, 0:N], (t["w" + kind + "_hi"], t["w" + kind + "_lo"]), slice(c * 128, (c + 1) * 128),
                                                 lambda block, rows: xt[0:rows, block, n * N:(n + 1) * N], False)
                        last.then_inc(lin_made.sem, 1)

                def copied_to(j):
                    pe.wait_ge(lin_copied_a.sem, lin_copied_a.now(it, j // 2 + 1))
                    pe.wait_ge(lin_copied_v.sem, lin_copied_v.now(it, (j + 1) // 2))

                def heads(im):
                    for step in range(H + 3):
                        if step < H:
                            u = im * H + step
                            if step == 0:
                                copied_to(LIN.index(("aug", 0, im)))
                            if step == 1:
                                copied_to(LIN.index(("aug", 1, im)))
                            if step == 2:
                                copied_to(LIN_IMAGE[im][-1])
                            if u >= 2:
                                pe.wait_ge(probs_ready.sem, probs_ready.now(it, u - 1))
                            for tile in range(2):
                                at = TILE0[tile]
                                last = pe.matmul(ps[0:TM, u % 2, tile * N:(tile + 1) * N], qa[:, step, at:at + TM], ka[:, step, :],
                                                 start=True, stop=True)
                            last.then_inc(scored.sem, 1)
                        if 0 <= step - 2 < H:
                            u = im * H + step - 2
                            pe.wait_ge(probs_ready.sem, probs_ready.now(it, u + 1))
                            if u >= 2:
                                pe.wait_ge(probs_copied.sem, probs_copied.now(it, u - 1))
                            for mt in range(2):
                                for tile in range(2):
                                    m = PART[tile]
                                    last = pe.transpose(ps[0:TM, 2 + u % 2, mt * N + TILE0[tile]:mt * N + TILE0[tile] + m],
                                                        probs[0:m, u % 2, tile, TILE0[mt]:TILE0[mt] + TM], ident[0:m, 0:m])
                            last.then_inc(probs_turned.sem, 1)
                        if 0 <= step - 3 < H:
                            h = step - 3
                            u = im * H + h
                            grp = u // 4
                            pe.wait_ge(probs_copied.sem, probs_copied.now(it, u + 1))
                            if u % 4 == 0 and grp >= 2:
                                pe.wait_ge(heads_copied.sem, heads_copied.now(it, grp - 1))
                            for tile in range(2):
                                for mt in range(2):
                                    last = pe.matmul(ps[0:TM, 4 + 2 * (grp % 2) + tile, (u % 4) * VW:(u % 4 + 1) * VW],
                                                     pts[u % 2][0:PART[mt], mt, TILE0[tile]:TILE0[tile] + TM],
                                                     va[0:PART[mt], 2 * im + mt, h, :], start=(mt == 0), stop=(mt == 1))
                            last.then_inc(heads_made.sem, 1)

                for im in range(2):
                    lins(im)
                    heads(im)
                for k in range(2 * TAIL):
                    im, j = divmod(k, TAIL)
                    if k >= 4:
                        copied, n = tail_copy(k - 4)
                        pe.wait_ge(copied.sem, copied.now(it, n))
                    if j == 0:
                        pe.wait_ge(heads_copied.sem, heads_copied.now(it, 3 * im + 3))
                    if j == 3:
                        pe.wait_ge(pf_loaded[im].sem, pf_loaded[im].now(it))
                    if j < 6:
                        src, w = (on, 128) if j < 3 else (pf, UC)
                        for c in range(2):
                            at = (2 * (j % 3) + c) * w
                            for tile in range(2):
                                m = PART[tile]
                                last = pe.transpose(ps[0:w, k % 4, c * N + TILE0[tile]:c * N + TILE0[tile] + m],
                                                    src[0:m, im, tile, at:at + w], ident[0:m, 0:m])
                    else:
                        pe.wait_ge(tail_copied_a.sem, tail_copied_a.now(it, 3 * im + 3))
                        pe.wait_ge(tail_copied_v.sem, tail_copied_v.now(it, 4 * im + 3))
                        if more and im == 1:
                            turn_patches(it + 1)
                        for tile in range(2):
                            n0 = TILE0[tile]
                            for c in range(12):
                                lhs, rhs = (ot[:, c, n0:n0 + TM], t["wp2"][:, c, :]) if c < 6 else (pft[:, c - 6, n0:n0 + TM], t["u_sb"][:, c - 6, :])
                                last = pe.matmul(ps[0:TM, k % 4, tile * D:(tile + 1) * D], lhs, rhs, start=(c == 0), stop=(c == 11))
                    last.then_inc(tail_made.sem, 1)
                if more:
                    pe.wait_ge(heads_copied.sem, heads_copied.now(it))
                    pe.wait_ge(tail_copied_a.sem, tail_copied_a.now(it))
                    pe.wait_ge(tail_copied_v.sem, tail_copied_v.now(it))
                    tokens(it + 1)
                turn_x(it, 1)
                for q in range(4):
                    at = (q // 2) * N + TILE0[q % 2]
                    last = width_product(pe, ps[0:TM, 6, q * NE:(q + 1) * NE], (t["sw_hi"], t["sw_lo"]), slice(0, NE),
                                         lambda block, rows: xt[0:rows, block, at:at + TM], True)
                last.then_inc(gate_made.sem, 1)
                if more:
                    turn_x(it + 1, 0)

            turn_patches(0)
            tokens(0)
            turn_x(0, 0)
            with pe.Fori(0, PAIRS - 1) as it:
                pair(it, True)
            pair(PAIRS - 1, False)


def constants():
    key = np.zeros((N, ONE + 1), np.float32)
    m = np.arange(1, N)
    key[m, (m - 1) // SIDE] = 1
    key[m, ROWS + (m - 1) % SIDE] = 1
    key[0, CLS] = 1
    key_aug = np.zeros((AUG, 2 * N), np.float32)
    key_aug[:ONE + 1] = np.concatenate([key, key]).T
    key[:, ONE] = 1
    val = np.stack([key[n0:n0 + TM] for n0 in TILE0])
    val_aug = np.ascontiguousarray(np.broadcast_to(val[:, :, None, :], (2, TM, H, ONE + 1)))
    rep = lambda v: np.ascontiguousarray(np.broadcast_to(v.astype(np.float32), (98, v.shape[-1])))
    return {
        "const_ident": np.eye(128, dtype=np.float32), "const_key_aug": key_aug, "const_val_aug": val_aug,
        "const_ones": np.ones((98, 98), np.float32),
        "const_before": np.triu(np.ones((98, 98), np.float32), 1),
        "const_rank": rep(NE - np.arange(NE)), "const_base": rep(CAP * np.arange(NE)),
        "const_own": (SLOTS + np.arange(128)[None, :] * 98 + np.arange(98)[:, None]).astype(np.float32),
    }


def dram(nc, kind="Internal"):
    def d(name, shape, dt=F32, kind=kind):
        return nc.dram_tensor(name, shape, dt, kind=kind).ap()

    return {
        "u": d("u", (TW, D), kind="Internal"),
        "qt": d("qt", (2, N * TW), kind="Internal"),
        "pr": d("pr", (2, N * TW), kind="Internal"),
        "h1": d("h1", (TOK, D)),
        "xs": d("xs", (SLOTS + TOK, D)),
        "ys": d("ys", (SLOTS + TOK, D)),
        "lg": d("lg", (TOK, NE)),
        "h3": d("h3", (TOK, D)),
        "slot": d("slot", (TOK, 1), I32),
        "pm": d("pm", (TOK, 1)),
    }


def keep(nc, ctx, t):
    for name, shape in {
        "eps": [128, 1], "w_tok_t": [128, 6, D], "wq_hi": [128, 3, HW], "wq_lo": [128, 2, HW], "wk_hi": [128, 3, HW],
        "wk_lo": [128, 2, HW], "wv_hi": [128, 3, HW], "wv_lo": [128, 2, HW], "cq_hi": [128, 3, TW], "cq_lo": [128, 2, TW], "wp2": [128, 6, D], "u_sb": [UC, 6, D],
        "sw_hi": [128, 3, NE], "sw_lo": [128, 2, NE],
        "b_tok": [TM, D], "b_proj": [TM, D], "b_gate": [TM, NE], "ka": [128, H, N], "va": [TM, 4, H, VW],
        "qaug": [TM, 4, AUG, H],
    }.items():
        t[name] = ctx.enter_context(nc.sbuf_tensor("k_" + name, shape, F32R if name[-3:] in ("_hi", "_lo") else F32))


RP = 98
RQ = TOK // RP
BITS = 28


def phase_route(nc, a, t):
    with ExitStack() as ctx:
        def sb(name, shape, dt=F32):
            return ctx.enter_context(nc.sbuf_tensor("r_" + name, shape, dt))

        def sem(name):
            return semaphore(nc, t, "r_" + name)

        lg = sb("lg", [RP, RQ, NE])
        e = sb("e", [RP, NE, RQ])
        eq = sb("eq", [RP, NE, RQ])
        key = sb("key", [RP, NE, RQ])
        hit = sb("hit", [RP, NE, RQ])
        kept = sb("kept", [RP, NE, RQ])
        before = sb("before", [RP, NE, RQ])
        totals = sb("totals", [RP, NE, RQ])
        ones_row = sb("ones_row", [RP, RQ])
        mx = sb("mx", [RP, RQ])
        sm = sb("sm", [RP, RQ])
        pm = sb("pm", [RP, RQ])
        slot = sb("slot", [RP, RQ])
        has = sb("has", [RP, RQ])
        own = sb("own", [RP, RQ])
        slot_t = sb("slot_t", [RQ, RP])
        pm_t = sb("pm_t", [RQ, RP])
        slot_ti = sb("slot_ti", [RQ, RP], I32)
        slot_i = sb("slot_i", [RP, RQ], I32)
        rank_w = sb("rank_w", [RP, NE])
        base_w = sb("base_w", [RP, NE])
        thr = sb("thr", [RP, NE])
        trial = sb("trial", [RP, NE])
        step = sb("step", [RP, 1])
        cnt = sb("cnt", [RP, NE])
        need = sb("need", [RP, NE])
        ok = sb("ok", [RP, NE])
        ones = sb("ones", [RP, RP])
        lower = sb("lower", [RP, RP])
        ident = t["ident"]
        now = sb("now", [RP, 8], I32)
        xin = sb("xin", [RP, 8, D])
        ps = ctx.enter_context(nc.psum_tensor("r_ps", [128, 8, 512], F32))

        loaded = sem("loaded")
        chain = sem("chain")
        bit_chain = sem("bit_chain")
        counted = sem("counted")
        summed = sem("summed")
        maxed = sem("maxed")
        expd = sem("expd")
        masked = sem("masked")
        ranked = sem("ranked")
        placed = sem("placed")
        slots_turned = sem("slots_turned")
        slots_copied = sem("slots_copied")
        stored = sem("stored")
        x_loaded = [sem(f"x_loaded{i}") for i in range(8)]
        x_sent = [sem(f"x_sent{i}") for i in range(8)]
        picked = sem("picked")
        block = ctx.enter_context(nc.Block())

        @block.sync
        def _(sp):
            for dst, src in ((lg[:, :, :], t["lg"].rearrange("(q p) e -> p q e", p=RP)),
                             (ones[:, :], a["const_ones"]), (lower[:, :], a["const_before"]), (rank_w[:, :], a["const_rank"]),
                             (base_w[:, :], a["const_base"]), (own[:, :], a["const_own"])):
                sp.dma_start(dst, src).then_inc(loaded, 16)
            rows = t["ys"][SLOTS:SLOTS + TOK, :].rearrange("(g p) d -> g p d", p=RP)
            for i in range(8):
                sp.dma_start(xin[:, i, :], rows[i]).then_inc(x_loaded[i], 16)
            sp.wait_ge(slots_copied, 1)
            sp.dma_start(t["slot"].rearrange("(q p) o -> q (p o)", p=RP), slot_ti[:, :]).then_inc(stored, 16)
            sp.dma_start(t["pm"].rearrange("(q p) o -> q (p o)", p=RP), pm_t[:, :]).then_inc(stored, 16)
            with sp.Fori(1, RQ // 8) as n:
                for i in range(8):
                    sp.wait_ge(x_sent[i], 16 * n)
                    sp.sem_inc(t["held"], 1)
                    sp.dma_start(xin[:, i, :], t["ys"][bass.ds(n * (8 * RP) + (SLOTS + i * RP), RP), :]).then_inc(x_loaded[i], 16)
            sp.wait_ge(stored, 32)

        @block.gpsimd
        def _(pool):
            pool.wait_ge(placed, 1)
            def send(n):
                pool.tensor_copy(now[:, :], slot_i[:, bass.ds(n * 8, 8)]).then_inc(picked, 1)
                pool.wait_ge(picked, n + 1)
                for i in range(8):
                    pool.wait_ge(x_loaded[i], n * 16 + 16)
                    pool.sem_inc(t["held"], 1)
                    pool.indirect_dma_start(t["xs"], bass.IndirectOffsetOnAxis(ap=now[:, i:i + 1], axis=0), xin[:, i, :], None
                                            ).then_inc(x_sent[i], 16)

            send(0)
            with pool.Fori(1, RQ // 8) as n:
                for i in range(8):
                    pool.wait_ge(x_sent[i], n * 16)
                pool.sem_inc(t["held"], 1)
                send(n)
            for i in range(8):
                pool.wait_ge(x_sent[i], 16 * (RQ // 8))

        @block.scalar
        def _(act):
            act.wait_ge(maxed, 1)
            act.activation(e[:, :, :], eq[:, :, :], ACT.Exp).then_inc(expd, 1)

        @block.vector
        def _(dve):
            done = [0]

            def link(ins):
                done[0] += 1
                ins.then_inc(chain, 1)
                dve.wait_ge(chain, done[0])

            def by_expert(v):
                return v.unsqueeze(1).to_broadcast([RP, NE, RQ])

            def by_token(v):
                return v.unsqueeze(2).to_broadcast([RP, NE, RQ])

            def sum_e(out, src, op=ALU.add):
                link(dve.tensor_reduce(out, src.rearrange("p e q -> p q e"), AX_X, op))

            dve.wait_ge(loaded, 16 * 6)
            link(dve.memset(ones_row[:, :], 1.0))
            link(dve.memset(thr[:, :], 0.0))
            link(dve.memset(step[:, :], 1.0))
            link(dve.tensor_reduce(mx[:, :], lg[:, :, :], AX_X, ALU.max))
            dve.tensor_tensor(eq[:, :, :], lg[:, :, :].rearrange("p q e -> p e q"), by_expert(mx[:, :]), ALU.subtract).then_inc(maxed, 1)
            dve.wait_ge(expd, 1)
            sum_e(sm[:, :], e[:, :, :])
            link(dve.reciprocal(mx[:, :], sm[:, :]))
            link(dve.tensor_tensor(e[:, :, :], e[:, :, :], by_expert(mx[:, :]), ALU.mult))
            sum_e(pm[:, :], e[:, :, :], ALU.max)
            link(dve.tensor_tensor(eq[:, :, :], e[:, :, :], by_expert(pm[:, :]), ALU.is_equal))
            link(dve.tensor_tensor(eq[:, :, :], eq[:, :, :], by_token(rank_w[:, :]), ALU.mult))
            sum_e(sm[:, :], eq[:, :, :], ALU.max)
            link(dve.tensor_tensor(eq[:, :, :], by_expert(sm[:, :]), by_token(rank_w[:, :]), ALU.is_equal))
            link(dve.tensor_scalar(hit[:, :, :], eq[:, :, :], 1.0, None, ALU.subtract))
            link(dve.tensor_tensor(key[:, :, :], eq[:, :, :], by_expert(pm[:, :]), ALU.mult))
            link(dve.tensor_tensor(key[:, :, :], key[:, :, :], hit[:, :, :], ALU.add))

            def reach(op, bound, ordered):
                ordered(dve.tensor_tensor(hit[:, :, :], key[:, :, :], by_token(bound), op))
                dve.tensor_reduce(cnt[:, :], hit[:, :, :], AX_X, ALU.add).then_inc(counted, 1)

            with dve.Fori(0, BITS) as b:
                bit = Chain(dve, bit_chain, b, 5)
                bit(dve.tensor_scalar(trial[:, :], thr[:, :], step[:, 0:1], None, ALU.add))
                reach(ALU.is_ge, trial[:, :], bit)
                dve.wait_ge(summed, b + 1)
                bit(dve.tensor_scalar(ok[:, :], ps[0:RP, 0, 0:NE], float(CAP), step[:, 0:1], ALU.is_ge, ALU.mult))
                bit(dve.tensor_tensor(thr[:, :], thr[:, :], ok[:, :], ALU.add))
                bit(dve.tensor_scalar(step[:, :], step[:, :], 0.5, None, ALU.mult))
                bit.end()
            reach(ALU.is_gt, thr[:, :], link)
            dve.wait_ge(summed, BITS + 1)
            link(dve.tensor_scalar(need[:, :], ps[0:RP, 0, 0:NE], -1.0, float(CAP), ALU.mult, ALU.add))
            link(dve.tensor_copy(kept[:, :, :], hit[:, :, :]))

            def rank(n):
                dve.wait_ge(ranked, n + 1)
                link(dve.tensor_copy(totals[:, :, :], ps[0:RP, 4:6, :].rearrange("p b (e q) -> p (b e) q", q=RQ)))
                for x in range(NE):
                    link(dve.tensor_tensor_scan(before[:, x, :], ones_row[:, :], totals[:, x, :], 0.0, ALU.mult, ALU.add))
                link(dve.tensor_tensor(before[:, :, :], before[:, :, :], totals[:, :, :], ALU.subtract))
                link(dve.tensor_tensor(before[:, :, :], before[:, :, :], ps[0:RP, 2:4, :].rearrange("p b (e q) -> p (b e) q", q=RQ), ALU.add))

            link(dve.tensor_tensor(hit[:, :, :], key[:, :, :], by_token(thr[:, :]), ALU.is_equal))
            dve.sem_inc(masked, 1)
            rank(0)
            link(dve.tensor_tensor(before[:, :, :], before[:, :, :], by_token(need[:, :]), ALU.is_lt))
            link(dve.tensor_tensor(hit[:, :, :], hit[:, :, :], before[:, :, :], ALU.mult))
            link(dve.tensor_tensor(hit[:, :, :], hit[:, :, :], kept[:, :, :], ALU.add))
            dve.sem_inc(masked, 1)
            rank(1)
            link(dve.tensor_tensor(before[:, :, :], before[:, :, :], by_token(base_w[:, :]), ALU.add))
            link(dve.tensor_tensor(before[:, :, :], before[:, :, :], hit[:, :, :], ALU.mult))
            sum_e(slot[:, :], before[:, :, :])
            sum_e(has[:, :], hit[:, :, :])
            link(dve.tensor_scalar(has[:, :], has[:, :], -1.0, 1.0, ALU.mult, ALU.add))
            link(dve.tensor_tensor(has[:, :], has[:, :], own[:, :], ALU.mult))
            link(dve.tensor_tensor(slot[:, :], slot[:, :], has[:, :], ALU.add))
            dve.tensor_copy(slot_i[:, :], slot[:, :]).then_inc(placed, 1)
            dve.wait_ge(slots_turned, 1)
            dve.tensor_copy(slot_ti[:, :], ps[0:RQ, 1, 0:RP])
            dve.tensor_copy(pm_t[:, :], ps[0:RQ, 1, RP:2 * RP]).then_inc(slots_copied, 1)

        @block.tensor
        def _(pe):
            pe.wait_ge(loaded, 16 * 6)
            with pe.Fori(0, BITS + 1) as b:
                pe.wait_ge(counted, b + 1)
                pe.matmul(ps[0:RP, 0, 0:NE], ones[:, :], cnt[:, :], start=True, stop=True).then_inc(summed, 1)
            for n in range(2):
                pe.wait_ge(masked, n + 1)
                for half in range(2):
                    src = hit[:, 4 * half:4 * half + 4, :].rearrange("p e q -> p (e q)")
                    pe.matmul(ps[0:RP, 2 + half, :], lower[:, :], src, start=True, stop=True)
                    last = pe.matmul(ps[0:RP, 4 + half, :], ones[:, :], src, start=True, stop=True)
                last.then_inc(ranked, 1)
            pe.wait_ge(placed, 1)
            pe.transpose(ps[0:RQ, 1, 0:RP], slot[:, :], ident[0:RP, 0:RP])
            pe.transpose(ps[0:RQ, 1, RP:2 * RP], pm[:, :], ident[0:RP, 0:RP]).then_inc(slots_turned, 1)


CT = CAP // 4
CQ = CT // RP


class Place:

    def __init__(self, i, k):
        self.i, self.k = i, k
        self.n, self.e, self.par, self.epar = i * 8 + k, i * 2 + k // 4, k % 2, k // 4 % 2
        self.turn, self.eturn = i * 4 + k // 2, i + k // 8

    def __add__(self, d):
        return Place(self.i, self.k + d)

    def __sub__(self, d):
        return Place(self.i, self.k - d)


def phase_experts(nc, a, t):
    with ExitStack() as ctx:
        def sb(name, shape, dt=F32):
            return ctx.enter_context(nc.sbuf_tensor("e_" + name, shape, dt))

        def sem(name):
            return semaphore(nc, t, "e_" + name)

        ident = t["ident"]
        w1_raw = sb("w1_raw", [128, 3, FF])
        w2_raw = sb("w2_raw", [128, FC, D])
        w1_hi = sb("w1_hi", [128, 2, 3, FF], F32R)
        w1_lo = sb("w1_lo", [128, 2, 2, FF], F32R)
        w2_hi = sb("w2_hi", [128, 2, FC, D], F32R)
        w2_lo = sb("w2_lo", [128, 2, FC, D], F32R)
        b1 = sb("b1", [128, 2, FC])
        b2 = sb("b2", [RP, 2, D])
        xin = sb("xin", [RP, 2, CQ, D])
        xs = sb("xs", [RP, 2, CQ, 2 * D], F32R)
        xt = sb("xt", [128, 3, CT], F32R)
        ht = sb("ht", [128, FC, CT])
        ht_hi = sb("ht_hi", [128, 2, FC, CT], F32R)
        ht_lo = sb("ht_lo", [128, 2, FC, CT], F32R)
        y = sb("y", [RP, 2, CQ, D])
        ps = ctx.enter_context(nc.psum_tensor("e_ps", [128, 8, 512], F32))

        x_loaded = [Dmas(sem(f"x_loaded{i}"), 1) for i in range(2)]
        w1_loaded = [Dmas(sem(f"w1_loaded{i}"), 5) for i in range(2)]
        w2_loaded = [Dmas(sem(f"w2_loaded{i}"), 2) for i in range(2)]
        stored = [Dmas(sem(f"stored{i}"), 1) for i in range(2)]
        w1_masked = Count(sem("w1_masked"), 1)
        w1_split = Count(sem("w1_split"), 1)
        w2_masked = Count(sem("w2_masked"), 1)
        w2_split = Count(sem("w2_split"), 1)
        x_masked = Count(sem("x_masked"), 1)
        x_split = Count(sem("x_split"), 1)
        x_turned = Count(sem("x_turned"), 3)
        x_copied_a = Count(sem("x_copied_a"), 2)
        x_copied_v = Count(sem("x_copied_v"), 1)
        up_made = Count(sem("up_made"), FC)
        gelu_done = Count(sem("gelu_done"), FC)
        h_masked = Count(sem("h_masked"), FC)
        h_split = Count(sem("h_split"), FC)
        down_made = Count(sem("down_made"), 3)
        y_ready = Count(sem("y_ready"), 3)
        stores_done = Count(sem("stores_done"), 1)
        PASSES = NE // 2
        FIRST, END = Place(0, 0), 8 * PASSES
        block = ctx.enter_context(nc.Block())

        def chunks(eng, body):
            with eng.Fori(0, PASSES - 1) as i:
                for k in range(8):
                    body(Place(i, k), 8)
            for k in range(8):
                body(Place(PASSES - 1, k), 7 - k)

        @block.sync
        def _(sp):
            sp.sem_inc(stores_done.sem, 2)

            def load_weights(c):
                p = c.epar
                w = a["L0_ffn_w1"].rearrange("e k n -> k e n")
                for rows, blk, to in ((0, 0, slice(0, 128)), (128, 1, slice(0, 64)), (0, 1, slice(64, 128)), (64, 2, slice(0, 128))):
                    sp.dma_start(w1_raw[to, blk, :].unsqueeze(1), w[rows:rows + to.stop - to.start, bass.ds(c.e, 1), :]).then_inc(w1_loaded[p].sem, 16)
                sp.dma_start(b1[:, p, :].unsqueeze(1), a["L0_ffn_b1"].rearrange("e (c p) -> p e c", p=128)[:, bass.ds(c.e, 1), :],
                             allow_slow_non_contiguous=True).then_inc(w1_loaded[p].sem, 16)
                sp.dma_start(w2_raw[:, :, :].unsqueeze(1), a["L0_ffn_w2"].rearrange("e (c p) n -> p e c n", p=128)[:, bass.ds(c.e, 1), :, :]
                             ).then_inc(w2_loaded[p].sem, 16)
                sp.dma_start(b2[:, p, :].unsqueeze(1), a["L0_ffn_b2"][bass.ds(c.e, 1), :].partition_broadcast(RP)).then_inc(w2_loaded[p].sem, 16)

            def load(c):
                rows = t["xs"][bass.ds(c.n * CT, CT), :].rearrange("(q p) d -> p q d", p=RP)
                sp.dma_start(xin[:, c.par, :, :], rows).then_inc(x_loaded[c.par].sem, 16)

            def body(c, more):
                if c.k % 4 == 0 and more > 4:
                    sp.wait_ge(w1_split.sem, w1_split.now(c.e))
                    sp.sem_inc(t["held"], 1)
                    sp.wait_ge(w2_split.sem, w2_split.now(c.e))
                    sp.sem_inc(t["held"], 1)
                    sp.wait_ge(y_ready.sem, y_ready.last(c.n))
                    sp.sem_inc(t["held"], 1)
                    load_weights(c + 4)
                if more >= 2:
                    sp.wait_ge(x_turned.sem, x_turned.now(c.n))
                    sp.sem_inc(t["held"], 1)
                    load(c + 2)
                sp.wait_ge(y_ready.sem, y_ready.now(c.n))
                sp.sem_inc(t["held"], 1)
                sp.dma_start(t["ys"][bass.ds(c.n * CT, CT), :].rearrange("(q p) d -> p q d", p=RP), y[:, c.par, :, :]).then_inc(stored[c.par].sem, 16)
                sp.wait_ge(stored[c.par].sem, stored[c.par].now(c.turn))
                sp.sem_inc(stores_done.sem, 1)

            load(FIRST)
            load_weights(FIRST)
            load(FIRST + 1)
            chunks(sp, body)

        @block.gpsimd
        def _(pool):
            for c in (w1_split, w2_split, h_split):
                pool.sem_inc(c.sem, c.per)

            def split_weights(c, which):
                masked, split, raw, hi, lo, n = ((w1_masked, w1_split, w1_raw, w1_hi, w1_lo, 2) if which == 1 else
                                                 (w2_masked, w2_split, w2_raw, w2_hi, w2_lo, FC))
                pool.wait_ge(masked.sem, masked.now(c.e))
                pool.sem_inc(t["held"], 1)
                pool.tensor_tensor(lo[:, c.epar, :, :], raw[:, 0:n, :], whole(hi[:, c.epar, 0:n, :]), ALU.subtract).then_inc(split.sem, 1)

            def split_hidden(c):
                for f in range(FC):
                    pool.wait_ge(h_masked.sem, h_masked.now(c.n, f + 1))
                    pool.sem_inc(t["held"], 1)
                    pool.tensor_tensor(ht_lo[:, c.par, f, :], ht[:, f, :], whole(ht_hi[:, c.par, f, :]), ALU.subtract).then_inc(h_split.sem, 1)

            def body(c, more):
                if c.k % 4 == 1 and more > 3:
                    split_weights(c + 3, 1)
                if c.k % 4 == 2 and more > 2:
                    split_weights(c + 2, 2)
                if more >= 1:
                    split_hidden(c + 1)

            split_weights(FIRST, 1)
            split_weights(FIRST, 2)
            split_hidden(FIRST)
            chunks(pool, body)

        @block.scalar
        def _(act):
            for c in (x_copied_a, gelu_done):
                act.sem_inc(c.sem, c.per)

            def hidden(c):
                for n in (0, 2):
                    act.wait_ge(x_turned.sem, x_turned.now(c.n, n + 1))
                    act.copy(xt[:, n, :], ps[:, n, 0:CT]).then_inc(x_copied_a.sem, 1)
                act.wait_ge(w1_loaded[c.epar].sem, w1_loaded[c.epar].now(c.eturn))
                for f in range(FC):
                    act.wait_ge(up_made.sem, up_made.now(c.n, f + 1))
                    act.wait_ge(h_split.sem, h_split.last(c.n, f + 1))
                    act.sem_inc(t["held"], 1)
                    act.activation(ht[:, f, :], ps[:, 3 + f % 2, 0:CT], ACT.Gelu, bias=b1[:, c.epar, f:f + 1]).then_inc(gelu_done.sem, 1)

            def body(c, more):
                if more >= 1:
                    hidden(c + 1)

            hidden(FIRST)
            chunks(act, body)

        @block.vector
        def _(dve):
            for c in (w1_masked, w2_masked, x_masked, x_split, x_copied_v, h_masked, y_ready):
                dve.sem_inc(c.sem, c.per)

            def mask_weights(c, which):
                loaded, masked, hi, raw = (w1_loaded, w1_masked, w1_hi, w1_raw) if which == 1 else (w2_loaded, w2_masked, w2_hi, w2_raw)
                dve.wait_ge(loaded[c.epar].sem, loaded[c.epar].now(c.eturn))
                dve.tensor_copy(hi[:, c.epar, :, :], raw[:, :, :]).then_inc(masked.sem, 1)

            def split_x(c):
                dve.wait_ge(x_loaded[c.par].sem, x_loaded[c.par].now(c.turn))
                dve.tensor_copy(xs[:, c.par, :, 0:D], xin[:, c.par, :, :]).then_inc(x_masked.sem, 1)
                dve.wait_ge(x_masked.sem, x_masked.now(c.n))
                dve.tensor_tensor(xs[:, c.par, :, D:2 * D], xin[:, c.par, :, :], whole(xs[:, c.par, :, 0:D]), ALU.subtract).then_inc(x_split.sem, 1)

            def hidden(c):
                dve.wait_ge(x_turned.sem, x_turned.now(c.n, 2))
                dve.tensor_copy(xt[:, 1, :], ps[:, 1, 0:CT]).then_inc(x_copied_v.sem, 1)
                for f in range(FC):
                    dve.wait_ge(gelu_done.sem, gelu_done.now(c.n, f + 1))
                    dve.tensor_copy(ht_hi[:, c.par, f, :], ht[:, f, :]).then_inc(h_masked.sem, 1)

            def body(c, more):
                if more >= 1:
                    hidden(c + 1)
                if more >= 2:
                    split_x(c + 2)
                dve.wait_ge(stores_done.sem, c.n + 1)
                for b in range(3):
                    n = min(2, CQ - 2 * b)
                    dve.wait_ge(down_made.sem, down_made.now(c.n, b + 1))
                    dve.tensor_tensor(y[:, c.par, 2 * b:2 * b + n, :], ps[0:RP, 5 + b, 0:n * D].rearrange("p (q d) -> p q d", q=n),
                                      b2[:, c.epar, :].unsqueeze(1).to_broadcast([RP, n, D]), ALU.add).then_inc(y_ready.sem, 1)
                if c.k % 4 == 0 and more > 4:
                    mask_weights(c + 4, 1)
                if c.k % 4 == 1 and more > 3:
                    mask_weights(c + 3, 2)

            split_x(FIRST)
            mask_weights(FIRST, 1)
            mask_weights(FIRST, 2)
            split_x(FIRST + 1)
            hidden(FIRST)
            chunks(dve, body)

        @block.tensor
        def _(pe):
            for c in (x_turned, up_made, down_made):
                pe.sem_inc(c.sem, c.per)

            def hidden(c):
                pe.wait_ge(x_split.sem, x_split.now(c.n))
                for n in range(3):
                    for q in range(CQ):
                        last = pe.transpose(parts(ps[:, n, q * RP:(q + 1) * RP]), xs[:, c.par, q, n * 128:(n + 1) * 128], t["ident_r"][0:RP, 0:RP])
                    last.then_inc(x_turned.sem, 1)
                pe.wait_ge(w1_split.sem, w1_split.now(c.e))
                pe.wait_ge(x_copied_a.sem, x_copied_a.now(c.n))
                pe.wait_ge(x_copied_v.sem, x_copied_v.now(c.n))
                for f in range(FC):
                    pe.wait_ge(gelu_done.sem, gelu_done.now(c.n, f - 1) if f >= 2 else gelu_done.last(c.n, FC - 1 + f))
                    width_product(pe, ps[:, 3 + f % 2, 0:CT], (w1_hi[:, c.epar], w1_lo[:, c.epar]), slice(f * 128, (f + 1) * 128),
                                  lambda block, rows: xt[0:rows, block, :], False).then_inc(up_made.sem, 1)

            def body(c, more):
                if more >= 1:
                    hidden(c + 1)
                pe.wait_ge(w2_split.sem, w2_split.now(c.e))
                pe.wait_ge(h_split.sem, h_split.now(c.n))
                for b in range(3):
                    pe.wait_ge(y_ready.sem, y_ready.last(c.n, b + 1))
                    for q in range(2 * b, min(2 * b + 2, CQ)):
                        last = hidden_product(pe, ps[0:RP, 5 + b, (q % 2) * D:(q % 2 + 1) * D], (ht_hi[:, c.par], ht_lo[:, c.par]), slice(q * RP, (q + 1) * RP),
                                              (w2_hi[:, c.epar], w2_lo[:, c.epar]), FC)
                    last.then_inc(down_made.sem, 1)

            hidden(FIRST)
            chunks(pe, body)


TC = 14
NTC = N // TC
ST = 8 * TC
SQ = 8
HB = B // 2
NB = D // 3
SF = TC * HB
TWO_PI = (6.28125, 1.9350051879882812e-03, 3.019916050561e-07)
ROUND = 1.5 * 2.0 ** 23


NCLS = 6
GT0 = [[0, 1, 0, 0, 1, 0], [0, 1, 0, 0, 0, 1], [0, 0, 1, 0, 1, 0], [0, 0, 1, 0, 0, 1], [0, 0, 0, 1, 1, 0], [0, 0, 0, 1, 0, 1]]
EXPERT_PAIRS = [[(j - 1, k - 1) for j in range(1, 6) for k in range(1, 6) if j != k and row[j] and row[k]] for row in GT0]


class Chunk:

    def __init__(self, i, k):
        self.i, self.k = i, k
        self.tc, self.buf, self.use = i * 4 + k, k % 4, i + k // 4
        self.par, self.turn = k % 2, i * 2 + k // 2

    def __add__(self, d):
        return Chunk(self.i, self.k + d)

    def __sub__(self, d):
        return Chunk(self.i, self.k - d)


def phase_states(nc, a, t, out):
    with ExitStack() as ctx:
        def sb(name, shape, dt=F32):
            return ctx.enter_context(nc.sbuf_tensor("s_" + name, shape, dt))

        def sem(name):
            return semaphore(nc, t, "s_" + name)

        ident = t["ident"]
        wt_hi = sb("wt_hi", [128, 3, 7 * NB], F32R)
        wt_lo = sb("wt_lo", [128, 2, 7 * NB], F32R)
        bias = sb("bias", [128, 7])
        h = sb("h", [ST, 4, SQ, D])
        slot = sb("slot", [ST, 4, SQ], I32)
        pm = sb("pm", [ST, 4, SQ])
        y = sb("y", [ST, 2, SQ, D])
        nf = sb("nf", [ST, SQ, D])
        xn = sb("xn", [ST, SQ, 2 * D], F32R)
        stats = sb("stats", [ST, SQ, 6])
        mv = sb("mv", [ST, SQ, 2])
        std = sb("std", [ST, SQ])
        rstd = sb("rstd", [ST, SQ])
        xt = sb("xt", [128, 3, 2, SF], F32R)
        eps = sb("eps", [128, 1])
        biv = sb("biv", [128, 3, SF])
        sq = sb("sq", [128, 3, SF])
        k = sb("k", [128, 3, SF])
        sk = sb("sk", [128, 3, SF])
        dec = sb("dec", [128, SF])
        th = sb("th", [128, SF])
        ang = sb("ang", [128, SF])
        rnd = sb("rnd", [128, SF])
        sn = sb("sn", [128, SF])
        sh = sb("sh", [128, SF])
        om = sb("om", [128, SF])
        a0 = ang
        mat = sb("mat", [128, TC, 9, HB])
        raw = mat[:, :, :, :].rearrange("p t m b -> p (t m b)")
        w1_raw = raw[:, 0:3 * FF].rearrange("p (k n) -> p k n", k=3)
        wt_raw = raw[:, 3 * FF:3 * FF + 21 * NB].rearrange("p (k n) -> p k n", k=3)
        u = sb("u", [128, 2, TC, 3, HB])
        prod = sb("prod", [128, 3, 3, HB])
        sum0 = sb("sum0", [128, 3, HB])
        sum1 = sb("sum1", [128, 3, HB])
        state = sb("state", [128, 2, TC, 3, HB])
        state2 = sb("state2", [128, 3, HB, TC])
        qk = state2[:, :, :, :].rearrange("p c b t -> p c (b t)")
        w1_hi = sb("w1_hi", [128, 3, FF], F32R)
        w1_lo = sb("w1_lo", [128, 2, FF], F32R)
        w2 = sb("w2", [128, FC, D])
        b1 = sb("b1", [128, FC])
        b2 = sb("b2", [ST, D])
        mv2 = sb("mv2", [ST, SQ, 2])
        std2 = sb("std2", [ST, SQ])
        rstd2 = sb("rstd2", [ST, SQ])
        zn = sb("zn", [ST, SQ, 2 * D], F32R)
        zt = sb("zt", [128, 3, 4 * ST], F32R)
        ht = sb("ht", [128, FC, 4 * ST])
        wrow = ht[0:NB, :, :].rearrange("p f n -> p (f n)").rearrange("p (c d) -> p c d", c=7)
        o = sb("o", [ST, SQ, D])
        ps = ctx.enter_context(nc.psum_tensor("s_ps", [128, 8, 512], F32))

        w_loaded = sem("w_loaded")
        W_LOADS = 2 * 7 + 5 + 4 + 3
        w_turned = sem("w_turned")
        w_copied = sem("w_copied")
        w_ready = sem("w_ready")
        h_loaded = [Dmas(sem(f"h_loaded{i}"), SQ) for i in range(4)]
        s_loaded = [Dmas(sem(f"s_loaded{i}"), 2 * SQ) for i in range(4)]
        y_loaded = [Dmas(sem(f"y_loaded{i}"), SQ) for i in range(2)]
        stored = Dmas(sem("stored"), SQ)
        h3_stored = sem("h3_stored")
        weighted = Count(sem("weighted"), 1)
        h2_ready = Count(sem("h2_ready"), 1)
        var_ready = Count(sem("var_ready"), 1)
        std_ready = Count(sem("std_ready"), 1)
        xn_ready = Count(sem("xn_ready"), 1)
        x_turned = Count(sem("x_turned"), 6)
        x_copied_a = Count(sem("x_copied_a"), 3)
        x_copied_v = Count(sem("x_copied_v"), 3)
        made = Count(sem("made"), 8)
        made_copied = Count(sem("made_copied"), 8)
        squared = Count(sem("squared"), 1)
        norm2_ready = Count(sem("norm2_ready"), 1)
        theta_ready = Count(sem("theta_ready"), 1)
        angle_ready = Count(sem("angle_ready"), 1)
        sines_ready = Count(sem("sines_ready"), 1)
        scanned = Count(sem("scanned"), 1)
        state_sorted = Count(sem("state_sorted"), 1)
        state_turned = Count(sem("state_turned"), 4)
        h3_ready = Count(sem("h3_ready"), 1)
        var2_ready = Count(sem("var2_ready"), 1)
        std2_ready = Count(sem("std2_ready"), 1)
        z_masked = Count(sem("z_masked"), 1)
        zn_ready = Count(sem("zn_ready"), 1)
        biased = Count(sem("biased"), 1)
        STEPS = [("turn", 0, c) for c in range(3)] + [("up", 0, f) for f in range(FC)]
        STEPS += [("turn", 1, c) for c in range(3)] + [("down", 0, b) for b in range(2)]
        STEPS += [("up", 1, f) for f in range(FC)] + [("down", 1, b) for b in range(2)]
        NS = len(STEPS)
        ffn_made = Count(sem("ffn_made"), NS)
        ffn_copied = Count(sem("ffn_copied"), NS)
        out_ready = Count(sem("out_ready"), 1)
        stores_done = Count(sem("stores_done"), 1)
        front_chain = sem("front_chain")
        elem_chain = sem("elem_chain")
        scan_chain = sem("scan_chain")
        norm_chain = sem("norm_chain")
        FRONT, ELEM = 4, 16

        def tile_rows(array, g, c):
            v = array.rearrange("(g b n) d -> g b n d", g=SQ, n=N)[g]
            return v[:, bass.ds(c.tc * TC, TC), :]

        def chunks(eng, body):
            body(Chunk(0, 0))
            body(Chunk(0, 1))
            with eng.Fori(0, (NTC - 2) // 4) as i:
                for j in range(4):
                    body(Chunk(i, 2 + j))

        def chunks_ahead(eng, body, more):
            body(Chunk(0, 0), NTC - 1)
            body(Chunk(0, 1), NTC - 2)
            with eng.Fori(0, (NTC - 2) // 4 - 1) as i:
                for j in range(4):
                    body(Chunk(i, 2 + j), more)
            for n in range(NTC - 4, NTC):
                body(Chunk(0, n), NTC - 1 - n)

        def behind(c, d):
            return not isinstance(c.tc, int) or c.tc >= d

        LAST = Chunk(0, NTC - 1)
        block = ctx.enter_context(nc.Block())

        @block.sync
        def _(sp):
            wb = a["L1_attn_W_biv"].rearrange("(k c) d -> c k d", c=3)
            wi = a["L1_attn_W_in"].rearrange("(k c) d -> c k d", c=3)
            for twice in range(2):
                cols = slice(twice * D, twice * D + D)
                for c in range(3):
                    sp.dma_start(wrow[:, c, cols], wb[c]).then_inc(w_loaded, 16)
                    sp.dma_start(wrow[:, 3 + c, cols], wi[c]).then_inc(w_loaded, 16)
                sp.dma_start(wrow[:, 6, cols], a["L1_attn_W_decay"].rearrange("o d -> (o d)").partition_broadcast(NB)).then_inc(w_loaded, 16)
            def places(c):
                for g in range(SQ):
                    for dst, name in ((slot, "slot"), (pm, "pm")):
                        sp.dma_start(dst[:, c.buf, g:g + 1], tile_rows(t[name], g, c)).then_inc(s_loaded[c.buf].sem, 16)

            places(Chunk(0, 0))
            places(Chunk(0, 1))
            for half in range(2):
                p = slice(half * NB, half * NB + NB)
                sp.dma_start(bias[p, 0:3], a["L1_attn_b_biv"].rearrange("(k c) -> k c", c=3)).then_inc(w_loaded, 16)
                sp.dma_start(bias[p, 3:6], a["L1_attn_b_in"].rearrange("(k c) -> k c", c=3)).then_inc(w_loaded, 16)
            sp.dma_start(bias[:, 6:7], a["L1_attn_b_decay"].partition_broadcast(128)).then_inc(w_loaded, 16)
            sp.dma_start(b1[:, :], a["L1_ffn_moe0_b1"].rearrange("(c p) -> p c", p=128), allow_slow_non_contiguous=True).then_inc(w_loaded, 16)
            load_blocks(sp, w1_raw, a["L1_ffn_moe0_W1"], w_loaded)
            for dst, src in ((w2[:, :, :], a["L1_ffn_moe0_W2"].rearrange("(c p) n -> p c n", p=128)),
                             (b2[:, :], a["L1_ffn_moe0_b2"].partition_broadcast(ST))):
                sp.dma_start(dst, src).then_inc(w_loaded, 16)
            sp.sem_inc(stores_done.sem, 1)

            def load(c):
                for g in range(SQ):
                    sp.dma_start(h[:, c.buf, g, :], tile_rows(t["h1"], g, c)).then_inc(h_loaded[c.buf].sem, 16)

            def body(c, more):
                if more >= 4:
                    sp.wait_ge(h2_ready.sem, h2_ready.now(c.tc))
                    sp.sem_inc(t["held"], 1)
                    places(c + 4)
                if not behind(c, 1):
                    sp.wait_ge(h3_ready.sem, h3_ready.now(0))
                    for g in range(SQ):
                        sp.dma_start(tile_rows(t["h3"], g, c), h[:, 0, g, :]).then_inc(h3_stored, 16)
                sp.wait_ge(out_ready.sem, out_ready.now(c.tc))
                sp.sem_inc(t["held"], 1)
                for g in range(SQ):
                    sp.dma_start(tile_rows(out, g, c), o[:, g, :]).then_inc(stored.sem, 16)
                if more >= 4:
                    load(c + 4)
                sp.wait_ge(stored.sem, stored.now(c.tc))
                sp.sem_inc(stores_done.sem, 1)

            for n in range(2):
                load(Chunk(0, n))
            for n in range(2, 4):
                places(Chunk(0, n))
                load(Chunk(0, n))
            chunks_ahead(sp, body, 4)
            sp.wait_ge(h3_stored, 16 * SQ)

        @block.gpsimd
        def _(pool):
            for c in (weighted, h2_ready, zn_ready, biased, out_ready):
                pool.sem_inc(c.sem, c.per)
            pool.wait_ge(w_loaded, 16 * W_LOADS)

            def gather(c):
                pool.wait_ge(s_loaded[c.buf].sem, s_loaded[c.buf].now(c.use))
                pool.sem_inc(t["held"], 1)
                for g in range(SQ):
                    pool.indirect_dma_start(y[:, c.par, g, :], None, t["ys"], bass.IndirectOffsetOnAxis(ap=slot[:, c.buf, g:g + 1], axis=0)
                                            ).then_inc(y_loaded[c.par].sem, 16)

            def residual(c):
                pool.wait_ge(y_loaded[c.par].sem, y_loaded[c.par].now(c.turn))
                pool.sem_inc(t["held"], 1)
                for g in range(SQ):
                    last = pool.tensor_tensor(y[:, c.par, g, :], y[:, c.par, g, :], pm[:, c.buf, g:g + 1].to_broadcast([ST, D]), ALU.mult)
                last.then_inc(weighted.sem, 1)
                pool.wait_ge(weighted.sem, weighted.now(c.tc))
                pool.wait_ge(h_loaded[c.buf].sem, h_loaded[c.buf].now(c.use))
                pool.sem_inc(t["held"], 1)
                for g in range(SQ):
                    last = pool.tensor_tensor(h[:, c.buf, g, :], h[:, c.buf, g, :], y[:, c.par, g, :], ALU.add)
                last.then_inc(h2_ready.sem, 1)
                pool.wait_ge(h2_ready.sem, h2_ready.now(c.tc))
                pool.sem_inc(t["held"], 1)

            def norm2(c):
                pool.wait_ge(z_masked.sem, z_masked.now(c.tc))
                pool.sem_inc(t["held"], 1)
                pool.tensor_tensor(zn[:, :, D:2 * D], nf[:, :, :], whole(zn[:, :, 0:D]), ALU.subtract).then_inc(zn_ready.sem, 1)
                if not behind(c, 1):
                    pool.wait_ge(h3_stored, 16 * SQ)
                for g in range(SQ):
                    last = pool.tensor_tensor(h[:, c.buf, g, :], h[:, c.buf, g, :], b2[:, :], ALU.add)
                last.then_inc(biased.sem, 1)

            def finish(c):
                pool.wait_ge(biased.sem, biased.now(c.tc))
                for half in range(2):
                    at = STEPS.index(("down", half, 1)) + 1
                    pool.wait_ge(ffn_copied.sem, ffn_copied.now(c.tc, at))
                    pool.sem_inc(t["held"], 1)
                    last = pool.tensor_tensor(o[:, 4 * half:4 * half + 4, :], o[:, 4 * half:4 * half + 4, :],
                                              h[:, c.buf, 4 * half:4 * half + 4, :], ALU.add)
                last.then_inc(out_ready.sem, 1)

            def body(c, more):
                if more >= 1:
                    residual(c + 1)
                if more >= 2:
                    gather(c + 2)
                if behind(c, 1):
                    norm2(c - 1)
                if behind(c, 2):
                    finish(c - 2)

            gather(Chunk(0, 0))
            gather(Chunk(0, 1))
            residual(Chunk(0, 0))
            chunks_ahead(pool, body, 4)
            norm2(LAST)
            finish(LAST - 1)
            finish(LAST)

        @block.scalar
        def _(act):
            for c in (std_ready, x_copied_a, made_copied, squared, theta_ready, sines_ready, state_sorted, std2_ready, ffn_copied):
                act.sem_inc(c.sem, c.per)
            act.wait_ge(w_ready, 1)

            def sort_states(c):
                act.wait_ge(scanned.sem, scanned.now(c.tc))
                act.copy(state2[:, :, :, :], state[:, c.par, :, :, :].rearrange("p t c b -> p c b t")).then_inc(state_sorted.sem, 1)

            def ffn(c, steps):
                for s in steps:
                    kind, half, n = STEPS[s]
                    act.wait_ge(ffn_made.sem, ffn_made.now(c.tc, s + 1))
                    src = ps[:, 4 + s % 4, 0:4 * ST]
                    if kind == "turn":
                        last = act.copy(zt[:, n, :], src)
                    elif kind == "up":
                        last = act.activation(ht[:, n, :], src, ACT.Gelu, bias=b1[:, n:n + 1])
                    else:
                        if half == 0 and n == 0:
                            act.wait_ge(stores_done.sem, stores_done.last(c.tc))
                            act.sem_inc(t["held"], 1)
                        g = 4 * half + 2 * n
                        last = act.copy(o[:, g:g + 2, :], ps[0:ST, 4 + s % 4, 0:2 * D].rearrange("p (g d) -> p g d", g=2))
                    last.then_inc(ffn_copied.sem, 1)

            def root2(c):
                act.wait_ge(var2_ready.sem, var2_ready.now(c.tc))
                act.activation(std2[:, :], mv2[:, :, 1], ACT.Sqrt, bias=eps[0:ST, :]).then_inc(std2_ready.sem, 1)

            def root(c):
                act.wait_ge(var_ready.sem, var_ready.now(c.tc))
                act.activation(std[:, :], mv[:, :, 1], ACT.Sqrt, bias=eps[0:ST, :]).then_inc(std_ready.sem, 1)

            def body(c, more):
                tc = c.tc
                for s in (0, 2, 4):
                    act.wait_ge(x_turned.sem, x_turned.now(tc, s + 1))
                    act.copy(xt[:, s % 3, s // 3, :].rearrange("p (t b) -> p t b", b=HB),
                             ps[:, s % 4, 0:SF].rearrange("p (b t) -> p t b", t=TC)).then_inc(x_copied_a.sem, 1)
                for s in range(8):
                    act.wait_ge(made.sem, made.now(tc, s + 1))
                    half = s % 2
                    to = slice(half * NB, half * NB + NB)
                    for n in range(s // 2 * 2, min(s // 2 * 2 + 2, 7)):
                        at = slice(n % 2 * NB, n % 2 * NB + NB)
                        src = ps[at, s % 4, 0:SF]
                        if n < 3:
                            last = act.activation(biv[to, n, :], src, ACT.Identity, bias=bias[at, n:n + 1])
                        elif n < 6:
                            last = act.activation(u[to, c.par, :, n - 3, :], src.rearrange("p (t b) -> p t b", b=HB), ACT.Identity, bias=bias[at, n:n + 1])
                        else:
                            last = act.activation(dec[to, :], src, ACT.Sigmoid, bias=bias[at, 6:7])
                    last.then_inc(made_copied.sem, 1)
                act.wait_ge(made_copied.sem, made_copied.now(tc))
                act.activation(sq[:, :, :], biv[:, :, :], ACT.Square).then_inc(squared.sem, 1)
                if behind(c, 1):
                    sort_states(c - 1)
                act.wait_ge(norm2_ready.sem, norm2_ready.now(tc))
                act.activation(th[:, :], om[:, :], ACT.Sqrt).then_inc(theta_ready.sem, 1)
                act.wait_ge(angle_ready.sem, angle_ready.now(tc))
                act.activation(sn[:, :], ang[:, :], ACT.Sin)
                act.activation(sh[:, :], ang[:, :], ACT.Sin, scale=0.5).then_inc(sines_ready.sem, 1)
                if behind(c, 2):
                    ffn(c - 2, range(ROOT_AT))
                if behind(c, 1):
                    root2(c - 1)
                if more >= 1:
                    root(c + 1)
                if behind(c, 2):
                    ffn(c - 2, range(ROOT_AT, NS))

            ROOT_AT = NS - 2
            root(Chunk(0, 0))
            chunks_ahead(act, body, 4)
            sort_states(LAST)
            ffn(LAST - 1, range(ROOT_AT))
            root2(LAST)
            ffn(LAST - 1, range(ROOT_AT, NS))
            ffn(LAST, range(NS))

        @block.vector
        def _(dve):
            for c in (var_ready, xn_ready, x_copied_v, norm2_ready, angle_ready, scanned, h3_ready, var2_ready, z_masked):
                dve.sem_inc(c.sem, c.per)
            dve.memset(eps[:, :], EPS)
            dve.memset(state[:, 1, TC - 1, :, :], 0.0)
            for c in range(7):
                dve.wait_ge(w_turned, c + 1)
                dve.tensor_copy(wt_raw[:, :, c * NB:(c + 1) * NB], ps[:, c, 0:3 * NB].rearrange("p (k n) -> p k n", k=3)).then_inc(w_copied, 1)
            dve.wait_ge(w_loaded, 16 * W_LOADS)
            dve.wait_ge(w_copied, 7)
            dve.tensor_copy(wt_hi[:, :, :], wt_raw[:, :, :])
            dve.tensor_copy(w1_hi[:, :, :], w1_raw[:, :, :]).then_inc(w_copied, 1)
            dve.wait_ge(w_copied, 8)
            dve.tensor_tensor(wt_lo[:, :, :], wt_raw[:, 0:2, :], whole(wt_hi[:, 0:2, :]), ALU.subtract)
            dve.tensor_tensor(w1_lo[:, :, :], w1_raw[:, 0:2, :], whole(w1_hi[:, 0:2, :]), ALU.subtract).then_inc(w_ready, 1)

            def three(v):
                return v.unsqueeze(1).to_broadcast([128, 3, SF])

            def front(c):
                tc = c.tc
                link = Chain(dve, front_chain, tc, FRONT)
                dve.wait_ge(h2_ready.sem, h2_ready.now(tc))
                dve.sem_inc(t["held"], 1)
                for g in range(SQ):
                    last = dve.bn_stats(stats[:, g, :], h[:, c.buf, g, :])
                link(last)
                dve.sem_inc(t["held"], 1)
                for g in range(SQ):
                    last = dve.bn_aggr(mv[:, g, :], stats[:, g, :])
                last.then_inc(var_ready.sem, 1)
                dve.wait_ge(std_ready.sem, std_ready.now(tc))
                link(dve.reciprocal(rstd[:, :], std[:, :]))
                if behind(c, 2):
                    dve.wait_ge(zn_ready.sem, zn_ready.now(tc - 2))
                for g in range(SQ):
                    last = dve.tensor_scalar(nf[:, g, :], h[:, c.buf, g, :], mv[:, g, 0:1], rstd[:, g:g + 1], ALU.subtract, ALU.mult)
                link(last)
                link(dve.tensor_copy(xn[:, :, 0:D], nf[:, :, :]))
                dve.tensor_tensor(xn[:, :, D:2 * D], nf[:, :, :], whole(xn[:, :, 0:D]), ALU.subtract).then_inc(xn_ready.sem, 1)
                for s in (1, 3, 5):
                    dve.wait_ge(x_turned.sem, x_turned.now(tc, s + 1))
                    dve.tensor_copy(xt[:, s % 3, s // 3, :].rearrange("p (t b) -> p t b", b=HB),
                                    ps[:, s % 4, 0:SF].rearrange("p (b t) -> p t b", t=TC)).then_inc(x_copied_v.sem, 1)
                link.end()

            def norm2(c):
                link = Chain(dve, norm_chain, c.tc, 3)
                dve.wait_ge(h3_ready.sem, h3_ready.now(c.tc))
                dve.sem_inc(t["held"], 1)
                for g in range(SQ):
                    last = dve.bn_stats(stats[:, g, :], h[:, c.buf, g, :])
                link(last)
                dve.sem_inc(t["held"], 1)
                for g in range(SQ):
                    last = dve.bn_aggr(mv2[:, g, :], stats[:, g, :])
                last.then_inc(var2_ready.sem, 1)
                dve.wait_ge(std2_ready.sem, std2_ready.now(c.tc))
                link(dve.reciprocal(rstd2[:, :], std2[:, :]))
                dve.wait_ge(ffn_made.sem, ffn_made.last(c.tc, STEPS.index(("turn", 1, 2)) + 1))
                for g in range(SQ):
                    last = dve.tensor_scalar(nf[:, g, :], h[:, c.buf, g, :], mv2[:, g, 0:1], rstd2[:, g:g + 1], ALU.subtract, ALU.mult)
                link(last)
                dve.tensor_copy(zn[:, :, 0:D], nf[:, :, :]).then_inc(z_masked.sem, 1)
                link.end()

            def scan(c):
                link = Chain(dve, scan_chain, c.tc, 3 * TC)
                for s in range(TC):
                    old = state[:, c.par, s - 1, :, :] if s else state[:, 1 - c.par, TC - 1, :, :]
                    link(dve.tensor_tensor(prod[:, :, :, :].rearrange("p i j b -> p i (j b)"),
                                           mat[:, s, :, :].rearrange("p (i j) b -> p i (j b)", i=3),
                                           old.rearrange("p j b -> p (j b)").unsqueeze(1).to_broadcast([128, 3, 3 * HB]), ALU.mult))
                    dve.tensor_tensor(sum0[:, :, :], prod[:, :, 0, :], prod[:, :, 1, :], ALU.add)
                    link(dve.tensor_tensor(sum1[:, :, :], prod[:, :, 2, :], u[:, c.par, s, :, :], ALU.add))
                    link(dve.tensor_tensor(state[:, c.par, s, :, :], sum0[:, :, :], sum1[:, :, :], ALU.add))
                link.end()
                dve.sem_inc(scanned.sem, 1)

            def elem(tc):
                link = Chain(dve, elem_chain, tc, ELEM)
                dve.wait_ge(squared.sem, squared.now(tc))
                link(dve.tensor_tensor(om[:, :], sq[:, 0, :], sq[:, 1, :], ALU.add))
                dve.scalar_tensor_tensor(om[:, :], sq[:, 2, :], 1e-32, om[:, :], ALU.max, ALU.add).then_inc(norm2_ready.sem, 1)
                dve.wait_ge(theta_ready.sem, theta_ready.now(tc))
                link(dve.tensor_scalar(rnd[:, :], th[:, :], 1.0 / (2.0 * np.pi), ROUND, ALU.mult, ALU.add))
                link(dve.tensor_scalar(rnd[:, :], rnd[:, :], ROUND, None, ALU.subtract))
                src = th
                for part in TWO_PI:
                    link(dve.scalar_tensor_tensor(ang[:, :], rnd[:, :], -part, src[:, :], ALU.mult, ALU.add))
                    src = ang
                dve.tensor_scalar(ang[:, :], ang[:, :], 3.1415925, -3.1415925, ALU.min, ALU.max).then_inc(angle_ready.sem, 1)
                link(dve.tensor_scalar(th[:, :], th[:, :], 1e-8, None, ALU.max))
                link(dve.reciprocal(rnd[:, :], th[:, :]))
                dve.tensor_tensor(k[:, :, :], biv[:, :, :], three(rnd[:, :]), ALU.mult)
                dve.wait_ge(sines_ready.sem, sines_ready.now(tc))
                link(dve.scalar_tensor_tensor(om[:, :], sh[:, :], 2.0, sh[:, :], ALU.mult, ALU.mult))
                link(dve.tensor_tensor(om[:, :], om[:, :], dec[:, :], ALU.mult))
                dve.tensor_tensor(a0[:, :], dec[:, :], om[:, :], ALU.subtract)
                link(dve.tensor_tensor(sn[:, :], sn[:, :], dec[:, :], ALU.mult))
                dve.tensor_tensor(sk[:, :, :], k[:, :, :], three(sn[:, :]), ALU.mult)
                dve.wait_ge(state_turned.sem, state_turned.last(tc))
                link(dve.tensor_tensor(qk[:, :, :], k[:, :, :], three(om[:, :]), ALU.mult))

                def rows(v, n):
                    return v.rearrange("p c (t b) -> p c t b", b=HB) if n > 1 else v.rearrange("p (t b) -> p t b", b=HB)

                link(dve.tensor_tensor(sq[:, :, :], qk[:, :, :], k[:, :, :], ALU.mult))
                link(dve.tensor_tensor(mat[:, :, 0:9:4, :].rearrange("p t c b -> p c t b"), rows(sq[:, :, :], 3), rows(three(a0[:, :]), 3), ALU.add))
                dve.tensor_tensor(sq[:, 0, :], qk[:, 0, :], k[:, 1, :], ALU.mult)
                dve.tensor_tensor(sq[:, 1, :], qk[:, 0, :], k[:, 2, :], ALU.mult)
                link(dve.tensor_tensor(sq[:, 2, :], qk[:, 1, :], k[:, 2, :], ALU.mult))
                for cell, p, c, op in ((1, 0, 2, ALU.subtract), (3, 0, 2, ALU.add), (2, 1, 1, ALU.add), (6, 1, 1, ALU.subtract),
                                       (5, 2, 0, ALU.subtract), (7, 2, 0, ALU.add)):
                    last = dve.tensor_tensor(mat[:, :, cell, :], rows(sq[:, p, :], 1), rows(sk[:, c, :], 1), op)
                link(last)
                link.end()

            def add(c):
                for g in range(4):
                    dve.wait_ge(state_turned.sem, state_turned.now(c.tc, g + 1))
                    for half in range(2):
                        v = h[:, c.buf, 4 * half + g, :].rearrange("p (k c) -> p k c", c=3)
                        last = dve.tensor_tensor(v, ps[0:ST, g, 0:3 * 128].rearrange("p (c h k) -> p h k c", c=3, h=2)[:, half, :, :], v, ALU.add)
                last.then_inc(h3_ready.sem, 1)

            def body(c):
                front(c)
                if behind(c, 1):
                    scan(c - 1)
                elem(c.tc)
                if behind(c, 1):
                    add(c - 1)
                    norm2(c - 1)

            chunks(dve, body)
            scan(LAST)
            add(LAST)
            norm2(LAST)

        @block.tensor
        def _(pe):
            for c in (x_turned, made, state_turned, ffn_made):
                pe.sem_inc(c.sem, c.per)
            pe.wait_ge(w_loaded, 16 * W_LOADS)
            for c in range(7):
                for n in range(3):
                    last = pe.transpose(ps[:, c, n * NB:(n + 1) * NB], wrow[:, c, n * 128:(n + 1) * 128], ident[0:NB, 0:NB])
                last.then_inc(w_turned, 1)
            pe.wait_ge(w_copied, 7)
            pe.wait_ge(w_ready, 1)

            def turn_states(c):
                pe.wait_ge(state_sorted.sem, state_sorted.now(c.tc))
                for g in range(4):
                    for n in range(3):
                        last = pe.transpose(ps[0:ST, g, n * 128:(n + 1) * 128],
                                            state2[:, n, 8 * g:8 * g + 8, :].rearrange("p b t -> p (b t)"), ident[:, :])
                    last.then_inc(state_turned.sem, 1)

            def ffn(c):
                for s, (kind, half, n) in enumerate(STEPS):
                    need = s - 3
                    if kind == "up":
                        need = max(need, STEPS.index(("turn", half, 2)) + 1)
                    elif kind == "down":
                        need = max(need, STEPS.index(("up", half, FC - 1)) + 1)
                    if s == 0:
                        pe.wait_ge(zn_ready.sem, zn_ready.now(c.tc))
                        pe.wait_ge(ffn_copied.sem, ffn_copied.last(c.tc))
                    elif need > 0:
                        pe.wait_ge(ffn_copied.sem, ffn_copied.now(c.tc, need))
                    bank = 4 + s % 4
                    if kind == "turn":
                        for g in range(4):
                            last = pe.transpose(parts(ps[:, bank, g * ST:(g + 1) * ST]), zn[:, 4 * half + g, n * 128:(n + 1) * 128],
                                                t["ident_r"][0:ST, 0:ST])
                    elif kind == "up":
                        last = width_product(pe, ps[:, bank, 0:4 * ST], (w1_hi, w1_lo), slice(n * 128, (n + 1) * 128),
                                             lambda block, rows: zt[0:rows, block, :], False)
                    else:
                        for g in range(2):
                            at = (2 * n + g) * ST
                            for f in range(FC):
                                last = pe.matmul(ps[0:ST, bank, g * D:(g + 1) * D], ht[:, f, at:at + ST], w2[:, f, :], start=(f == 0), stop=(f == FC - 1))
                    last.then_inc(ffn_made.sem, 1)

            def body(c):
                tc = c.tc
                pe.wait_ge(xn_ready.sem, xn_ready.now(tc))
                pe.wait_ge(h3_ready.sem, h3_ready.last(tc - 1) if behind(c, 1) else h3_ready.per)
                pe.sem_inc(t["held"], 1)
                for s in range(6):
                    half, n = divmod(s, 3)
                    if s == 4:
                        pe.wait_ge(x_copied_a.sem, x_copied_a.now(tc, 1))
                    if s == 5:
                        pe.wait_ge(x_copied_v.sem, x_copied_v.now(tc, 1))
                    for g in range(4):
                        last = pe.transpose(parts(ps[:, s % 4, g * ST:(g + 1) * ST]), xn[:, 4 * half + g, n * 128:(n + 1) * 128],
                                            t["ident_r"][0:ST, 0:ST])
                    last.then_inc(x_turned.sem, 1)
                pe.wait_ge(x_copied_a.sem, x_copied_a.now(tc))
                pe.wait_ge(x_copied_v.sem, x_copied_v.now(tc))
                for s in range(8):
                    if s >= 4:
                        pe.wait_ge(made_copied.sem, made_copied.now(tc, s - 3))
                    lo, hi = s // 2 * 128, min(s // 2 * 128 + 128, 7 * NB)
                    width_product(pe, ps[0:hi - lo, s % 4, 0:SF], (wt_hi, wt_lo), slice(lo, hi),
                                  lambda block, rows: xt[0:rows, block, s % 2, :], False).then_inc(made.sem, 1)
                if behind(c, 1):
                    pe.wait_ge(made_copied.sem, made_copied.now(tc))
                    turn_states(c - 1)
                if behind(c, 2):
                    ffn(c - 2)

            chunks(pe, body)
            turn_states(LAST)
            ffn(LAST - 1)
            ffn(LAST)


def phase_first(nc, a, t, out):
    with ExitStack() as ctx:
        def sb(name, shape, dt=F32):
            return ctx.enter_context(nc.sbuf_tensor("f_" + name, shape, dt))

        def sem(name):
            return semaphore(nc, t, "f_" + name)

        NA = 5
        users = [[(i, s) for i in range(NCLS) for s in range(2) if EXPERT_PAIRS[i][s][0] == x] for x in range(NA)]
        place, n = {}, 0
        for x in range(NA):
            for key in users[x]:
                place[key] = n
                n += 1
        ident = t["ident"]
        w1 = sb("w1", [HD, NA, 2, FF])
        w2 = sb("w2", [128, NA, FC, D])
        b1 = sb("b1", [128, NA, FC])
        b2 = sb("b2", [B, NA, D])
        gw = sb("gw", [HD, NCLS, 2, 2])
        eps = sb("eps", [128, 1])
        h = sb("h", [B, NCLS, D])
        xn = sb("xn", [B, NCLS, D])
        stats = sb("stats", [B, NCLS, 6])
        mv = sb("mv", [B, NCLS, 2])
        std = sb("std", [B, NCLS])
        rstd = sb("rstd", [B, NCLS])
        xt = sb("xt", [HD, 2, NCLS * B])
        ht = sb("ht", [128, FC, 2 * NCLS * B])
        lg = sb("lg", [B, NCLS, 2])
        g = sb("g", [B, NCLS, 2])
        mask = sb("mask", [B, NCLS, 2])
        one = sb("one", [B, NCLS])
        e0 = sb("e0", [B, NCLS, 2, D])
        ps = ctx.enter_context(nc.psum_tensor("f_ps", [128, 8, 512], F32))

        loaded = sem("loaded")
        late = sem("late")
        chain = sem("chain")
        eps_set = sem("eps_set")
        var_ready = sem("var_ready")
        std_ready = sem("std_ready")
        xn_ready = sem("xn_ready")
        x_turned = sem("x_turned")
        x_copied = sem("x_copied")
        gate_made = sem("gate_made")
        gate_in = sem("gate_in")
        gate_exp = sem("gate_exp")
        up_made = sem("up_made")
        gelu_done = sem("gelu_done")
        down_made = sem("down_made")
        down_copied = sem("down_copied")
        y_ready = sem("y_ready")
        stored = sem("stored")
        block = ctx.enter_context(nc.Block())
        rows = t["h3"].rearrange("(b n) d -> b n d", n=N)[:, 0:NCLS, :]

        @block.sync
        def _(sp):
            for dst, src in ((h[:, :, :], rows),
                             (gw[:, :, 0, :], a["L1_ffn_G_W"].rearrange("i (c p) o -> c p i o", p=HD)[0]),
                             (gw[:, :, 1, :], a["L1_ffn_G_W"].rearrange("i (c p) o -> c p i o", p=HD)[1])):
                sp.dma_start(dst, src).then_inc(loaded, 16)
            for x in range(NA):
                sp.dma_start(w1[:, x, :, :], halves(a["L1_ffn_A1_W"][x])).then_inc(late, 16)
                sp.dma_start(b1[:, x, :], a["L1_ffn_A1_b"][x].rearrange("(c p) -> p c", p=128), allow_slow_non_contiguous=True).then_inc(late, 16)
                sp.dma_start(w2[:, x, :, :], a["L1_ffn_A2_W"][x].rearrange("(c p) n -> p c n", p=128)).then_inc(late, 16)
                sp.dma_start(b2[:, x, :], a["L1_ffn_A2_b"][x].partition_broadcast(B)).then_inc(late, 16)
            sp.wait_ge(y_ready, 1)
            sp.dma_start(out.rearrange("(b n) d -> b n d", n=N)[:, 0:NCLS, :], h[:, :, :]).then_inc(stored, 16)
            sp.wait_ge(stored, 16)

        @block.gpsimd
        def _(pool):
            pool.memset(eps[:, :], EPS).then_inc(eps_set, 1)

        @block.scalar
        def _(act):
            act.wait_ge(eps_set, 1)
            act.wait_ge(var_ready, 1)
            act.activation(std[:, :], mv[:, :, 1], ACT.Sqrt, bias=eps[0:B, :]).then_inc(std_ready, 1)
            act.wait_ge(gate_in, 1)
            act.activation(g[:, :, :], lg[:, :, :], ACT.Exp).then_inc(gate_exp, 1)
            act.wait_ge(late, 16 * 4 * NA)
            n = 0
            for x in range(NA):
                lo = place[users[x][0]] * B
                for f in range(FC):
                    act.wait_ge(up_made, n + 1)
                    w = len(users[x]) * B
                    act.activation(ht[:, f, lo:lo + w], ps[:, 3 + n % 2, 0:w], ACT.Gelu, bias=b1[:, x, f:f + 1]).then_inc(gelu_done, 1)
                    n += 1

        @block.vector
        def _(dve):
            done = [0]

            def link(ins):
                done[0] += 1
                ins.then_inc(chain, 1)
                dve.wait_ge(chain, done[0])

            dve.wait_ge(loaded, 16 * 3)
            for i in range(NCLS):
                last = dve.bn_stats(stats[:, i, :], h[:, i, :])
            link(last)
            for i in range(NCLS):
                last = dve.bn_aggr(mv[:, i, :], stats[:, i, :])
            last.then_inc(var_ready, 1)
            dve.wait_ge(std_ready, 1)
            link(dve.reciprocal(rstd[:, :], std[:, :]))
            for i in range(NCLS):
                last = dve.tensor_scalar(xn[:, i, :], h[:, i, :], mv[:, i, 0:1], rstd[:, i:i + 1], ALU.subtract, ALU.mult)
            last.then_inc(xn_ready, 1)
            for c in range(2):
                dve.wait_ge(x_turned, c + 1)
                dve.tensor_copy(xt[:, c, :], ps[0:HD, c, 0:NCLS * B]).then_inc(x_copied, 1)
            dve.wait_ge(gate_made, 1)
            link(dve.tensor_copy(lg[:, :, :], ps[0:B, 2, 0:2 * NCLS].rearrange("p (i o) -> p i o", o=2)))
            link(dve.tensor_reduce(one[:, :], lg[:, :, :], AX_X, ALU.max))
            dve.tensor_tensor(lg[:, :, :], lg[:, :, :], spread(one[:, :], 2), ALU.subtract).then_inc(gate_in, 1)
            dve.wait_ge(gate_exp, 1)
            link(dve.tensor_reduce(one[:, :], g[:, :, :], AX_X, ALU.add))
            link(dve.reciprocal(one[:, :], one[:, :]))
            link(dve.tensor_tensor(g[:, :, :], g[:, :, :], spread(one[:, :], 2), ALU.mult))
            link(dve.tensor_reduce(one[:, :], g[:, :, :], AX_X, ALU.min))
            link(dve.tensor_tensor(mask[:, :, :], g[:, :, :], spread(one[:, :], 2), ALU.is_gt))
            link(dve.tensor_tensor(g[:, :, :], g[:, :, :], mask[:, :, :], ALU.mult))
            link(dve.tensor_reduce(one[:, :], g[:, :, :], AX_X, ALU.add))
            link(dve.tensor_scalar(one[:, :], one[:, :], 1e-6, None, ALU.max))
            link(dve.reciprocal(one[:, :], one[:, :]))
            link(dve.tensor_tensor(g[:, :, :], g[:, :, :], spread(one[:, :], 2), ALU.mult))
            for i in range(NCLS):
                dve.wait_ge(down_made, i + 1)
                for s in range(2):
                    last = dve.tensor_tensor(e0[:, i, s, :], ps[0:B, 5 + i % 3, s * D:(s + 1) * D], b2[:, EXPERT_PAIRS[i][s][1], :], ALU.add)
                last.then_inc(down_copied, 1)
                dve.wait_ge(down_copied, i + 1)
                for s in range(2):
                    link(dve.scalar_tensor_tensor(h[:, i, :], e0[:, i, s, :], g[:, i, s:s + 1], h[:, i, :], ALU.mult, ALU.add))
            dve.sem_inc(y_ready, 1)

        @block.tensor
        def _(pe):
            pe.wait_ge(xn_ready, 1)
            for c in range(2):
                for i in range(NCLS):
                    last = pe.transpose(ps[0:HD, c, i * B:(i + 1) * B], xn[:, i, c * HD:(c + 1) * HD], ident[0:B, 0:B])
                last.then_inc(x_turned, 1)
            pe.wait_ge(x_copied, 2)
            for i in range(NCLS):
                for c in range(2):
                    last = pe.matmul(ps[0:B, 2, 2 * i:2 * i + 2], xt[:, c, i * B:(i + 1) * B], gw[:, i, c, :], start=(c == 0), stop=(c == 1))
            last.then_inc(gate_made, 1)
            pe.wait_ge(late, 16 * 4 * NA)
            n = 0
            for x in range(NA):
                tokens = [i for i, _ in users[x]]
                step = tokens[1] - tokens[0]
                assert tokens == list(range(tokens[0], tokens[-1] + 1, step))
                for f in range(FC):
                    if n >= 2:
                        pe.wait_ge(gelu_done, n - 1)
                    for c in range(2):
                        cols = xt[:, c, :].rearrange("p (i b) -> p i b", b=B)[:, tokens[0]:tokens[-1] + 1:step, :]
                        last = pe.matmul(ps[:, 3 + n % 2, 0:len(tokens) * B].rearrange("p (i b) -> p i b", b=B), w1[:, x, c, f * 128:(f + 1) * 128], cols,
                                         start=(c == 0), stop=(c == 1))
                    last.then_inc(up_made, 1)
                    n += 1
            pe.wait_ge(gelu_done, NA * FC)
            for i in range(NCLS):
                if i >= 3:
                    pe.wait_ge(down_copied, i - 2)
                for s in range(2):
                    at = place[(i, s)] * B
                    for f in range(FC):
                        last = pe.matmul(ps[0:B, 5 + i % 3, s * D:(s + 1) * D], ht[:, f, at:at + B], w2[:, EXPERT_PAIRS[i][s][1], f, :],
                                         start=(f == 0), stop=(f == FC - 1))
                last.then_inc(down_made, 1)


def vit_tower(nc, a, out):
    t = dram(nc)
    t["held"] = nc.alloc_semaphore("held")
    t["in_use"] = []
    out = out.rearrange("b n d -> (b n) d")
    with nc.sbuf_tensor("ident", [128, 128], F32) as ident, nc.sbuf_tensor("ident_r", [128, 128], F32R) as ident_r:
        t["ident"], t["ident_r"] = ident, ident_r
        with ExitStack() as ctx:
            keep(nc, ctx, t)
            phase_setup(nc, a, t)
            clear(nc, t)
            phase_tokens(nc, a, t)
        clear(nc, t)
        phase_route(nc, a, t)
        clear(nc, t)
        phase_experts(nc, a, t)
        clear(nc, t)
        phase_states(nc, a, t, out)
        clear(nc, t)
        phase_first(nc, a, t, out)


def kernel(**inputs):
    import concourse.bacc as bacc
    from concourse.bass_utils import run_bass_kernel_spmd

    nc = bacc.Bacc("TRN2", target_bir_lowering=False, num_devices=1)
    arrays = {k: np.ascontiguousarray(v) for k, v in inputs.items() if k != "L1_ffn_mids"}
    arrays.update(constants())
    a = {k: nc.dram_tensor("in_" + k, v.shape, mybir.dt.from_np(v.dtype), kind="ExternalInput").ap() for k, v in arrays.items()}
    out = nc.dram_tensor("out", (B, N, D), F32, kind="ExternalOutput").ap()
    vit_tower(nc, a, out)
    r = run_bass_kernel_spmd(nc, [{"in_" + k: v for k, v in arrays.items()}], core_ids=[0])
    return r.results[0]["out"]
```
